# Optimizing a Trainium2 kernel written in Bass

```python
import numpy as np
import jax
import jax.numpy as jnp

def _softmax(x, axis=-1):
    return jax.nn.softmax(x, axis=axis)

def _gelu(x):
    return jax.nn.gelu(x, approximate=True)

def _silu(x):
    return jax.nn.silu(x)

def _sigmoid(x):
    return jax.nn.sigmoid(x)

def _layernorm(x, axis=-1, eps=1e-05):
    m = jnp.mean(x, axis=axis, keepdims=True)
    v = jnp.var(x, axis=axis, keepdims=True)
    return (x - m) / jnp.sqrt(v + eps)

def _scatter_add(tgt, idx, src, axis=0):
    return tgt.at[idx].add(src)

def _segment_sum(src, seg, n):
    return jax.ops.segment_sum(src, seg, n)
kernel_name = 'mk_cond_seq_d4_seqx_r4_331e31'

def setup_inputs(seed: int=0):
    np.random.seed(seed)
    _w = jnp.asarray

    def _rec_inputs():
        import jax
        import jax.numpy as jnp
        _rk = jax.random.key(seed)
        x = -0.0002928 + 1 * jax.random.normal(jax.random.fold_in(_rk, 1), (16, 256, 256), jnp.float32)
        _lenS = 256 - jax.random.randint(jax.random.fold_in(_rk, 7), (16,), 0, max(1, 256 // 4) + 1, jnp.int32)
        _lenS2 = 256 - jax.random.randint(jax.random.fold_in(_rk, 8), (16,), 0, max(1, 256 // 4) + 1, jnp.int32)
        cond_1024 = 0.0061147 + 1.02565 * jax.random.normal(jax.random.fold_in(_rk, 11), (16, 256), jnp.float32)
        _validS = jnp.arange(256)[None, :] < _lenS[:, None]
        _validS2 = jnp.arange(256)[None, :] < _lenS2[:, None]
        _causal = jnp.tril(jnp.ones((256, 256), dtype=bool))
        mask_BxS_bk0 = jnp.logical_not(jnp.broadcast_to(_validS[:, :], (16, 256)))
        return (x, cond_1024, mask_BxS_bk0)
    x, cond_1024, mask_BxS_bk0 = _rec_inputs()

    def _L0_cond_setup():
        import jax, jax.numpy as jnp
        import numpy as np
        B, T, DIM = (4, 256, 256)
        COND = 256
        HEADS, DH = (16, 64)
        INNER = HEADS * DH
        MLP = 1024
        EPS = 1e-05

        def _layernorm(x):
            mu = jnp.mean(x, axis=-1, keepdims=True)
            var = jnp.mean(jnp.square(x - mu), axis=-1, keepdims=True)
            return (x - mu) * jax.lax.rsqrt(var + EPS)

        def _modulate(x, shift, scale):
            return x * (1.0 + scale) + shift

        def _attention(x, W_qkv, W_out, b_out):
            Bq, Tq, _ = x.shape
            qkv = x @ W_qkv
            q, k, v = jnp.split(qkv, 3, axis=-1)
            q = q.reshape(Bq, Tq, HEADS, DH)
            k = k.reshape(Bq, Tq, HEADS, DH)
            v = v.reshape(Bq, Tq, HEADS, DH)
            scale = DH ** (-0.5)
            attn = jnp.einsum('bqhd,bkhd->bhqk', q, k) * scale
            attn = jax.nn.softmax(attn, axis=-1)
            out = jnp.einsum('bhqk,bkhd->bqhd', attn, v).reshape(Bq, Tq, INNER)
            return out @ W_out + b_out

        def _ff(x, W1, b1, W2, b2):
            return jax.nn.gelu(x @ W1 + b1, approximate=False) @ W2 + b2
        key = jax.random.key(seed)
        ks = jax.random.split(key, 12)
        s = 0.02
        return {'x': jax.random.normal(ks[0], (B, T, DIM), jnp.float32), 'c': jax.random.normal(ks[1], (B, 1, COND), jnp.float32), 'W_mod': jax.random.normal(ks[2], (COND, 6 * DIM), jnp.float32) * s, 'b_mod': jax.random.normal(ks[3], (6 * DIM,), jnp.float32) * s, 'W_qkv': jax.random.normal(ks[4], (DIM, 3 * INNER), jnp.float32) * s, 'W_out': jax.random.normal(ks[5], (INNER, DIM), jnp.float32) * s, 'b_out': jax.random.normal(ks[6], (DIM,), jnp.float32) * s, 'W1': jax.random.normal(ks[7], (DIM, MLP), jnp.float32) * s, 'b1': jax.random.normal(ks[8], (MLP,), jnp.float32) * s, 'W2': jax.random.normal(ks[9], (MLP, DIM), jnp.float32) * s, 'b2': jax.random.normal(ks[10], (DIM,), jnp.float32) * s}
    _L0_cond_all = _L0_cond_setup()
    _L0_cond_in = {k: v for k, v in _L0_cond_all.items() if k in ('W_mod', 'b_mod', 'W_qkv', 'W_out', 'b_out', 'W1', 'b1', 'W2', 'b2')}
    del _L0_cond_all

    def _L1_cond_setup():
        import jax, jax.numpy as jnp
        import numpy as np
        DIM = 256
        MLP_RATIO = 4
        EPS = 1e-06

        def rmsnorm(x, w):
            return x * jax.lax.rsqrt(jnp.mean(x * x, axis=-1, keepdims=True) + EPS) * w

        def film(x, cond, w, b):
            ss = cond @ w + b
            scale, shift = jnp.split(ss, 2, axis=-1)
            return x * (1.0 + scale[:, None, :]) + shift[:, None, :]
        key = jax.random.key(seed)
        ks = jax.random.split(key, 16)
        B, N, D = (4, 512, DIM)
        H = D * MLP_RATIO
        s = lambda fan_in: 1.0 / np.sqrt(fan_in)
        return {'x': jax.random.normal(ks[0], (B, N, D), jnp.float32), 'cond': jax.random.normal(ks[1], (B, D), jnp.float32), 'norm1_w': jnp.ones((D,), jnp.float32), 'film1_w': jax.random.normal(ks[2], (D, 2 * D), jnp.float32) * s(D), 'film1_b': jnp.zeros((2 * D,), jnp.float32), 'q_w': jax.random.normal(ks[3], (D, D), jnp.float32) * s(D), 'q_b': jnp.zeros((D,), jnp.float32), 'k_w': jax.random.normal(ks[4], (D, D), jnp.float32) * s(D), 'k_b': jnp.zeros((D,), jnp.float32), 'v_w': jax.random.normal(ks[5], (D, D), jnp.float32) * s(D), 'v_b': jnp.zeros((D,), jnp.float32), 'proj_w': jax.random.normal(ks[6], (D, D), jnp.float32) * s(D), 'proj_b': jnp.zeros((D,), jnp.float32), 'norm2_w': jnp.ones((D,), jnp.float32), 'film2_w': jax.random.normal(ks[7], (D, 2 * D), jnp.float32) * s(D), 'film2_b': jnp.zeros((2 * D,), jnp.float32), 'mlp_w1': jax.random.normal(ks[8], (D, H), jnp.float32) * s(D), 'mlp_b1': jnp.zeros((H,), jnp.float32), 'mlp_w2': jax.random.normal(ks[9], (H, D), jnp.float32) * s(H), 'mlp_b2': jnp.zeros((D,), jnp.float32)}
    _L1_cond_all = _L1_cond_setup()
    _L1_cond_in = {k: v for k, v in _L1_cond_all.items() if k in ('norm1_w', 'film1_w', 'film1_b', 'q_w', 'q_b', 'k_w', 'k_b', 'v_w', 'v_b', 'proj_w', 'proj_b', 'norm2_w', 'film2_w', 'film2_b', 'mlp_w1', 'mlp_b1', 'mlp_w2', 'mlp_b2')}
    del _L1_cond_all

    def _L2_cond_setup():
        import jax, jax.numpy as jnp
        import numpy as np
        B, N, C = (4, 256, 256)
        H = 16
        D = C // H
        FF = 4 * C
        EPS = 1e-05

        def _layernorm(x):
            mu = jnp.mean(x, axis=-1, keepdims=True)
            var = jnp.mean(jnp.square(x - mu), axis=-1, keepdims=True)
            return (x - mu) * jax.lax.rsqrt(var + EPS)

        def _modulate(x, shift, scale):
            return x * (1.0 + scale[:, None, :]) + shift[:, None, :]

        def _attention(x, node_mask, qkv_w, proj_w, proj_b):
            b, n, c = x.shape
            qkv = (x @ qkv_w).reshape(b, n, 3, H, D)
            q, k, v = jnp.moveaxis(qkv, 2, 0)
            q = q.transpose(0, 2, 1, 3)
            k = k.transpose(0, 2, 1, 3)
            v = v.transpose(0, 2, 1, 3)
            scale = D ** (-0.5)
            scores = jnp.einsum('bhnd,bhmd->bhnm', q, k) * scale
            mask = node_mask[:, None, None, :]
            scores = jnp.where(mask, scores, -jnp.inf)
            attn = jax.nn.softmax(scores, axis=-1)
            out = jnp.einsum('bhnm,bhmd->bhnd', attn, v)
            out = out.transpose(0, 2, 1, 3).reshape(b, n, c)
            return out @ proj_w + proj_b

        def _mlp(x, fc1_w, fc1_b, fc2_w, fc2_b):
            h = jax.nn.gelu(x @ fc1_w + fc1_b, approximate=False)
            return h @ fc2_w + fc2_b
        key = jax.random.key(seed)
        ks = jax.random.split(key, 16)
        s = 0.02
        return {'x': jax.random.normal(ks[0], (B, N, C), jnp.float32), 'c': jax.random.normal(ks[1], (B, C), jnp.float32), 'node_mask': jax.random.randint(ks[2], (B, N), 0, 2) > 0, 'qkv_w': jax.random.normal(ks[3], (C, 3 * C), jnp.float32) * s, 'proj_w': jax.random.normal(ks[4], (C, C), jnp.float32) * s, 'proj_b': jnp.zeros((C,), jnp.float32), 'fc1_w': jax.random.normal(ks[5], (C, FF), jnp.float32) * s, 'fc1_b': jnp.zeros((FF,), jnp.float32), 'fc2_w': jax.random.normal(ks[6], (FF, C), jnp.float32) * s, 'fc2_b': jnp.zeros((C,), jnp.float32), 'ada1_w': jax.random.normal(ks[7], (C, C), jnp.float32) * s, 'ada1_b': jnp.zeros((C,), jnp.float32), 'ada2_w': jax.random.normal(ks[8], (C, 6 * C), jnp.float32) * s, 'ada2_b': jnp.zeros((6 * C,), jnp.float32)}
    _L2_cond_all = _L2_cond_setup()
    _L2_cond_in = {k: v for k, v in _L2_cond_all.items() if k in ('qkv_w', 'proj_w', 'proj_b', 'fc1_w', 'fc1_b', 'fc2_w', 'fc2_b', 'ada1_w', 'ada1_b', 'ada2_w', 'ada2_b')}
    del _L2_cond_all

    def _L3_cond_setup():
        import jax, jax.numpy as jnp
        import numpy as np
        B, N, D = (2, 512, 256)
        H, HD = (16, 64)
        E, DD = (8, 1024)
        EPS = 1e-05

        def _ln(x, g, b):
            m = jnp.mean(x, axis=-1, keepdims=True)
            v = jnp.var(x, axis=-1, keepdims=True)
            return (x - m) * jax.lax.rsqrt(v + EPS) * g + b
        key = jax.random.key(seed)
        ks = jax.random.split(key, 16)
        s = 0.02
        return {'x': jax.random.normal(ks[0], (B, N, D), jnp.float32), 't': jax.random.normal(ks[1], (B, 1, D), jnp.float32), 'W_ada': jax.random.normal(ks[2], (D, D), jnp.float32) * s, 'b_ada': jnp.zeros((D,), jnp.float32), 'ln1_g': jnp.ones((D,), jnp.float32), 'ln1_b': jnp.zeros((D,), jnp.float32), 'Wqkv': jax.random.normal(ks[3], (3 * H * HD, D), jnp.float32) * s, 'qn_g': jnp.ones((HD,), jnp.float32), 'qn_b': jnp.zeros((HD,), jnp.float32), 'kn_g': jnp.ones((HD,), jnp.float32), 'kn_b': jnp.zeros((HD,), jnp.float32), 'Wout': jax.random.normal(ks[4], (D, H * HD), jnp.float32) * s, 'mlp_g': jnp.ones((D,), jnp.float32), 'mlp_b': jnp.zeros((D,), jnp.float32), 'Wgate': jax.random.normal(ks[5], (E, D), jnp.float32) * s, 'fc1s': jax.random.normal(ks[6], (E, DD, D), jnp.float32) * s, 'b1s': jnp.zeros((E, DD), jnp.float32), 'fc2s': jax.random.normal(ks[7], (E, D, DD), jnp.float32) * s, 'b2s': jnp.zeros((E, D), jnp.float32)}
    _L3_cond_all = _L3_cond_setup()
    _L3_cond_in = {k: v for k, v in _L3_cond_all.items() if k in ('W_ada', 'b_ada', 'ln1_g', 'ln1_b', 'Wqkv', 'qn_g', 'qn_b', 'kn_g', 'kn_b', 'Wout', 'mlp_g', 'mlp_b', 'Wgate', 'fc1s', 'b1s', 'fc2s', 'b2s')}
    del _L3_cond_all
    return {'x': x, 'cond_1024': cond_1024, 'mask_BxS_bk0': mask_BxS_bk0, 'L0_cond_W_mod': _L0_cond_in['W_mod'], 'L0_cond_b_mod': _L0_cond_in['b_mod'], 'L0_cond_W_qkv': _L0_cond_in['W_qkv'], 'L0_cond_W_out': _L0_cond_in['W_out'], 'L0_cond_b_out': _L0_cond_in['b_out'], 'L0_cond_W1': _L0_cond_in['W1'], 'L0_cond_b1': _L0_cond_in['b1'], 'L0_cond_W2': _L0_cond_in['W2'], 'L0_cond_b2': _L0_cond_in['b2'], 'L1_cond_norm1_w': _L1_cond_in['norm1_w'], 'L1_cond_film1_w': _L1_cond_in['film1_w'], 'L1_cond_film1_b': _L1_cond_in['film1_b'], 'L1_cond_q_w': _L1_cond_in['q_w'], 'L1_cond_q_b': _L1_cond_in['q_b'], 'L1_cond_k_w': _L1_cond_in['k_w'], 'L1_cond_k_b': _L1_cond_in['k_b'], 'L1_cond_v_w': _L1_cond_in['v_w'], 'L1_cond_v_b': _L1_cond_in['v_b'], 'L1_cond_proj_w': _L1_cond_in['proj_w'], 'L1_cond_proj_b': _L1_cond_in['proj_b'], 'L1_cond_norm2_w': _L1_cond_in['norm2_w'], 'L1_cond_film2_w': _L1_cond_in['film2_w'], 'L1_cond_film2_b': _L1_cond_in['film2_b'], 'L1_cond_mlp_w1': _L1_cond_in['mlp_w1'], 'L1_cond_mlp_b1': _L1_cond_in['mlp_b1'], 'L1_cond_mlp_w2': _L1_cond_in['mlp_w2'], 'L1_cond_mlp_b2': _L1_cond_in['mlp_b2'], 'L2_cond_qkv_w': _L2_cond_in['qkv_w'], 'L2_cond_proj_w': _L2_cond_in['proj_w'], 'L2_cond_proj_b': _L2_cond_in['proj_b'], 'L2_cond_fc1_w': _L2_cond_in['fc1_w'], 'L2_cond_fc1_b': _L2_cond_in['fc1_b'], 'L2_cond_fc2_w': _L2_cond_in['fc2_w'], 'L2_cond_fc2_b': _L2_cond_in['fc2_b'], 'L2_cond_ada1_w': _L2_cond_in['ada1_w'], 'L2_cond_ada1_b': _L2_cond_in['ada1_b'], 'L2_cond_ada2_w': _L2_cond_in['ada2_w'], 'L2_cond_ada2_b': _L2_cond_in['ada2_b'], 'L3_cond_W_ada': _L3_cond_in['W_ada'], 'L3_cond_b_ada': _L3_cond_in['b_ada'], 'L3_cond_ln1_g': _L3_cond_in['ln1_g'], 'L3_cond_ln1_b': _L3_cond_in['ln1_b'], 'L3_cond_Wqkv': _L3_cond_in['Wqkv'], 'L3_cond_qn_g': _L3_cond_in['qn_g'], 'L3_cond_qn_b': _L3_cond_in['qn_b'], 'L3_cond_kn_g': _L3_cond_in['kn_g'], 'L3_cond_kn_b': _L3_cond_in['kn_b'], 'L3_cond_Wout': _L3_cond_in['Wout'], 'L3_cond_mlp_g': _L3_cond_in['mlp_g'], 'L3_cond_mlp_b': _L3_cond_in['mlp_b'], 'L3_cond_Wgate': _L3_cond_in['Wgate'], 'L3_cond_fc1s': _L3_cond_in['fc1s'], 'L3_cond_b1s': _L3_cond_in['b1s'], 'L3_cond_fc2s': _L3_cond_in['fc2s'], 'L3_cond_b2s': _L3_cond_in['b2s']}

def reference(x, cond_1024, mask_BxS_bk0, L0_cond_W_mod, L0_cond_b_mod, L0_cond_W_qkv, L0_cond_W_out, L0_cond_b_out, L0_cond_W1, L0_cond_b1, L0_cond_W2, L0_cond_b2, L1_cond_norm1_w, L1_cond_film1_w, L1_cond_film1_b, L1_cond_q_w, L1_cond_q_b, L1_cond_k_w, L1_cond_k_b, L1_cond_v_w, L1_cond_v_b, L1_cond_proj_w, L1_cond_proj_b, L1_cond_norm2_w, L1_cond_film2_w, L1_cond_film2_b, L1_cond_mlp_w1, L1_cond_mlp_b1, L1_cond_mlp_w2, L1_cond_mlp_b2, L2_cond_qkv_w, L2_cond_proj_w, L2_cond_proj_b, L2_cond_fc1_w, L2_cond_fc1_b, L2_cond_fc2_w, L2_cond_fc2_b, L2_cond_ada1_w, L2_cond_ada1_b, L2_cond_ada2_w, L2_cond_ada2_b, L3_cond_W_ada, L3_cond_b_ada, L3_cond_ln1_g, L3_cond_ln1_b, L3_cond_Wqkv, L3_cond_qn_g, L3_cond_qn_b, L3_cond_kn_g, L3_cond_kn_b, L3_cond_Wout, L3_cond_mlp_g, L3_cond_mlp_b, L3_cond_Wgate, L3_cond_fc1s, L3_cond_b1s, L3_cond_fc2s, L3_cond_b2s):
    import jax
    import jax.numpy as jnp

    def _L0_cond_ref(x, c, W_mod, b_mod, W_qkv, W_out, b_out, W1, b1, W2, b2):
        import jax, jax.numpy as jnp
        import numpy as np
        B, T, DIM = (4, 256, 256)
        COND = 256
        HEADS, DH = (16, 64)
        INNER = HEADS * DH
        MLP = 1024
        EPS = 1e-05

        def _layernorm(x):
            mu = jnp.mean(x, axis=-1, keepdims=True)
            var = jnp.mean(jnp.square(x - mu), axis=-1, keepdims=True)
            return (x - mu) * jax.lax.rsqrt(var + EPS)

        def _modulate(x, shift, scale):
            return x * (1.0 + scale) + shift

        def _attention(x, W_qkv, W_out, b_out):
            Bq, Tq, _ = x.shape
            qkv = x @ W_qkv
            q, k, v = jnp.split(qkv, 3, axis=-1)
            q = q.reshape(Bq, Tq, HEADS, DH)
            k = k.reshape(Bq, Tq, HEADS, DH)
            v = v.reshape(Bq, Tq, HEADS, DH)
            scale = DH ** (-0.5)
            attn = jnp.einsum('bqhd,bkhd->bhqk', q, k) * scale
            attn = jax.nn.softmax(attn, axis=-1)
            out = jnp.einsum('bhqk,bkhd->bqhd', attn, v).reshape(Bq, Tq, INNER)
            return out @ W_out + b_out

        def _ff(x, W1, b1, W2, b2):
            return jax.nn.gelu(x @ W1 + b1, approximate=False) @ W2 + b2
        mod = jax.nn.silu(c) @ W_mod + b_mod
        sh_msa, sc_msa, g_msa, sh_mlp, sc_mlp, g_mlp = jnp.split(mod, 6, axis=-1)
        x = x + g_msa * _attention(_modulate(_layernorm(x), sh_msa, sc_msa), W_qkv, W_out, b_out)
        x = x + g_mlp * _ff(_modulate(_layernorm(x), sh_mlp, sc_mlp), W1, b1, W2, b2)
        return x

    def _L1_cond_ref(x, cond, norm1_w, film1_w, film1_b, q_w, q_b, k_w, k_b, v_w, v_b, proj_w, proj_b, norm2_w, film2_w, film2_b, mlp_w1, mlp_b1, mlp_w2, mlp_b2):
        import jax, jax.numpy as jnp
        import numpy as np
        DIM = 256
        MLP_RATIO = 4
        EPS = 1e-06

        def rmsnorm(x, w):
            return x * jax.lax.rsqrt(jnp.mean(x * x, axis=-1, keepdims=True) + EPS) * w

        def film(x, cond, w, b):
            ss = cond @ w + b
            scale, shift = jnp.split(ss, 2, axis=-1)
            return x * (1.0 + scale[:, None, :]) + shift[:, None, :]
        B, N, D = x.shape
        x_in = x
        h = film(rmsnorm(x, norm1_w), cond, film1_w, film1_b)
        Q = h @ q_w + q_b
        K = h @ k_w + k_b
        V = h @ v_w + v_b
        scores = jnp.einsum('bnd,bmd->bnm', Q, K) * D ** (-0.5)
        attn = jax.nn.softmax(scores, axis=-1)
        out = jnp.einsum('bnm,bmd->bnd', attn, V)
        x = x_in + (out @ proj_w + proj_b)
        x_in = x
        h = film(rmsnorm(x, norm2_w), cond, film2_w, film2_b)
        h = jax.nn.gelu(h @ mlp_w1 + mlp_b1, approximate=False) @ mlp_w2 + mlp_b2
        return x_in + h

    def _L2_cond_ref(x, c, node_mask, qkv_w, proj_w, proj_b, fc1_w, fc1_b, fc2_w, fc2_b, ada1_w, ada1_b, ada2_w, ada2_b):
        import jax, jax.numpy as jnp
        import numpy as np
        B, N, C = (4, 256, 256)
        H = 16
        D = C // H
        FF = 4 * C
        EPS = 1e-05

        def _layernorm(x):
            mu = jnp.mean(x, axis=-1, keepdims=True)
            var = jnp.mean(jnp.square(x - mu), axis=-1, keepdims=True)
            return (x - mu) * jax.lax.rsqrt(var + EPS)

        def _modulate(x, shift, scale):
            return x * (1.0 + scale[:, None, :]) + shift[:, None, :]

        def _attention(x, node_mask, qkv_w, proj_w, proj_b):
            b, n, c = x.shape
            qkv = (x @ qkv_w).reshape(b, n, 3, H, D)
            q, k, v = jnp.moveaxis(qkv, 2, 0)
            q = q.transpose(0, 2, 1, 3)
            k = k.transpose(0, 2, 1, 3)
            v = v.transpose(0, 2, 1, 3)
            scale = D ** (-0.5)
            scores = jnp.einsum('bhnd,bhmd->bhnm', q, k) * scale
            mask = node_mask[:, None, None, :]
            scores = jnp.where(mask, scores, -jnp.inf)
            attn = jax.nn.softmax(scores, axis=-1)
            out = jnp.einsum('bhnm,bhmd->bhnd', attn, v)
            out = out.transpose(0, 2, 1, 3).reshape(b, n, c)
            return out @ proj_w + proj_b

        def _mlp(x, fc1_w, fc1_b, fc2_w, fc2_b):
            h = jax.nn.gelu(x @ fc1_w + fc1_b, approximate=False)
            return h @ fc2_w + fc2_b
        ada = jax.nn.silu(c @ ada1_w + ada1_b) @ ada2_w + ada2_b
        shift_msa, scale_msa, gate_msa, shift_mlp, scale_mlp, gate_mlp = jnp.split(ada, 6, axis=1)
        attn_out = _attention(x, node_mask, qkv_w, proj_w, proj_b)
        x = x + gate_msa[:, None, :] * _modulate(_layernorm(attn_out), shift_msa, scale_msa)
        mlp_out = _mlp(x, fc1_w, fc1_b, fc2_w, fc2_b)
        x = x + gate_mlp[:, None, :] * _modulate(_layernorm(mlp_out), shift_mlp, scale_mlp)
        return x

    def _L3_cond_ref(x, t, W_ada, b_ada, ln1_g, ln1_b, Wqkv, qn_g, qn_b, kn_g, kn_b, Wout, mlp_g, mlp_b, Wgate, fc1s, b1s, fc2s, b2s):
        import jax, jax.numpy as jnp
        import numpy as np
        B, N, D = (2, 512, 256)
        H, HD = (16, 64)
        E, DD = (8, 1024)
        EPS = 1e-05

        def _ln(x, g, b):
            m = jnp.mean(x, axis=-1, keepdims=True)
            v = jnp.var(x, axis=-1, keepdims=True)
            return (x - m) * jax.lax.rsqrt(v + EPS) * g + b
        b, n, d = x.shape
        shift = jax.nn.silu(t) @ W_ada.T + b_ada
        h = _ln(x, ln1_g, ln1_b) + shift
        qkv = (h @ Wqkv.T).reshape(b, n, 3, H, HD)
        q = _ln(qkv[:, :, 0].transpose(0, 2, 1, 3), qn_g, qn_b)
        k = _ln(qkv[:, :, 1].transpose(0, 2, 1, 3), kn_g, kn_b)
        v = qkv[:, :, 2].transpose(0, 2, 1, 3)
        scores = jnp.einsum('bhnd,bhmd->bhnm', q, k) / jnp.sqrt(jnp.float32(HD))
        attn = jax.nn.softmax(scores, axis=-1)
        o = jnp.einsum('bhnm,bhmd->bhnd', attn, v)
        o = o.transpose(0, 2, 1, 3).reshape(b, n, H * HD)
        x = x + o @ Wout.T
        tok = x.reshape(-1, d)
        bs = tok.shape[0]
        gate = jax.nn.softmax(tok @ Wgate.T, axis=-1)
        k_cap = bs // E
        vals, idx = jax.lax.top_k(gate.T, k_cap)
        idx_flat = idx.T.reshape(-1)
        w = vals.T
        g = _ln(tok[idx_flat], mlp_g, mlp_b).reshape(k_cap, E, d)
        y = jnp.einsum('ked,ehd->keh', g, fc1s) + b1s
        y = jax.nn.gelu(y, approximate=True)
        y = jnp.einsum('keh,edh->ked', y, fc2s) + b2s
        y = y * w[..., None]
        tok = tok.at[idx_flat].add(y.reshape(-1, d))
        return tok.reshape(x.shape)
    x = _L0_cond_ref(x, cond_1024[:, None, :], L0_cond_W_mod, L0_cond_b_mod, L0_cond_W_qkv, L0_cond_W_out, L0_cond_b_out, L0_cond_W1, L0_cond_b1, L0_cond_W2, L0_cond_b2)
    x = _L1_cond_ref(x, cond_1024, L1_cond_norm1_w, L1_cond_film1_w, L1_cond_film1_b, L1_cond_q_w, L1_cond_q_b, L1_cond_k_w, L1_cond_k_b, L1_cond_v_w, L1_cond_v_b, L1_cond_proj_w, L1_cond_proj_b, L1_cond_norm2_w, L1_cond_film2_w, L1_cond_film2_b, L1_cond_mlp_w1, L1_cond_mlp_b1, L1_cond_mlp_w2, L1_cond_mlp_b2)
    x = _L2_cond_ref(x, cond_1024, mask_BxS_bk0, L2_cond_qkv_w, L2_cond_proj_w, L2_cond_proj_b, L2_cond_fc1_w, L2_cond_fc1_b, L2_cond_fc2_w, L2_cond_fc2_b, L2_cond_ada1_w, L2_cond_ada1_b, L2_cond_ada2_w, L2_cond_ada2_b)
    x = _L3_cond_ref(x, cond_1024[:, None, :], L3_cond_W_ada, L3_cond_b_ada, L3_cond_ln1_g, L3_cond_ln1_b, L3_cond_Wqkv, L3_cond_qn_g, L3_cond_qn_b, L3_cond_kn_g, L3_cond_kn_b, L3_cond_Wout, L3_cond_mlp_g, L3_cond_mlp_b, L3_cond_Wgate, L3_cond_fc1s, L3_cond_b1s, L3_cond_fc2s, L3_cond_b2s)
    return x

_drawn_inputs = setup_inputs


def setup_inputs(seed=0):
    import zlib

    import numpy as np

    out = dict(_drawn_inputs(seed))
    spreads = {'L1_cond_norm1_w': (1.0, 0.2),
     'L1_cond_film1_b': (0.0, 0.1),
     'L1_cond_q_b': (0.0, 0.1),
     'L1_cond_k_b': (0.0, 0.8),
     'L1_cond_v_b': (0.0, 0.1),
     'L1_cond_proj_b': (0.0, 0.1),
     'L1_cond_norm2_w': (1.0, 0.2),
     'L1_cond_film2_b': (0.0, 0.1),
     'L1_cond_mlp_b1': (0.0, 0.1),
     'L1_cond_mlp_b2': (0.0, 0.1),
     'L2_cond_proj_b': (0.0, 0.1),
     'L2_cond_fc1_b': (0.0, 0.8),
     'L2_cond_fc2_b': (0.0, 0.4),
     'L2_cond_ada1_b': (0.0, 0.646),
     'L2_cond_ada2_b': (0.0, 0.1),
     'L3_cond_b_ada': (0.0, 0.8),
     'L3_cond_ln1_g': (1.0, 0.6),
     'L3_cond_ln1_b': (0.0, 0.793),
     'L3_cond_qn_g': (1.0, 0.6),
     'L3_cond_qn_b': (0.0, 0.8),
     'L3_cond_kn_g': (1.0, 0.6),
     'L3_cond_kn_b': (0.0, 0.8),
     'L3_cond_mlp_g': (1.0, 0.6),
     'L3_cond_mlp_b': (0.0, 0.8),
     'L3_cond_b1s': (0.0, 0.8),
     'L3_cond_b2s': (0.0, 0.593)}
    factors = {'L0_cond_b_mod': 8.0,
     'L0_cond_W_qkv': 5.393,
     'L0_cond_W_out': 5.201,
     'L0_cond_b_out': 8.0,
     'L0_cond_b1': 8.0,
     'L0_cond_b2': 8.0,
     'L3_cond_W_ada': 2.841,
     'L3_cond_Wgate': 2.806,
     'L3_cond_fc1s': 3.644,
     'L3_cond_fc2s': 3.372}
    for name, (base, spread) in spreads.items():
        noise = np.random.default_rng([zlib.crc32(name.encode()), seed]).standard_normal(out[name].shape)
        drawn = base * np.exp(spread * noise) if base else spread * noise
        out[name] = jnp.asarray(drawn.astype(out[name].dtype))
    for name, factor in factors.items():
        out[name] = (out[name] * factor).astype(out[name].dtype)
    return out
```

```python
from contextlib import ExitStack, contextmanager

import numpy as np
import concourse.bass as bass
from concourse import mybir

F32 = mybir.dt.float32
F32R = mybir.dt.float32r
U8 = mybir.dt.uint8
U32 = mybir.dt.uint32
I32 = mybir.dt.int32
ALU = mybir.AluOpType
ACT = mybir.ActivationFunctionType
AX = mybir.AxisListType

P = 128
B, N, D = 16, 256, 256
TT = N // P
KD = D // P
TILES = B * TT
MLP = 1024
MC = MLP // P
E = 8
CAP = B * N // E
SC = CAP // P

COL_VECS = [("L0_cond_b_mod", 12), ("L0_cond_b1", 8),
            ("L1_cond_norm1_w", 2), ("L1_cond_film1_b", 4), ("L1_cond_q_b", 2), ("L1_cond_k_b", 2),
            ("L1_cond_v_b", 2), ("L1_cond_norm2_w", 2), ("L1_cond_film2_b", 4), ("L1_cond_mlp_b1", 8),
            ("L2_cond_fc1_b", 8), ("L2_cond_ada1_b", 2),
            ("L3_cond_b_ada", 2), ("L3_cond_ln1_g", 2), ("L3_cond_ln1_b", 2),
            ("qn_g2", 1), ("qn_b2", 1), ("kn_g2", 1), ("kn_b2", 1),
            ("L3_cond_mlp_g", 2), ("L3_cond_mlp_b", 2), ("L3_cond_b1s", 64)]
COL_AT = {}
for _name, _n in COL_VECS:
    COL_AT[_name] = sum(n for _, n in COL_VECS[:len(COL_AT)])
NCOL = sum(n for _, n in COL_VECS)
ROW_VECS = [("L0_cond_b_mod", 1536), ("L0_cond_b_out", 256), ("L0_cond_b2", 256), ("L2_cond_ada2_b", 1536)]
ROW_AT = {"L0_cond_b_mod": 0, "L0_cond_b_out": 1536, "L0_cond_b2": 1792, "L2_cond_ada2_b": 2048}
NROW = 3584

MOD_AT = {"L0a": 0, "L0m": 4, "L1a": 8, "L1m": 12, "L3a": 16}
NMOD = 20
GATE_AT = {"L0a": 0, "L0m": 2, "L2a": 4, "L2m": 6}
NGATE = 8


@contextmanager
def semaphores(nc, prefix):
    with ExitStack() as ctx:
        made = []

        def sem(name):
            made.append(ctx.enter_context(nc.semaphore(f"{prefix}_{name}")))
            return made[-1]

        yield sem
        with nc.Block() as block:
            @block.gpsimd
            def _(pool):
                for s in made:
                    pool.sem_clear(s)


def conditioning(nc, t, g):
    with semaphores(nc, "c") as sem, ExitStack() as ctx:
        sb = lambda n, s, d=F32: ctx.enter_context(nc.sbuf_tensor(n, s, d))
        ps = [ctx.enter_context(nc.psum_tensor(f"c_ps{i}", [P, 512], F32)) for i in range(4)]
        c_t = sb("c_t", [P, KD, B])
        silu_c = sb("c_silu", [P, KD, B])
        h1 = sb("c_h1", [P, KD, B])
        w_mod = sb("c_wmod", [P, KD, 1536])
        film = [sb(f"c_film{j}", [P, KD, 512]) for j in range(2)]
        ada1 = sb("c_ada1", [P, KD, 256])
        ada2 = sb("c_ada2", [P, KD, 1536])
        w_ada = sb("c_wada", [P, KD, 256])
        rows_b = sb("c_rows", [B, NROW])
        raw = sb("c_raw", [B, 2048])
        gates = sb("c_gates", [B, NGATE, D])
        colraw = sb("c_colraw", [P, 18, B])
        loaded, silu_done, mm_done, h1_done, v, stored, memz = (sem(f"s{i}") for i in range(7))
        chained = sem("chained")
        block = ctx.enter_context(nc.Block())
        chunked = lambda w: w.rearrange("(k p) n -> p k n", p=P)

        @block.sync
        def _(sp):
            sp.dma_start(c_t[:], chunked(t["c_t"])).then_inc(loaded, 16)
            sp.dma_start(g["cols"][:], t["cols"]).then_inc(loaded, 16)
            sp.dma_start(rows_b[:], t["rows"].partition_broadcast(B)).then_inc(loaded, 16)
            for dst, name in ((w_mod, "L0_cond_W_mod"), (film[0], "L1_cond_film1_w"),
                              (film[1], "L1_cond_film2_w"), (ada1, "L2_cond_ada1_w"),
                              (ada2, "L2_cond_ada2_w"), (w_ada, "W_ada_t")):
                sp.dma_start(dst[:], chunked(t[name])).then_inc(loaded, 16)
            sp.wait_ge(v, 1)
            sp.dma_start(t["gate_rows"].rearrange("g b d -> b g d"), gates[:]).then_inc(stored, 16)
            sp.wait_ge(stored, 16)

        @block.scalar
        def _(act):
            act.wait_ge(loaded, 16 * 9)
            nc.scalar.activation(silu_c[:], c_t[:], ACT.Silu).then_inc(silu_done, 1)
            act.wait_ge(mm_done, 2)
            for k in range(KD):
                nc.scalar.activation(h1[:, k, :], ps[2][:, k * B:(k + 1) * B], ACT.Silu,
                                     bias=g["cols"][:, COL_AT["L2_cond_ada1_b"] + k:COL_AT["L2_cond_ada1_b"] + k + 1]).then_inc(h1_done, 1)

        @block.tensor
        def _(pe):
            def columns(bank, j, w, col, x):
                for k in range(KD):
                    last = nc.tensor.matmul(bank[:, j * B:(j + 1) * B], w[:, k, col * P:(col + 1) * P],
                                            x[:, k, :], start=(k == 0), stop=(k == KD - 1))
                return last

            def row(bank, w, c0, n, x):
                for k in range(KD):
                    last = nc.tensor.matmul(bank[0:B, 0:n], x[:, k, :], w[:, k, c0:c0 + n],
                                            start=(k == 0), stop=(k == KD - 1))
                return last

            pe.wait_ge(silu_done, 1)
            for j, col in enumerate((0, 1, 2, 3, 6, 7, 8, 9)):
                columns(ps[0], j, w_mod, col, silu_c)
            for j in range(4):
                columns(ps[0], 8 + j, film[0], j, c_t)
            for j in range(4):
                columns(ps[0], 12 + j, film[1], j, c_t)
            for j in range(2):
                columns(ps[0], 16 + j, w_ada, j, silu_c)
            row(ps[1], w_mod, 512, 256, silu_c)
            for k in range(KD):
                last = nc.tensor.matmul(ps[1][0:B, 256:512], silu_c[:, k, :], w_mod[:, k, 1280:1536],
                                        start=(k == 0), stop=(k == KD - 1))
            last.then_inc(mm_done, 1)
            for j in range(2):
                last = columns(ps[2], j, ada1, j, c_t)
            last.then_inc(mm_done, 1)
            pe.wait_ge(h1_done, 2)
            pe.wait_ge(memz, 1)
            for n, bank in enumerate((ps[1], ps[2], ps[3])):
                last = row(bank, ada2, 512 * n, 512, h1)
            last.then_inc(mm_done, 1)

        @block.vector
        def _(dve):
            mod, cols = g["mod"], g["cols"]
            done = [0]
            chain = chained

            def step(ins):
                done[0] += 1
                ins.then_inc(chain, 1)
                dve.wait_ge(chain, done[0])

            dve.wait_ge(loaded, 16 * 9)
            step(nc.vector.memset(mod[:], 0.0))
            dve.wait_ge(mm_done, 1)
            step(nc.vector.tensor_copy(colraw[:], ps[0][:, 0:18 * B].rearrange("p (j b) -> p j b", b=B)))
            nc.vector.tensor_copy(raw[:, 0:512], ps[1][0:B, :]).then_inc(memz, 1)
            dve.wait_ge(memz, 1)

            def biased(j, bias, plus=0.0):
                step(nc.vector.tensor_scalar(colraw[:, j, :], colraw[:, j, :], cols[:, bias:bias + 1], plus,
                                             ALU.add, ALU.add))

            bm = COL_AT["L0_cond_b_mod"]
            for j, col in enumerate((0, 1, 2, 3, 6, 7, 8, 9)):
                biased(j, bm + col, 1.0 if j in (2, 3, 6, 7) else 0.0)
            for part, base in ((0, 8), (1, 12)):
                fb = COL_AT[f"L1_cond_film{part + 1}_b"]
                for j in range(4):
                    biased(base + j, fb + j, 1.0 if j < 2 else 0.0)
            for j in range(2):
                biased(16 + j, COL_AT["L3_cond_b_ada"] + j)
            for k in range(KD):
                for name, shift, scale in (("L0a", 0, 2), ("L0m", 4, 6), ("L1a", 10, 8), ("L1m", 14, 12)):
                    at = MOD_AT[name]
                    if name[1] == "0":
                        step(nc.vector.tensor_copy(mod[:, at + k, 0:B], colraw[:, scale + k, :]))
                    else:
                        nw = COL_AT["L1_cond_norm1_w" if name == "L1a" else "L1_cond_norm2_w"] + k
                        step(nc.vector.tensor_scalar(mod[:, at + k, 0:B], colraw[:, scale + k, :],
                                                     cols[:, nw:nw + 1], None, ALU.mult))
                    step(nc.vector.tensor_copy(mod[:, at + 2 + k, 0:B], colraw[:, shift + k, :]))
                at = MOD_AT["L3a"]
                gcol, bcol = COL_AT["L3_cond_ln1_g"] + k, COL_AT["L3_cond_ln1_b"] + k
                step(nc.vector.tensor_scalar(mod[:, at + k, 0:B], mod[:, at + k, 0:B],
                                             cols[:, gcol:gcol + 1], None, ALU.add))
                step(nc.vector.tensor_scalar(mod[:, at + 2 + k, 0:B], colraw[:, 16 + k, :],
                                             cols[:, bcol:bcol + 1], None, ALU.add))
            for half, name, bias in ((0, "L0a", "L0_cond_b_out"), (1, "L0m", "L0_cond_b2")):
                r = 512 if half == 0 else 1280
                at = GATE_AT[name]
                step(nc.vector.tensor_tensor(gates[:, at, :], raw[:, 256 * half:256 * half + 256],
                                             rows_b[:, r:r + 256], ALU.add))
                step(nc.vector.tensor_tensor(gates[:, at + 1, :], gates[:, at, :],
                                             rows_b[:, ROW_AT[bias]:ROW_AT[bias] + 256], ALU.mult))
            dve.wait_ge(mm_done, 3)
            ab = ROW_AT["L2_cond_ada2_b"]
            for n in range(3):
                step(nc.vector.tensor_tensor(raw[:, 512 + 512 * n:1024 + 512 * n], ps[n + 1][0:B, :],
                                             rows_b[:, ab + 512 * n:ab + 512 * n + 512], ALU.add))
            for half, name in ((0, "L2a"), (1, "L2m")):
                o = 512 + 768 * half
                at = GATE_AT[name]
                step(nc.vector.scalar_tensor_tensor(gates[:, at, :], raw[:, o + 256:o + 512], 1.0,
                                                    raw[:, o + 512:o + 768], ALU.add, ALU.mult))
                step(nc.vector.tensor_tensor(gates[:, at + 1, :], raw[:, o:o + 256],
                                             raw[:, o + 512:o + 768], ALU.mult))
            nc.vector.engine_nop().then_inc(v, 1)


def split_weights(nc, engines, stage, sems, pieces, centre=None):
    sp, pool, dve = engines
    landed, hi_done, lo_done = sems

    def sync_share():
        for n, (src, hi, lo, c) in enumerate(pieces):
            if n >= 2:
                sp.wait_ge(lo_done, n - 1)
            w = hi.shape[-1]
            sp.dma_start(stage[:, n % 2, 0:w], src).then_inc(landed[n % 2], 16)

    def pool_share():
        for n, (src, hi, lo, c) in enumerate(pieces):
            w = hi.shape[-1]
            if c:
                pool.wait_ge(centre[1], 2 * sum(x[3] for x in pieces[:n]) + 2)
            pool.wait_ge(landed[n % 2], 16 * (n // 2 + 1))
            nc.gpsimd.tensor_copy(hi, stage[:, n % 2, 0:w]).then_inc(hi_done, 1)

    def vector_share():
        seen = 0
        for n, (src, hi, lo, c) in enumerate(pieces):
            w = hi.shape[-1]
            if c:
                means, steps = centre
                dve.wait_ge(landed[n % 2], 16 * (n // 2 + 1))
                heads = stage[:, n % 2, 0:w].rearrange("p (h d) -> p h d", d=64)
                if seen:
                    dve.wait_ge(steps, 2 * seen)
                nc.vector.tensor_reduce(means[:], heads, AX.X, ALU.add).then_inc(steps, 1)
                dve.wait_ge(steps, 2 * seen + 1)
                mb = means[:].unsqueeze(2).to_broadcast([P, w // 64, 64])
                nc.vector.scalar_tensor_tensor(heads, mb, -1.0 / 64, heads, ALU.mult, ALU.add).then_inc(steps, 1)
                seen += 1
            dve.wait_ge(hi_done, n + 1)
            nc.vector.tensor_tensor(lo, stage[:, n % 2, 0:w], hi.bitcast(F32), ALU.subtract).then_inc(lo_done, 1)

    return sync_share, pool_share, vector_share


class Attention:

    def __init__(self, name, heads, d, scale, gated, norm, eps):
        self.name, self.heads, self.d, self.scale = name, heads, d, scale
        self.gated, self.norm, self.eps = gated, norm, eps
        self.chunks = heads * d // P
        self.one = heads == 1
        self.units = 1 if self.one else heads // 2
        self.vd = max(d, 32) if not self.one else d
        self.vw = heads * self.vd
        self.oc = heads * self.vd // P
        self.vpiece = min(512, self.vw)
        self.vpieces = TT * self.vw // self.vpiece
        self.upc = 2 if self.vd == 32 else 1
        self.groups = self.units // self.upc
        self.hn = 2 if not self.one else 1
        self.per_chunk = P // d if d < P else 1


def o_row(a, u, h):
    return 64 * h if a.d == 64 else 64 * (u % 2) + 32 * h


def o_rows(a, u):
    return slice(64 * (u % 2), 64 * (u % 2) + 64) if a.vd == 32 else slice(0, P)


def o_slices(a, c, dst, src):
    if a.one:
        return dst[:].rearrange("p c n -> p (c n)"), src[:, 0, :]
    return dst[:, c, :], src[:, c % 2, 0:N]


def residual(nc, dve, s, nm, i, tiles, outs, gate_of, eps, bufs, g, per, gate_ready):
    y, y2, xh, stats, mv, ve, rstd, y_bias = bufs
    n = len(tiles)
    step = [0]

    def chained(ins, last):
        step[0] += 1
        ins.then_inc(s["step"], 1)
        if last:
            dve.wait_ge(s["step"], per * i + step[0])

    tile = lambda j: g["x"][:, bass.ds(tiles[0] + j, 1), :].squeeze(1)
    if gate_ready is not None:
        dve.wait_ge(*gate_ready)
    src = outs
    if nm[:2] == "L2":
        for j in range(n):
            chained(nc.vector.tensor_tensor(y[:, j, :], outs[j], y_bias[:], ALU.add), j == n - 1)
        for j in range(n):
            chained(nc.vector.bn_stats(stats[:, j, :], y[:, j, :]), j == n - 1)
        dve.sem_inc(s["passed"], 1)
        for j in range(n):
            chained(nc.vector.bn_aggr(mv[:, j, :], stats[:, j, :]), j == n - 1)
        nc.vector.tensor_scalar(ve[:, 0:n], mv[:, 0:n, 1], eps, None, ALU.add).then_inc(s["ve2"], 1)
        dve.wait_ge(s["rstd2"], i + 1)
        for j in range(n):
            chained(nc.vector.tensor_scalar(y2[:, j, :], y[:, j, :], mv[:, j, 0:1], rstd[:, j:j + 1],
                                            ALU.subtract, ALU.mult), j == n - 1)
        src = [y2[:, j, :] for j in range(n)]
    if nm[:2] in ("L0", "L2"):
        for j in range(n):
            chained(nc.vector.tensor_tensor(y[:, j, :], src[j], gate_of(j), ALU.mult), j == n - 1)
        src = [y[:, j, :] for j in range(n)]
    if nm[:2] != "L3":
        dve.wait_ge(s["xh"], n * (i + 1))
    for j in range(n):
        other = tile(j) if nm[:2] == "L3" else xh[:, j, :]
        ins = nc.vector.tensor_tensor(tile(j), src[j], other, ALU.add)
        if j == n - 1:
            ins.then_inc(s["done"], 1)
        else:
            ins.then_inc(s["step"], 1)
            step[0] += 1
    assert step[0] == per, (nm, step[0], per)


def residual_steps(nm, n):
    return {"L0": 2 * n - 1, "L1": n - 1, "L2": 6 * n - 1, "L3": n - 1}[nm[:2]]


def attention(nc, t, g, a):
    nm, C, U, HN, OC = a.name, a.chunks, a.units, a.hn, a.oc
    LN_AT, OUT_AT = C + a.vpieces, C + a.vpieces + 1
    NR = C + a.vpieces + 2
    LN_STEP = min(3, U)
    qknorm, masked = nm == "L3a", nm == "L2a"
    MASK0 = 0 if a.d == 64 else 2
    cols = g["cols"]
    with semaphores(nc, nm) as sem, ExitStack() as ctx:
        sb = lambda n, s, d=F32: ctx.enter_context(nc.sbuf_tensor(f"{nm}_{n}", s, d))
        pb = lambda n: ctx.enter_context(nc.psum_tensor(f"{nm}_{n}", [P, 512], F32))
        ring = [pb("ring0"), pb("ring1")]
        s_ps = [pb("s0"), pb("s1")]
        st_ps = [pb("st0"), pb("st1")]
        o_ps, sum_ps = pb("o"), pb("sum")

        QW = a.heads * a.d
        wq = [sb(f"wq{j}", [P, KD, QW], F32R) for j in range(2)]
        wk = [sb(f"wk{j}", [P, KD, QW], F32R) for j in range(2)]
        wv = [sb(f"wv{j}", [P, KD, a.vw], F32R) for j in range(2)]
        wo = [sb(f"wo{j}", [P, OC, D], F32R) for j in range(2)]
        stage = sb("stage", [P, 2, 1024])
        means = sb("means", [P, 16])
        xn = sb("xn", [P, TT, D])
        xm = sb("xm", [P, KD, N])
        xt = [sb(f"xt{j}", [P, KD, N], F32R) for j in range(2)]
        stats = sb("stats", [P, TT, 6])
        mv = sb("mv", [P, TT, 2])
        ve = sb("ve", [P, TT])
        rstd = sb("rstd", [P, TT])
        q32 = sb("q32", [P, C, N])
        k_hi = sb("k_hi", [P, C, N], F32R)
        k_lo = sb("k_lo", [P, C, N], F32R)
        v = sb("v", [P, TT, a.vw])
        q_hi = sb("q_hi", [P, 2, 512], F32R)
        q_lo = sb("q_lo", [P, 2, 512], F32R)
        mx = sb("mx", [P, 4])
        shift = sb("shift", [P, 2, 512], F32R)
        prob = sb("prob", [P, 2, TT, 512])
        rsum = sb("rsum", [P, N])
        o32 = sb("o32", [P, 2, 512 if a.one else N])
        o_hi = sb("o_hi", [P, OC, N], F32R)
        o_lo = sb("o_lo", [P, OC, N], F32R)
        gate = xh = y = y2 = y_bias = None
        if not qknorm:
            gate, xh = sb("gate", [P, 2, D]), sb("xh", [P, TT, D])
        if a.gated:
            y = sb("y", [P, TT, D])
        if masked:
            y2, y_bias = sb("y2", [P, TT, D]), sb("y_bias", [P, D])
        if qknorm:
            sq = sb("sq", [P, 512])
            lnv = sb("lnv", [P, 512])
            rstdq = sb("rstdq", [P, 512])
            qn = sb("qn", [P, 512])
            k32 = sb("k32", [P, N])
            eps_col = sb("eps_col", [P, 1])
        rstd2, ve2 = sb("rstd2", [P, TT]), sb("ve2", [P, TT])
        if masked:
            kbias = sb("kbias", [P, TT])
            mask_u8 = sb("mask_u8", [P, TT, B], U8)
            key_bias = sb("key_bias", [P, TT, B])
            mrow_u8 = sb("mrow_u8", [P, 2, B, N], U8)
            mrow = sb("mrow", [P, 512], F32R)

        landed = [sem("landed0"), sem("landed1")]
        hi_done, lo_done, centred = sem("hi_done"), sem("lo_done"), sem("centred")
        pre, consts = sem("pre"), sem("consts")
        stats_done, aggr_done, ve_done, rstd_done, xn_done = (sem(x) for x in ("stats", "aggr", "ve", "rstd", "xn"))
        xm_done, xhi_done, xlo_done = sem("xm"), sem("xhi"), sem("xlo")
        pe_first = sem("pe_first")
        turn_done, turn_free = sem("turn_done"), sem("turn_free")
        q32_done, khi_done = sem("q32"), sem("khi")
        qhi_done, qlo_done = sem("qhi"), sem("qlo")
        s_done, mx_done, mxt_done, shift_done = sem("s_done"), sem("mx"), sem("mxt"), sem("shift")
        st_done, p_done, pv_done = sem("st"), sem("p"), sem("pv")
        rsum_done, o_done, ohi_done, olo_done = sem("rsum"), sem("o32"), sem("ohi"), sem("olo")
        gate_in, ep_done, xh_done, ep_step = sem("gate_in"), sem("ep"), sem("xh"), sem("ep_step")
        passed = sem("passed")
        sq_done, var_done, ln_done, rq_done, qn_done, kn_done = (sem(x) for x in ("sq", "var", "lnv", "rq", "qn", "kn"))
        ve2_done, rstd2_done, passed_dve = sem("ve2"), sem("rstd2"), sem("passed_dve")
        mask_in, mrow_done, kb_done = sem("mask_in"), sem("mrow"), sem("kb")

        pieces = []
        part = lambda w, k, c0, c1: w[k * P:(k + 1) * P, c0:c1]
        for w_dram, dst, width in ((t[nm + "_wq"], wq, QW), (t[nm + "_wk"], wk, QW), (t[nm + "_wv"], wv, a.vw)):
            for k in range(KD):
                centred_piece = qknorm and dst is not wv
                pieces.append((w_dram[k * P:(k + 1) * P, :], dst[0][:, k, :], dst[1][:, k, :], centred_piece))
        for c in range(OC):
            pieces.append((t[nm + "_wo"][c * P:(c + 1) * P, :], wo[0][:, c, :], wo[1][:, c, :], False))
        NP_ = len(pieces)

        block = ctx.enter_context(nc.Block())
        loader = lambda sp=None, pool=None, dve=None: split_weights(
            nc, (sp, pool, dve), stage, (landed, hi_done, lo_done), pieces, (means, centred))

        @block.sync
        def _(sp):
            if masked:
                sp.dma_start(mask_u8[:], t["mask_t"].bitcast(U8).rearrange("(k p) b -> p k b", p=P)).then_inc(mask_in, 16)
                for h in range(2):
                    sp.dma_start(mrow_u8[0:1, h, :, :], t["mask"].bitcast(U8).partition_broadcast(1)).then_inc(mask_in, 16)
            if a.gated:
                at = GATE_AT[nm]
                for j in range(2):
                    sp.dma_start(gate[:, j, :], t["gate_rows"][at + j, 0, :].partition_broadcast(P)).then_inc(gate_in, 16)
            elif nm == "L1a":
                sp.dma_start(gate[:, 0, :], t["L1_cond_proj_b"].partition_broadcast(P)).then_inc(gate_in, 16)
            if nm == "L2a":
                sp.dma_start(y_bias[:], t["L2_cond_proj_b"].partition_broadcast(P)).then_inc(gate_in, 16)
            loader(sp=sp)[0]()
            if a.gated:
                extra = 16 if nm == "L2a" else 0
                with sp.Fori(0, B - 1) as i:
                    sp.wait_ge(ep_done, i + 1)
                    for j in range(2):
                        sp.dma_start(gate[:, j, :], t["gate_rows"][at + j, bass.ds(i + 1, 1), :].squeeze(0).partition_broadcast(P)).then_inc(gate_in, 16)

        @block.gpsimd
        def _(pool):
            def gated_wait(s, val):
                pool.wait_ge(s, val)
                pool.sem_inc(passed, 1)

            for slot in range(2):
                nc.gpsimd.memset(shift[:, slot, :].bitcast(F32), 0.0).then_inc(pre, 1)
            if masked:
                nc.gpsimd.memset(mrow[:].bitcast(F32), 0.0).then_inc(pre, 1)
            loader(pool=pool)[1]()

            def token_rstd(i):
                gated_wait(ve_done, i + 1)
                nc.gpsimd.tensor_tensor(rstd[:], ve[:], g["mhalf"][:, 0:TT], ALU.pow).then_inc(rstd_done, 1)

            def x_hi(i):
                gated_wait(xm_done, i + 1)
                nc.gpsimd.tensor_copy(xt[0][:], xm[:]).then_inc(xhi_done, 1)

            if a.norm:
                token_rstd(0)
            x_hi(0)
            with pool.Fori(0, B) as i:
                if qknorm:
                    for c in range(C):
                        gated_wait(kn_done, i * C + c + 1)
                        nc.gpsimd.tensor_copy(k_hi[:, c, :], k32[:]).then_inc(khi_done, 1)
                for step in range(U + 3):
                    if step == 1 and a.norm:
                        token_rstd(i + 1)
                    u = step - 3
                    if u >= 0 and u % a.upc == a.upc - 1:
                        gated_wait(o_done, i * U + u + 1)
                        dst, src = o_slices(a, u // a.upc, o_hi, o32)
                        nc.gpsimd.tensor_copy(dst, src).then_inc(ohi_done, 1)
                    if step == LN_STEP:
                        x_hi(i + 1)
                if a.gated or nm == "L1a":
                    gated_wait(gate_in, (32 * i + 32 + (16 if nm == "L2a" else 0)) if a.gated else 16)
                    for tt in range(TT):
                        hrow = gate[:, 1 if a.gated else 0, :]
                        nc.gpsimd.tensor_tensor(xh[:, tt, :], g["x"][:, bass.ds(i * TT + tt, 1), :].squeeze(1), hrow, ALU.add).then_inc(xh_done, 1)
                if nm == "L2a":
                    gated_wait(ve2_done, i + 1)
                    nc.gpsimd.tensor_tensor(rstd2[:], ve2[:], g["mhalf"][:, 0:TT], ALU.pow).then_inc(rstd2_done, 1)

        @block.scalar
        def _(act):
            with act.Fori(0, B) as i:
                for c in range(C):
                    bank = ring[c % 2]
                    act.wait_ge(turn_done, i * NR + c + 1)
                    if qknorm:
                        nc.scalar.activation(sq[:], bank[:], ACT.Square).then_inc(sq_done, 1)
                        act.wait_ge(var_done, i * C + c + 1)
                        nc.scalar.activation(lnv[:], s_ps[c % 2][:], ACT.Ln, bias=eps_col[:, 0:1], scale=1.0 / a.d).then_inc(ln_done, 1)
                        act.wait_ge(ln_done, i * C + c + 1)
                        if c >= 1:
                            act.wait_ge(qn_done, i * C + c)
                        nc.scalar.activation(rstdq[:], lnv[:], ACT.Exp, scale=-0.5).then_inc(rq_done, 1)
                    else:
                        if nm == "L1a":
                            qb, kb = COL_AT["L1_cond_q_b"] + c, COL_AT["L1_cond_k_b"] + c
                            nc.scalar.activation(q32[:, c, :], bank[:, 0:N], ACT.Identity, bias=cols[:, qb:qb + 1]).then_inc(q32_done, 1)
                            nc.scalar.activation(k_hi[:, c, :], bank[:, N:2 * N], ACT.Identity, bias=cols[:, kb:kb + 1]).then_inc(khi_done, 1)
                        else:
                            nc.scalar.activation(q32[:, c, :], bank[:, 0:N], ACT.Copy).then_inc(q32_done, 1)
                            nc.scalar.activation(k_hi[:, c, :], bank[:, N:2 * N], ACT.Copy).then_inc(khi_done, 1)

                def mask_q(u):
                    if a.one:
                        act.wait_ge(q32_done, i * C + C)
                        nc.scalar.activation(q_hi[:, 0, :], q32[:].rearrange("p c n -> p (c n)"), ACT.Copy).then_inc(qhi_done, 1)
                        return
                    c = 2 * u // a.per_chunk
                    act.wait_ge(q32_done, i * C + c + 1)
                    for h in range(2):
                        m = (2 * u + h) % a.per_chunk
                        ins = nc.scalar.activation(q_hi[:, u % 2, h * N:(h + 1) * N], q32[:, c, :], ACT.Copy,
                                                   scale=g["hmask"][:, MASK0 + m:MASK0 + m + 1])
                    ins.then_inc(qhi_done, 1)

                def exp(u):
                    for kt in range(TT):
                        act.wait_ge(st_done, 2 * (i * U + u) + kt + 1)
                        if u >= 2 and kt == 0:
                            act.wait_ge(pv_done, i * U + u - 1)
                        bias = kbias[:, kt:kt + 1] if masked else 0.0
                        nc.scalar.activation(prob[:, u % 2, kt, 0:HN * N], st_ps[kt][:, 0:HN * N], ACT.Exp,
                                             scale=a.scale, bias=bias).then_inc(p_done, 1)

                for step in range(U + 3):
                    if step == 0:
                        mask_q(0)
                    if 1 <= step <= U:
                        exp(step - 1)
                    if step + 1 < U:
                        mask_q(step + 1)

        @block.tensor
        def _(pe):
            mm = nc.tensor.matmul

            def three(out, lhs, rhs, start, stop):
                mm(out, lhs[0], rhs[0], start=start, stop=False)
                mm(out, lhs[1], rhs[0], start=False, stop=False)
                return mm(out, lhs[0], rhs[1], start=False, stop=stop)

            def transposes(bank):
                for k in range(KD):
                    for tt in range(TT):
                        last = nc.tensor.transpose(bank[:, k * N + tt * P:k * N + (tt + 1) * P],
                                                   xn[:, tt, k * P:(k + 1) * P], g["ident"][:])
                return last

            pe.wait_ge(xn_done, 1)
            transposes(ring[0]).then_inc(pe_first, 1)
            pe.wait_ge(lo_done, NP_)
            pe.wait_ge(pre, 3 if masked else 2)
            def variances(i, c):
                pe.wait_ge(sq_done, i * C + c + 1)
                if c >= 2:
                    pe.wait_ge(ln_done, i * C + c - 1)
                mm(s_ps[c % 2][:], g["block_ones"][:], sq[:], start=True, stop=True).then_inc(var_done, 1)

            with pe.Fori(0, B) as i:
                pe.wait_ge(xlo_done, i + 1)
                for c in range(C):
                    bank = ring[c % 2]
                    pe.wait_ge(turn_free, i * NR + c + 1)
                    for part, w in ((0, wq), (1, wk)):
                        for k in range(KD):
                            last = three(bank[:, part * N:(part + 1) * N],
                                         [w[j][:, k, c * P:(c + 1) * P] for j in range(2)],
                                         [xt[j][:, k, :] for j in range(2)], k == 0, k == KD - 1)
                    last.then_inc(turn_done, 1)
                    if qknorm and c >= 1:
                        variances(i, c - 1)
                if qknorm:
                    variances(i, C - 1)
                for n in range(a.vpieces):
                    tt, c0 = n * a.vpiece // a.vw, n * a.vpiece % a.vw
                    r = C + n
                    pe.wait_ge(turn_free, i * NR + r + 1)
                    for k in range(KD):
                        last = three(ring[r % 2][:, 0:a.vpiece],
                                     [xt[j][:, k, tt * P:(tt + 1) * P] for j in range(2)],
                                     [wv[j][:, k, c0:c0 + a.vpiece] for j in range(2)], k == 0, k == KD - 1)
                    last.then_inc(turn_done, 1)

                def scores(u):
                    pe.wait_ge(qhi_done, i * U + u + 1)
                    if masked and u == 0:
                        pe.wait_ge(mrow_done, i + 1)
                    for qt in range(TT):
                        if masked:
                            mm(s_ps[qt][:], g["ones_r"][:], mrow[:], start=True, stop=False, skip_group_check=True)
                        for h in range(HN):
                            if a.one:
                                for c in range(C):
                                    last = mm(s_ps[qt][:, 0:N], q_hi[:, 0, c * N + qt * P:c * N + (qt + 1) * P],
                                              k_hi[:, c, :], start=(c == 0), stop=(c == C - 1))
                            else:
                                last = mm(s_ps[qt][:, h * N:(h + 1) * N],
                                          q_hi[:, u % 2, h * N + qt * P:h * N + (qt + 1) * P],
                                          k_hi[:, 2 * u // a.per_chunk, :], start=not masked, stop=True,
                                          skip_group_check=masked)
                        last.then_inc(s_done, 1)

                def max_rows(u):
                    pe.wait_ge(mx_done, i * U + u + 1)
                    n = 2 * HN
                    nc.tensor.transpose(sum_ps[0:n, 256:384], mx[:, 0:n], g["ident"][:]).then_inc(mxt_done, 1)

                def scores_t(u):
                    pe.wait_ge(qlo_done, i * U + u + 1)
                    pe.wait_ge(shift_done, i * U + u + 1)
                    for kt in range(TT):
                        if u >= 1:
                            pe.wait_ge(p_done, 2 * (i * U + u) - 1 + kt)
                        out = st_ps[kt][:, 0:HN * N]
                        ks = slice(kt * P, (kt + 1) * P)
                        if a.one:
                            for c in range(C):
                                three(out, [k_hi[:, c, ks], k_lo[:, c, ks]],
                                      [x[:, 0, c * N:(c + 1) * N] for x in (q_hi, q_lo)], c == 0, False)
                        else:
                            c = 2 * u // a.per_chunk
                            three(out, [k_hi[:, c, ks], k_lo[:, c, ks]],
                                  [x[:, u % 2, :] for x in (q_hi, q_lo)], True, False)
                        mm(out, g["ones_r"][:], shift[:, u % 2, 0:HN * N], start=False, stop=True).then_inc(st_done, 1)

                def weighted(u):
                    if u >= 1:
                        pe.wait_ge(o_done, i * U + u)
                    for kt in range(TT):
                        pe.wait_ge(p_done, 2 * (i * U + u) + kt + 1)
                        if a.one:
                            for c in range(C):
                                mm(o_ps[:, c * N:(c + 1) * N], v[:, kt, c * P:(c + 1) * P], prob[:, 0, kt, 0:N],
                                   start=(kt == 0 and c == 0), stop=(kt == TT - 1), skip_group_check=True)
                            last = mm(sum_ps[:, 0:N], g["ones"][:], prob[:, 0, kt, 0:N],
                                      start=(kt == 0), stop=(kt == TT - 1))
                        else:
                            for h in range(2):
                                r = o_row(a, u, h)
                                hd = 2 * u + h
                                mm(o_ps[r:r + a.vd, 0:N], v[:, kt, hd * a.vd:(hd + 1) * a.vd],
                                   prob[:, u % 2, kt, h * N:(h + 1) * N], start=(kt == 0), stop=(kt == TT - 1))
                                last = mm(sum_ps[r:r + a.vd, 0:N], g["ones"][:, 0:a.vd],
                                          prob[:, u % 2, kt, h * N:(h + 1) * N], start=(kt == 0), stop=(kt == TT - 1))
                    last.then_inc(pv_done, 1)

                for step in range(U + 3):
                    if 1 <= step <= U:
                        max_rows(step - 1)
                    if step < U:
                        scores(step)
                    if 1 <= step <= U:
                        scores_t(step - 1)
                    if 2 <= step <= U + 1:
                        weighted(step - 2)
                    if step == LN_STEP:
                        pe.wait_ge(xn_done, i + 2)
                        pe.wait_ge(turn_free, i * NR + LN_AT + 1)
                        transposes(ring[LN_AT % 2]).then_inc(turn_done, 1)
                pe.wait_ge(turn_free, i * NR + OUT_AT + 1)
                pe.wait_ge(olo_done, (i + 1) * a.groups)
                for tt in range(TT):
                    for c in range(OC):
                        last = three(ring[OUT_AT % 2][:, tt * D:(tt + 1) * D],
                                     [o[:, c, tt * P:(tt + 1) * P] for o in (o_hi, o_lo)],
                                     [w[:, c, :] for w in wo], c == 0, c == OC - 1)
                last.then_inc(turn_done, 1)

        @block.vector
        def _(dve):
            V = nc.vector
            tile = lambda j: g["x"][:, bass.ds(j, 1), :].squeeze(1)
            column = lambda row, i: g["mod"][:, row, bass.ds(i, 1)]

            def normalise(j):
                if not a.norm:
                    for tt in range(TT):
                        ins = V.tensor_copy(xn[:, tt, :], tile(j * TT + tt))
                    ins.then_inc(xn_done, 1)
                    return
                for tt in range(TT):
                    V.bn_stats(stats[:, tt, :], tile(j * TT + tt)).then_inc(stats_done, 1)
                for tt in range(TT):
                    dve.wait_ge(stats_done, TT * j + tt + 1)
                    dve.sem_inc(passed_dve, 1)
                    V.bn_aggr(mv[:, tt, :], stats[:, tt, :]).then_inc(aggr_done, 1)
                if a.norm == "rms":
                    dve.wait_ge(aggr_done, (TT + 1) * j + TT)
                    V.tensor_tensor(ve2[:], mv[:, :, 0], mv[:, :, 0], ALU.mult).then_inc(aggr_done, 1)
                    dve.wait_ge(aggr_done, (TT + 1) * j + TT + 1)
                    V.scalar_tensor_tensor(ve[:], ve2[:], a.eps, mv[:, :, 1], ALU.add, ALU.add).then_inc(ve_done, 1)
                else:
                    dve.wait_ge(aggr_done, TT * (j + 1))
                    V.tensor_scalar(ve[:], mv[:, :, 1], a.eps, None, ALU.add).then_inc(ve_done, 1)
                dve.wait_ge(rstd_done, j + 1)
                for tt in range(TT):
                    if a.norm == "rms":
                        ins = V.tensor_scalar(xn[:, tt, :], tile(j * TT + tt), rstd[:, tt:tt + 1], None, ALU.mult)
                    else:
                        ins = V.tensor_scalar(xn[:, tt, :], tile(j * TT + tt), mv[:, tt, 0:1], rstd[:, tt:tt + 1],
                                              ALU.subtract, ALU.mult)
                ins.then_inc(xn_done, 1)

            def modulate(j, bank):
                for k in range(KD):
                    if nm == "L2a":
                        ins = V.tensor_copy(xm[:, k, :], bank[:, k * N:(k + 1) * N])
                    else:
                        at = MOD_AT[nm]
                        ins = V.tensor_scalar(xm[:, k, :], bank[:, k * N:(k + 1) * N], column(at + k, j),
                                              column(at + 2 + k, j), ALU.mult, ALU.add)
                ins.then_inc(xm_done, 1)

            def x_lo(j):
                dve.wait_ge(xhi_done, j + 1)
                V.tensor_tensor(xt[1][:], xm[:], xt[0][:].bitcast(F32), ALU.subtract).then_inc(xlo_done, 1)

            dve.sem_inc(turn_free, 2)
            if qknorm:
                V.memset(eps_col[:], a.eps).then_inc(consts, 1)
            loader(dve=dve)[2]()
            if masked:
                dve.wait_ge(mask_in, 48)
                V.tensor_scalar(key_bias[:], mask_u8[:], 1.0, 3.0e38, ALU.subtract, ALU.mult).then_inc(kb_done, 1)
                dve.wait_ge(kb_done, 1)
                dve.wait_ge(pre, 3)
            normalise(0)
            dve.wait_ge(pe_first, 1)
            modulate(0, ring[0])
            x_lo(0)
            with dve.Fori(0, B) as i:
                if masked:
                    V.tensor_copy(kbias[:], key_bias[:, :, bass.ds(i, 1)].squeeze(2)).then_inc(kb_done, 1)
                    V.tensor_scalar(mrow[0:1, :].rearrange("o (h n) -> o h n", h=2), mrow_u8[0:1, :, bass.ds(i, 1), :].squeeze(2),
                                    1.0, 1.0e30, ALU.subtract, ALU.mult).then_inc(mrow_done, 1)
                for c in range(C):
                    bank = ring[c % 2]
                    if qknorm:
                        dve.wait_ge(rq_done, i * C + c + 1)
                        V.tensor_tensor(qn[:], bank[:], rstdq[:], ALU.mult).then_inc(qn_done, 1)
                        dve.wait_ge(qn_done, i * C + c + 1)
                        dve.sem_inc(turn_free, 1)
                        col = lambda n: cols[:, COL_AT[n]:COL_AT[n] + 1]
                        V.tensor_scalar(q32[:, c, :], qn[:, 0:N], col("qn_g2"), col("qn_b2"), ALU.mult, ALU.add)\
                            .then_inc(q32_done, 1)
                        V.tensor_scalar(k32[:], qn[:, N:2 * N], col("kn_g2"), col("kn_b2"), ALU.mult, ALU.add)\
                            .then_inc(kn_done, 1)
                        dve.wait_ge(khi_done, i * C + c + 1)
                        V.tensor_tensor(k_lo[:, c, :], k32[:], k_hi[:, c, :].bitcast(F32), ALU.subtract)
                    else:
                        dve.wait_ge(khi_done, i * C + c + 1)
                        if nm == "L1a":
                            kb = COL_AT["L1_cond_k_b"] + c
                            ins = V.scalar_tensor_tensor(k_lo[:, c, :], bank[:, N:2 * N], cols[:, kb:kb + 1],
                                                         k_hi[:, c, :].bitcast(F32), ALU.add, ALU.subtract)
                        else:
                            ins = V.tensor_tensor(k_lo[:, c, :], bank[:, N:2 * N], k_hi[:, c, :].bitcast(F32),
                                                  ALU.subtract)
                        ins.then_inc(turn_free, 1)
                for n in range(a.vpieces):
                    tt, c0 = n * a.vpiece // a.vw, n * a.vpiece % a.vw
                    dve.wait_ge(turn_done, i * NR + C + n + 1)
                    V.tensor_copy(v[:, tt, c0:c0 + a.vpiece], ring[(C + n) % 2][:, 0:a.vpiece]).then_inc(turn_free, 1)

                def q_low(u):
                    dve.wait_ge(qhi_done, i * U + u + 1)
                    if a.one:
                        V.tensor_tensor(q_lo[:, 0, :], q32[:].rearrange("p c n -> p (c n)"),
                                        q_hi[:, 0, :].bitcast(F32), ALU.subtract).then_inc(qlo_done, 1)
                        return
                    for h in range(2):
                        m = MASK0 + (2 * u + h) % a.per_chunk
                        ins = V.scalar_tensor_tensor(q_lo[:, u % 2, h * N:(h + 1) * N], q32[:, 2 * u // a.per_chunk, :],
                                                     g["hmask"][:, m:m + 1],
                                                     q_hi[:, u % 2, h * N:(h + 1) * N].bitcast(F32),
                                                     ALU.mult, ALU.subtract)
                    ins.then_inc(qlo_done, 1)

                def maxes(u):
                    for qt in range(TT):
                        dve.wait_ge(s_done, 2 * (i * U + u) + qt + 1)
                        ins = V.tensor_reduce(mx[:, 0:2 * HN].rearrange("p (h q) -> p h q", q=2)[:, :, qt],
                                              s_ps[qt][:, 0:HN * N].rearrange("p (h n) -> p h n", h=HN), AX.X, ALU.max)
                    ins.then_inc(mx_done, 1)

                def shifts(u):
                    dve.wait_ge(mxt_done, i * U + u + 1)
                    if u >= 2:
                        dve.wait_ge(st_done, 2 * (i * U + u) - 2)
                    n = 2 * HN
                    rows = sum_ps[0:n, 256:384].unsqueeze(1).to_broadcast([n, n, P])
                    V.tensor_tensor(shift[0:n, u % 2, 0:HN * N].rearrange("r (b q) -> r b q", q=P),
                                    g["neg_block"][0:n, 0:HN * N].rearrange("r (b q) -> r b q", q=P),
                                    rows, ALU.mult).then_inc(shift_done, 1)

                def outputs(u):
                    rows = o_rows(a, u)
                    dve.wait_ge(pv_done, i * U + u + 1)
                    V.reciprocal(rsum[rows, 0:N], sum_ps[rows, 0:N]).then_inc(rsum_done, 1)
                    if a.one:
                        dve.wait_ge(rsum_done, 3 * i + 1)
                        for c in range(C):
                            V.tensor_tensor(o32[:, 0, c * N:(c + 1) * N], o_ps[:, c * N:(c + 1) * N], rsum[:, 0:N],
                                            ALU.mult).then_inc(rsum_done, 1)
                        dve.wait_ge(rsum_done, 3 * i + 3)
                        for c in range(C):
                            vb = COL_AT["L1_cond_v_b"] + c
                            ins = V.tensor_scalar(o32[:, 0, c * N:(c + 1) * N], o32[:, 0, c * N:(c + 1) * N],
                                                  cols[:, vb:vb + 1], None, ALU.add)
                        ins.then_inc(o_done, 1)
                    else:
                        dve.wait_ge(rsum_done, i * U + u + 1)
                        V.tensor_tensor(o32[rows, u // a.upc % 2, 0:N], o_ps[rows, 0:N], rsum[rows, 0:N], ALU.mult)\
                            .then_inc(o_done, 1)

                def o_low(c):
                    dve.wait_ge(ohi_done, i * a.groups + c + 1)
                    hi, src = o_slices(a, c, o_hi, o32)
                    lo, _ = o_slices(a, c, o_lo, o32)
                    V.tensor_tensor(lo, src, hi.bitcast(F32), ALU.subtract).then_inc(olo_done, 1)

                for step in range(U + 3):
                    if step == 0:
                        q_low(0)
                    if 1 <= step <= U:
                        shifts(step - 1)
                    if step < U:
                        maxes(step)
                    if step + 1 < U:
                        q_low(step + 1)
                    if step == 1:
                        normalise(i + 1)
                    if step >= 3:
                        outputs(step - 3)
                        if (step - 3) % a.upc == a.upc - 1:
                            o_low((step - 3) // a.upc)
                    if step == LN_STEP:
                        dve.wait_ge(turn_done, i * NR + LN_AT + 1)
                        modulate(i + 1, ring[LN_AT % 2])
                        dve.wait_ge(xm_done, i + 2)
                        dve.sem_inc(turn_free, 1)
                        x_lo(i + 1)
                bank = ring[OUT_AT % 2]
                dve.wait_ge(turn_done, i * NR + OUT_AT + 1)
                gates_at = None
                if a.gated:
                    gates_at = (gate_in, 32 * i + 32 + (16 if nm == "L2a" else 0))
                residual(nc, dve, {"step": ep_step, "done": ep_done, "xh": xh_done, "ve2": ve2_done, "rstd2": rstd2_done, "passed": passed_dve},
                         nm, i, [i * TT + tt for tt in range(TT)], [bank[:, tt * D:(tt + 1) * D] for tt in range(TT)],
                         lambda j: gate[:, 0, :], a.eps, (y, y2, xh, stats, mv, ve2, rstd2, y_bias), g,
                         residual_steps(nm, TT), gates_at)
                dve.wait_ge(ep_done, i + 1)
                dve.sem_inc(turn_free, 1)


BB = 2
T4 = BB * TT
NN = BB * N


def mlp(nc, t, g, nm, norm, eps):
    gated = nm != "L1m"
    with semaphores(nc, nm) as sem, ExitStack() as ctx:
        sb = lambda n, s, d=F32: ctx.enter_context(nc.sbuf_tensor(f"{nm}_{n}", s, d))
        pb = lambda n: ctx.enter_context(nc.psum_tensor(f"{nm}_{n}", [P, 512], F32))
        up_ps, tp_ps, down_ps = [pb(f"up{j}") for j in range(2)], [pb(f"tp{k}") for k in range(KD)], \
            [pb(f"down{j}") for j in range(T4)]
        w1 = [sb(f"w1{j}", [P, KD, MLP], F32R) for j in range(2)]
        w2 = [sb(f"w2{j}", [P, MC, D], F32R) for j in range(2)]
        stage = sb("stage", [P, 2, 1024])
        xn, xm = sb("xn", [P, T4, D]), sb("xm", [P, KD, NN])
        xt = [sb(f"xt{j}", [P, KD, NN], F32R) for j in range(2)]
        stats, mv = sb("stats", [P, T4, 6]), sb("mv", [P, T4, 2])
        ve, ve2, rstd, rstd2 = sb("ve", [P, T4]), sb("ve2", [P, T4]), sb("rstd", [P, T4]), sb("rstd2", [P, T4])
        h32 = sb("h32", [P, 2, NN])
        h = [sb(f"h{j}", [P, MC, NN], F32R) for j in range(2)]
        y, y2, xh = sb("y", [P, T4, D]), sb("y2", [P, T4, D]), sb("xh", [P, T4, D])
        gate, y_bias = sb("gate", [P, BB, 2, D]), sb("y_bias", [P, D])

        landed = [sem("landed0"), sem("landed1")]
        hi_done, lo_done = sem("hi_done"), sem("lo_done")
        stats_done, aggr_done, ve_done, rstd_done, xn_done = (sem(x) for x in ("stats", "aggr", "ve", "rstd", "xn"))
        tp_done, xm_done, xhi_done, xlo_done = sem("tp"), sem("xm"), sem("xhi"), sem("xlo")
        up_done, gelu_done, hhi_done, hlo_done = sem("up"), sem("gelu"), sem("hhi"), sem("hlo")
        down_done, down_free, ep_done, ep_step, xh_done = (sem(x) for x in ("down", "down_free", "ep", "ep_step", "xh"))
        gate_in, ve2_done, rstd2_done, passed = sem("gate_in"), sem("ve2"), sem("rstd2"), sem("passed")
        passed_dve = sem("passed_dve")

        pieces = []
        for k in range(KD):
            pieces.append((t[nm + "_w1"][k * P:(k + 1) * P, :], w1[0][:, k, :], w1[1][:, k, :], False))
        for m in range(MC):
            pieces.append((t[nm + "_w2"][m * P:(m + 1) * P, :], w2[0][:, m, :], w2[1][:, m, :], False))
        loader = lambda sp=None, pool=None, dve=None: split_weights(
            nc, (sp, pool, dve), stage, (landed, hi_done, lo_done), pieces)
        extra = 16 if nm == "L2m" else 0
        gates_in = lambda i: 16 * 2 * BB * i + 16 * 2 * BB + extra
        IT = B // BB
        block = ctx.enter_context(nc.Block())

        @block.sync
        def _(sp):
            if gated:
                at = GATE_AT[nm]
                for bb in range(BB):
                    for j in range(2):
                        sp.dma_start(gate[:, bb, j, :], t["gate_rows"][at + j, bb, :].partition_broadcast(P)).then_inc(gate_in, 16)
            else:
                sp.dma_start(gate[:, 0, 0, :], t["L1_cond_mlp_b2"].partition_broadcast(P)).then_inc(gate_in, 16)
            if nm == "L2m":
                sp.dma_start(y_bias[:], t["L2_cond_fc2_b"].partition_broadcast(P)).then_inc(gate_in, 16)
            loader(sp=sp)[0]()
            if gated:
                with sp.Fori(0, IT - 1) as i:
                    sp.wait_ge(ep_done, i + 1)
                    for bb in range(BB):
                        for j in range(2):
                            sp.dma_start(gate[:, bb, j, :], t["gate_rows"][at + j, bass.ds(BB * i + BB + bb, 1), :]
                                         .squeeze(0).partition_broadcast(P)).then_inc(gate_in, 16)

        @block.gpsimd
        def _(pool):
            def gated_wait(s, val):
                pool.wait_ge(s, val)
                pool.sem_inc(passed, 1)

            def token_rstd(j):
                if norm:
                    gated_wait(ve_done, j + 1)
                    nc.gpsimd.tensor_tensor(rstd[:], ve[:], g["mhalf"][:, 0:T4], ALU.pow).then_inc(rstd_done, 1)

            def x_hi(j):
                gated_wait(xm_done, j + 1)
                nc.gpsimd.tensor_copy(xt[0][:], xm[:]).then_inc(xhi_done, 1)

            loader(pool=pool)[1]()
            token_rstd(0)
            x_hi(0)
            with pool.Fori(0, IT) as i:
                for m in range(MC):
                    gated_wait(gelu_done, MC * i + m + 1)
                    nc.gpsimd.tensor_copy(h[0][:, m, :], h32[:, m % 2, :]).then_inc(hhi_done, 1)
                    if m == 3:
                        token_rstd(i + 1)
                x_hi(i + 1)
                gated_wait(gate_in, gates_in(i) if gated else 16)
                for j in range(T4):
                    hrow = gate[:, j // TT, 1, :] if gated else gate[:, 0, 0, :]
                    nc.gpsimd.tensor_tensor(xh[:, j, :], g["x"][:, bass.ds(i * T4 + j, 1), :].squeeze(1), hrow,
                                            ALU.add).then_inc(xh_done, 1)
                if nm == "L2m":
                    gated_wait(ve2_done, i + 1)
                    nc.gpsimd.tensor_tensor(rstd2[:], ve2[:], g["mhalf"][:, 0:T4], ALU.pow).then_inc(rstd2_done, 1)

        @block.scalar
        def _(act):
            b1 = COL_AT[{"L0m": "L0_cond_b1", "L1m": "L1_cond_mlp_b1", "L2m": "L2_cond_fc1_b"}[nm]]
            with act.Fori(0, IT) as i:
                for m in range(MC):
                    act.wait_ge(up_done, MC * i + m + 1)
                    if m >= 2:
                        act.wait_ge(hlo_done, MC * i + m - 1)
                    nc.scalar.activation(h32[:, m % 2, :], up_ps[m % 2][:], ACT.Gelu,
                                         bias=g["cols"][:, b1 + m:b1 + m + 1]).then_inc(gelu_done, 1)

        @block.tensor
        def _(pe):
            mm = nc.tensor.matmul

            def three(out, lhs, rhs, start, stop):
                mm(out, lhs[0], rhs[0], start=start, stop=False)
                mm(out, lhs[1], rhs[0], start=False, stop=False)
                return mm(out, lhs[0], rhs[1], start=False, stop=stop)

            def transposes(j):
                pe.wait_ge(xn_done, j + 1)
                for k in range(KD):
                    for tt in range(T4):
                        last = nc.tensor.transpose(tp_ps[k][:, tt * P:(tt + 1) * P], xn[:, tt, k * P:(k + 1) * P],
                                                   g["ident"][:])
                last.then_inc(tp_done, 1)

            transposes(0)
            pe.wait_ge(lo_done, len(pieces))
            with pe.Fori(0, IT) as i:
                pe.wait_ge(xlo_done, i + 1)
                for m in range(MC):
                    if m >= 2:
                        pe.wait_ge(gelu_done, MC * i + m - 1)
                    for k in range(KD):
                        last = three(up_ps[m % 2][:], [w[:, k, m * P:(m + 1) * P] for w in w1],
                                     [x[:, k, :] for x in xt], k == 0, k == KD - 1)
                    last.then_inc(up_done, 1)
                pe.wait_ge(down_free, i + 1)
                for m in range(MC):
                    pe.wait_ge(hlo_done, MC * i + m + 1)
                    for tt in range(T4):
                        last = three(down_ps[tt][:, 0:D], [x[:, m, tt * P:(tt + 1) * P] for x in h],
                                     [w[:, m, :] for w in w2], m == 0, m == MC - 1)
                    if m == 3:
                        transposes(i + 1)
                last.then_inc(down_done, 1)

        @block.vector
        def _(dve):
            V = nc.vector
            tile = lambda j: g["x"][:, bass.ds(j, 1), :].squeeze(1)

            def normalise(j):
                if not norm:
                    for tt in range(T4):
                        ins = V.tensor_copy(xn[:, tt, :], tile(j * T4 + tt))
                    ins.then_inc(xn_done, 1)
                    return
                for tt in range(T4):
                    V.bn_stats(stats[:, tt, :], tile(j * T4 + tt)).then_inc(stats_done, 1)
                for tt in range(T4):
                    dve.wait_ge(stats_done, T4 * j + tt + 1)
                    dve.sem_inc(passed_dve, 1)
                    V.bn_aggr(mv[:, tt, :], stats[:, tt, :]).then_inc(aggr_done, 1)
                if norm == "rms":
                    dve.wait_ge(aggr_done, (T4 + 1) * j + T4)
                    V.tensor_tensor(ve2[:], mv[:, :, 0], mv[:, :, 0], ALU.mult).then_inc(aggr_done, 1)
                    dve.wait_ge(aggr_done, (T4 + 1) * j + T4 + 1)
                    V.scalar_tensor_tensor(ve[:], ve2[:], eps, mv[:, :, 1], ALU.add, ALU.add).then_inc(ve_done, 1)
                else:
                    dve.wait_ge(aggr_done, T4 * (j + 1))
                    V.tensor_scalar(ve[:], mv[:, :, 1], eps, None, ALU.add).then_inc(ve_done, 1)
                dve.wait_ge(rstd_done, j + 1)
                for tt in range(T4):
                    if norm == "rms":
                        ins = V.tensor_scalar(xn[:, tt, :], tile(j * T4 + tt), rstd[:, tt:tt + 1], None, ALU.mult)
                    else:
                        ins = V.tensor_scalar(xn[:, tt, :], tile(j * T4 + tt), mv[:, tt, 0:1], rstd[:, tt:tt + 1],
                                              ALU.subtract, ALU.mult)
                ins.then_inc(xn_done, 1)

            def modulate(j):
                dve.wait_ge(tp_done, j + 1)
                for k in range(KD):
                    if not norm:
                        ins = V.tensor_copy(xm[:, k, :], tp_ps[k][:])
                        continue
                    at = MOD_AT[nm]
                    for bb in range(BB):
                        col = lambda row: g["mod"][:, row, bass.ds(BB * j + bb, 1)]
                        ins = V.tensor_scalar(xm[:, k, bb * N:(bb + 1) * N], tp_ps[k][:, bb * N:(bb + 1) * N],
                                              col(at + k), col(at + 2 + k), ALU.mult, ALU.add)
                ins.then_inc(xm_done, 1)
                dve.wait_ge(xhi_done, j + 1)
                V.tensor_tensor(xt[1][:], xm[:], xt[0][:].bitcast(F32), ALU.subtract).then_inc(xlo_done, 1)

            dve.sem_inc(down_free, 1)
            loader(dve=dve)[2]()
            normalise(0)
            modulate(0)
            with dve.Fori(0, IT) as i:
                for m in range(MC):
                    dve.wait_ge(hhi_done, MC * i + m + 1)
                    V.tensor_tensor(h[1][:, m, :], h32[:, m % 2, :], h[0][:, m, :].bitcast(F32), ALU.subtract)\
                        .then_inc(hlo_done, 1)
                    if m == 3:
                        normalise(i + 1)
                modulate(i + 1)
                dve.wait_ge(down_done, i + 1)
                residual(nc, dve, {"step": ep_step, "done": ep_done, "xh": xh_done, "ve2": ve2_done, "rstd2": rstd2_done, "passed": passed_dve},
                         nm, i, [i * T4 + tt for tt in range(T4)], [p[:, 0:D] for p in down_ps],
                         lambda j: gate[:, j // TT, 0, :], eps, (y, y2, xh, stats, mv, ve2, rstd2, y_bias), g,
                         residual_steps(nm, T4), (gate_in, gates_in(i)) if gated else None)
                dve.wait_ge(ep_done, i + 1)
                dve.sem_inc(down_free, 1)


BF16 = mybir.dt.bfloat16
ROW = D + E
BITS = 30


def route(nc, t, g, out):
    with semaphores(nc, "r") as sem, ExitStack() as ctx:
        sb = lambda n, s, d=F32: ctx.enter_context(nc.sbuf_tensor(f"r_{n}", s, d))
        pb = lambda n: ctx.enter_context(nc.psum_tensor(f"r_{n}", [P, 512], F32))
        tp_ps, lg_ps, cnt_ps, pre_ps, tot_ps = [pb("tp0"), pb("tp1")], pb("lg"), pb("cnt"), pb("pre"), pb("tot")
        list_ps = [pb("list0"), pb("list1")]
        wg, tri, iota_f = sb("wg", [P, KD, E]), sb("tri", [P, P]), sb("iota_f", [P, P])
        tval, pval = sb("tval", [P, TILES]), sb("pval", [P, 1])
        xs, xt = sb("xs", [P, T4, D]), sb("xt", [P, KD, NN])
        logit = sb("logit", [P, TILES, E])
        lmax, lsum, lrec, e_base = sb("lmax", [P, TILES]), sb("lsum", [P, TILES]), sb("lrec", [P, TILES]), sb("e_base", [P, TILES * E])
        centred, ex, gates = (sb(n, [P, TILES, E]) for n in ("centred", "ex", "gates"))
        ge = sb("ge", [P, E, TILES])
        thr, cand, bit = (sb(n, [P, E], U32) for n in ("thr", "cand", "bit"))
        hit, keep = sb("hit", [P, E, TILES]), sb("keep", [P, E], U32)
        part_count, need = sb("part_count", [P, E]), sb("need", [P, E])
        above, equal, sel = (sb(n, [P, E, TILES]) for n in ("above", "equal", "sel"))
        totals, scan, zeros = (sb(n, [P, E, TILES]) for n in ("totals", "scan", "zeros"))
        rank, low = sb("rank", [P, E, TILES]), sb("low", [P, E, TILES])
        ge_h = [sb(f"ge_h{h}", [P, E, TILES]) for h in range(SC + 1)]
        hs = sb("hs", [P, E, TILES])
        vals = sb("vals", [P, E, TILES, 2 * SC], BF16)
        onehot = sb("onehot", [P, 2, TILES, P], BF16)
        iota_b, low_b = sb("iota_b", [P, P], BF16), sb("low_b", [P, E, TILES], BF16)
        lists, idx_f = sb("lists", [P, E, 2 * SC]), sb("idx_f", [P, E, SC])

        const_in, xs_done, tp_done, xt_done, lg_done, lgc_done = (sem(n) for n in ("const", "xs", "tp", "xt", "lg", "lgc"))
        xt2_done, pow_in, pow_done, chain, made = sem("xt2"), sem("pow_in"), sem("pow"), sem("chain"), sem("made")
        count_in, count_done, pre_in, pre_done = sem("count_in"), sem("count_done"), sem("pre_in"), sem("pre_done")
        hot_done, list_done, list_read, stored, rows_ready = (sem(n) for n in ("hot", "list", "list_read", "stored", "rows"))
        bchain, passed = sem("bchain"), sem("passed")
        IT = TILES // T4
        block = ctx.enter_context(nc.Block())

        @block.sync
        def _(sp):
            for dst, name in ((tri, "tri"), (iota_f, "iota"), (tval, "tval"), (pval, "pval")):
                sp.dma_start(dst[:], t[name]).then_inc(const_in, 16)
            sp.dma_start(wg[:], t["wg_t"].rearrange("(k p) e -> p k e", p=P)).then_inc(const_in, 16)
            sp.dma_start(out.rearrange("b (t p) d -> p (b t) d", p=P), g["x"][:, 0:TILES, :]).then_inc(stored, 16)
            rows = t["token_rows"].rearrange("(t p) r -> p t r", p=P)
            sp.dma_start(rows[:, :, 0:D], g["x"][:, 0:TILES, :]).then_inc(stored, 16)
            sp.wait_ge(rows_ready, 1)
            sp.dma_start(rows[:, :, D:ROW], gates[:]).then_inc(stored, 16)
            sp.wait_ge(stored, 48)

        @block.gpsimd
        def _(pool):
            nc.gpsimd.memset(e_base[:], float(np.e)).then_inc(made, 1)
            nc.gpsimd.memset(zeros[:], 0.0).then_inc(made, 1)
            pool.wait_ge(pow_in, 1)
            pool.wait_ge(made, 2)
            nc.gpsimd.tensor_tensor(ex[:].rearrange("p t e -> p (t e)"), e_base[:],
                                    centred[:].rearrange("p t e -> p (t e)"), ALU.pow).then_inc(pow_done, 1)

        @block.scalar
        def _(act):
            with act.Fori(0, IT) as i:
                act.wait_ge(tp_done, i + 1)
                nc.scalar.activation(xt[:, 1, :], tp_ps[1][:], ACT.Copy).then_inc(xt2_done, 1)

        @block.tensor
        def _(pe):
            mm = nc.tensor.matmul
            pe.wait_ge(const_in, 80)
            with pe.Fori(0, IT) as i:
                pe.wait_ge(xs_done, i + 1)
                for k in range(KD):
                    for tt in range(T4):
                        last = nc.tensor.transpose(tp_ps[k][:, tt * P:(tt + 1) * P], xs[:, tt, k * P:(k + 1) * P],
                                                   g["ident"][:])
                last.then_inc(tp_done, 1)
                pe.wait_ge(xt_done, i + 1)
                pe.wait_ge(xt2_done, i + 1)
                for tt in range(T4):
                    for k in range(KD):
                        last = mm(lg_ps[:, tt * E:(tt + 1) * E], xt[:, k, tt * P:(tt + 1) * P], wg[:, k, :],
                                  start=(k == 0), stop=(k == KD - 1))
                last.then_inc(lg_done, 1)
            with pe.Fori(0, BITS + 1) as n:
                pe.wait_ge(count_in, n + 1)
                mm(cnt_ps[:, 0:E], g["ones"][:], part_count[:], start=True, stop=True).then_inc(count_done, 1)
            for n, what in enumerate((equal, sel)):
                pe.wait_ge(pre_in, n + 1)
                flat = what[:].rearrange("p e t -> p (e t)")
                mm(pre_ps[:, 0:E * TILES], tri[:], flat, start=True, stop=True)
                mm(tot_ps[:, 0:E * TILES], g["ones"][:], flat, start=True, stop=True).then_inc(pre_done, 1)
            with pe.Fori(0, E // 2) as i:
                for par in range(2):
                    pe.wait_ge(hot_done, 2 * i + par + 1)
                    for tile in range(TILES):
                        last = mm(list_ps[par][:, 0:2 * SC], onehot[:, par, tile, :],
                                  vals[:, bass.ds(2 * i + par, 1), tile, :].squeeze(1),
                                  start=(tile == 0), stop=(tile == TILES - 1))
                    last.then_inc(list_done, 1)

        @block.vector
        def _(dve):
            V = nc.vector
            done = [0]

            def step(ins):
                done[0] += 1
                ins.then_inc(chain, 1)
                dve.wait_ge(chain, done[0])

            with dve.Fori(0, IT) as i:
                V.tensor_copy(xs[:], g["x"][:, bass.ds(i * T4, T4), :]).then_inc(xs_done, 1)
                dve.wait_ge(tp_done, i + 1)
                V.tensor_copy(xt[:, 0, :], tp_ps[0][:]).then_inc(xt_done, 1)
                dve.wait_ge(lg_done, i + 1)
                V.tensor_copy(logit[:, bass.ds(i * T4, T4), :], lg_ps[:, 0:T4 * E].rearrange("p (t e) -> p t e", e=E))\
                    .then_inc(lgc_done, 1)
            dve.wait_ge(lgc_done, IT)
            bc = lambda col: col[:].unsqueeze(2).to_broadcast([P, TILES, E])
            step(V.tensor_reduce(lmax[:], logit[:], AX.X, ALU.max))
            step(V.tensor_tensor(centred[:], logit[:], bc(lmax), ALU.subtract))
            V.engine_nop().then_inc(pow_in, 1)
            dve.wait_ge(pow_done, 1)
            step(V.tensor_reduce(lsum[:], ex[:], AX.X, ALU.add))
            step(V.reciprocal(lrec[:], lsum[:]))
            step(V.tensor_tensor(gates[:], ex[:], bc(lrec), ALU.mult))
            V.engine_nop().then_inc(rows_ready, 1)
            step(V.tensor_copy(ge[:], gates[:].rearrange("p t e -> p e t")))
            step(V.memset(thr[:], 0))
            step(V.memset(bit[:], 1 << (BITS - 1)))
            over = lambda col: col[:].unsqueeze(2).to_broadcast([P, E, TILES])
            per = 5
            with dve.Fori(0, BITS) as n:
                V.tensor_tensor(cand[:], thr[:], bit[:], ALU.bitwise_or).then_inc(bchain, 1)
                dve.wait_ge(bchain, per * n + 1)
                V.tensor_tensor(hit[:], ge[:], over(cand).bitcast(F32), ALU.is_ge).then_inc(bchain, 1)
                V.tensor_scalar(bit[:], bit[:], 1, None, ALU.logical_shift_right).then_inc(bchain, 1)
                dve.wait_ge(bchain, per * n + 3)
                V.tensor_reduce(part_count[:], hit[:], AX.X, ALU.add).then_inc(count_in, 1)
                dve.wait_ge(count_done, n + 1)
                V.tensor_scalar(keep[:], cnt_ps[:, 0:E], float(CAP), None, ALU.is_ge).then_inc(bchain, 1)
                dve.wait_ge(bchain, per * n + 4)
                dve.sem_inc(passed, 1)
                V.copy_predicated(thr[:], keep[:], cand[:]).then_inc(bchain, 1)
                dve.wait_ge(bchain, per * n + 5)
            th = over(thr).bitcast(F32)
            step(V.tensor_tensor(above[:], ge[:], th, ALU.is_gt))
            step(V.tensor_tensor(equal[:], ge[:], th, ALU.is_equal))
            V.tensor_reduce(part_count[:], above[:], AX.X, ALU.add).then_inc(count_in, 1)
            V.engine_nop().then_inc(pre_in, 1)
            dve.wait_ge(count_done, BITS + 1)
            step(V.tensor_scalar(need[:], cnt_ps[:, 0:E], -1.0, float(CAP), ALU.mult, ALU.add))

            def ranks(n):
                dve.wait_ge(pre_done, n + 1)
                step(V.tensor_copy(totals[:].rearrange("p e t -> p (e t)"), tot_ps[:, 0:E * TILES]))
                for e in range(E):
                    step(V.tensor_tensor_scan(scan[:, e, :], totals[:, e, :], zeros[:, e, :], 0.0, ALU.add, ALU.add))
                step(V.tensor_tensor(scan[:], scan[:], totals[:], ALU.subtract))
                step(V.tensor_tensor(rank[:], pre_ps[:, 0:E * TILES].rearrange("p (e t) -> p e t", t=TILES),
                                     scan[:], ALU.add))

            dve.wait_ge(made, 2)
            dve.wait_ge(const_in, 80)
            ranks(0)
            step(V.tensor_tensor(sel[:], rank[:], over(need), ALU.is_lt))
            step(V.tensor_tensor(sel[:], sel[:], equal[:], ALU.mult))
            step(V.tensor_tensor(sel[:], sel[:], above[:], ALU.add))
            V.engine_nop().then_inc(pre_in, 1)
            ranks(1)
            for h in range(1, SC):
                step(V.tensor_scalar(ge_h[h][:], rank[:], float(P * h), None, ALU.is_ge))
            step(V.scalar_tensor_tensor(low[:], ge_h[1][:], -float(P), rank[:], ALU.mult, ALU.add))
            for h in range(2, SC):
                step(V.scalar_tensor_tensor(low[:], ge_h[h][:], -float(P), low[:], ALU.mult, ALU.add))
            step(V.scalar_tensor_tensor(low[:], low[:], 1.0, sel[:], ALU.add, ALU.mult))
            step(V.tensor_scalar(low_b[:], low[:], -1.0, None, ALU.add))
            step(V.tensor_copy(iota_b[:], iota_f[:]))
            step(V.memset(ge_h[0][:], 1.0))
            step(V.memset(ge_h[SC][:], 0.0))
            for h in range(SC):
                step(V.tensor_tensor(hs[:], ge_h[h][:], ge_h[h + 1][:], ALU.subtract))
                step(V.tensor_tensor(vals[:, :, :, 2 * h], hs[:], tval[:].unsqueeze(1).to_broadcast([P, E, TILES]), ALU.mult))
                step(V.tensor_scalar(vals[:, :, :, 2 * h + 1], hs[:], pval[:, 0:1], None, ALU.mult))
            with dve.Fori(0, E // 2) as i:
                for par in range(2):
                    V.tensor_tensor(onehot[:, par, :, :], iota_b[:].unsqueeze(1).to_broadcast([P, TILES, P]),
                                    low_b[:, bass.ds(2 * i + par, 1), :].squeeze(1).unsqueeze(2).to_broadcast([P, TILES, P]),
                                    ALU.is_equal).then_inc(hot_done, 1)
                for par in range(2):
                    dve.wait_ge(list_done, 2 * i + par + 1)
                    V.tensor_copy(lists[:, bass.ds(2 * i + par, 1), :].squeeze(1), list_ps[par][:, 0:2 * SC]).then_inc(list_read, 1)
            dve.wait_ge(list_read, E)
            pairs = lists[:].rearrange("p e (h two) -> p e h two", two=2)
            step(V.scalar_tensor_tensor(idx_f[:], pairs[:, :, :, 0], float(P), pairs[:, :, :, 1], ALU.mult, ALU.add))
            step(V.tensor_copy(g["idx"][:], idx_f[:]))


def experts(nc, t, g, out):
    nm = "moe"
    with semaphores(nc, nm) as sem, ExitStack() as ctx:
        sb = lambda n, s, d=F32: ctx.enter_context(nc.sbuf_tensor(f"{nm}_{n}", s, d))
        pb = lambda n: ctx.enter_context(nc.psum_tensor(f"{nm}_{n}", [P, 512], F32))
        up_ps, tp_ps, down_ps = [pb(f"up{j}") for j in range(2)], [pb(f"tp{k}") for k in range(KD)], \
            [pb(f"down{j}") for j in range(SC)]
        stage1, stage2 = sb("stage1", [P, KD, MLP]), sb("stage2", [P, MC, D])
        w1 = [sb(f"w1{j}", [P, KD, MLP], F32R) for j in range(2)]
        w2 = [sb(f"w2{j}", [P, MC, D], F32R) for j in range(2)]
        idx_now, idx_out = sb("idx_now", [P, SC], U32), sb("idx_out", [P, SC], U32)
        xg = sb("xg", [P, SC, ROW])
        weight, weight_next = sb("weight", [P, SC]), sb("weight_next", [P, SC])
        xn, xm = sb("xn", [P, SC, D]), sb("xm", [P, KD, CAP])
        xt = [sb(f"xt{j}", [P, KD, CAP], F32R) for j in range(2)]
        stats, mv = sb("stats", [P, SC, 6]), sb("mv", [P, SC, 2])
        ve, rstd = sb("ve", [P, SC]), sb("rstd", [P, SC])
        h32 = sb("h32", [P, 2, CAP])
        h = [sb(f"h{j}", [P, MC, CAP], F32R) for j in range(2)]
        b2, y, y2 = sb("b2", [P, D]), sb("y", [P, SC, D]), sb("y2", [P, SC, D])

        stats_done, aggr_done, ve_done, rstd_done, xn_done = (sem(x) for x in ("stats", "aggr", "ve", "rstd", "xn"))
        tp_done, xm_done, xhi_done, xlo_done = sem("tp"), sem("xm"), sem("xhi"), sem("xlo")
        up_done, gelu_done, hhi_done, hlo_done = sem("up"), sem("gelu"), sem("hhi"), sem("hlo")
        down_done, down_free, y_step, y_done = sem("down"), sem("down_free"), sem("y_step"), sem("y_done")
        w1_in, w2_in, b2_in, w1_hi, w1_lo, w2_hi, w2_lo = (sem(x) for x in ("w1_in", "w2_in", "b2_in", "w1_hi", "w1_lo", "w2_hi", "w2_lo"))
        idx_done, gathered, scattered, weight_done, passed, passed_dve = (sem(x) for x in ("idx", "gathered", "scattered", "weight", "passed", "passed_dve"))
        idxo_done, weight_now, y2_free = sem("idxo"), sem("weight_now"), sem("y2_free")
        block = ctx.enter_context(nc.Block())
        w1_d = t["moe_w1"].rearrange("e (k p) n -> e p k n", p=P)
        w2_d = t["moe_w2"].rearrange("e (m p) n -> e p m n", p=P)

        @block.sync
        def _(sp):
            sp.dma_start(stage1[:], w1_d[0]).then_inc(w1_in, 16)
            sp.dma_start(stage2[:], w2_d[0]).then_inc(w2_in, 16)
            sp.dma_start(b2[:], t["L3_cond_b2s"][0, :].partition_broadcast(P)).then_inc(b2_in, 16)
            with sp.Fori(0, E - 1) as e:
                sp.wait_ge(w1_lo, e + 1)
                sp.dma_start(stage1[:], w1_d[bass.ds(e + 1, 1), :, :, :].squeeze(0)).then_inc(w1_in, 16)
                sp.wait_ge(w2_lo, e + 1)
                sp.dma_start(stage2[:], w2_d[bass.ds(e + 1, 1), :, :, :].squeeze(0)).then_inc(w2_in, 16)
                sp.wait_ge(y_done, e + 1)
                sp.dma_start(b2[:], t["L3_cond_b2s"][bass.ds(e + 1, 1), :].squeeze(0).partition_broadcast(P)).then_inc(b2_in, 16)

        @block.gpsimd
        def _(pool):
            def gated_wait(s, val):
                pool.wait_ge(s, val)
                pool.sem_inc(passed, 1)

            def gather(e):
                nc.gpsimd.tensor_copy(idx_now[:], g["idx"][:, bass.ds(e, 1), :].squeeze(1)).then_inc(idx_done, 1)
                gated_wait(idx_done, e + 1)
                for s in range(SC):
                    pool.indirect_dma_start(xg[:, s, :], None, t["token_rows"][:, :],
                                            bass.IndirectOffsetOnAxis(ap=idx_now[:, s:s + 1], axis=0)).then_inc(gathered, 16)

            def token_rstd(e):
                gated_wait(ve_done, e + 1)
                nc.gpsimd.tensor_tensor(rstd[:], ve[:], g["mhalf"][:, 0:SC], ALU.pow).then_inc(rstd_done, 1)

            def x_hi(e):
                gated_wait(xm_done, e + 1)
                nc.gpsimd.tensor_copy(xt[0][:], xm[:]).then_inc(xhi_done, 1)

            def w1_high(e):
                gated_wait(w1_in, 16 * e + 16)
                nc.gpsimd.tensor_copy(w1[0][:], stage1[:]).then_inc(w1_hi, 1)

            def w2_high(e):
                gated_wait(w2_in, 16 * e + 16)
                nc.gpsimd.tensor_copy(w2[0][:], stage2[:]).then_inc(w2_hi, 1)

            def body(e, more):
                if more:
                    gated_wait(xn_done, e + 1)
                    gated_wait(weight_done, e + 1)
                    gather(e + 1)
                for m in range(MC):
                    gated_wait(gelu_done, MC * e + m + 1)
                    nc.gpsimd.tensor_copy(h[0][:, m, :], h32[:, m % 2, :]).then_inc(hhi_done, 1)
                    if m == 3 and more:
                        token_rstd(e + 1)
                if more:
                    w1_high(e + 1)
                    x_hi(e + 1)
                    gated_wait(down_done, e + 1)
                    w2_high(e + 1)
                nc.gpsimd.tensor_copy(idx_out[:], g["idx"][:, bass.ds(e, 1), :].squeeze(1)).then_inc(idxo_done, 1)
                gated_wait(idxo_done, e + 1)
                gated_wait(y_done, e + 1)
                for s in range(SC):
                    pool.indirect_dma_start(out.rearrange("b n d -> (b n) d"),
                                            bass.IndirectOffsetOnAxis(ap=idx_out[:, s:s + 1], axis=0),
                                            y2[:, s, :], None, compute_op=ALU.add).then_inc(scattered, 16)
                gated_wait(scattered, 16 * SC * e + 16 * SC)
                pool.sem_inc(y2_free, 1)

            pool.sem_inc(y2_free, 1)
            gather(0)
            w1_high(0)
            token_rstd(0)
            x_hi(0)
            w2_high(0)
            with pool.Fori(0, E - 1) as e:
                body(e, True)
            body(E - 1, False)
            pool.wait_ge(scattered, 16 * SC * E)

        @block.scalar
        def _(act):
            b1 = COL_AT["L3_cond_b1s"]
            with act.Fori(0, E) as e:
                for m in range(MC):
                    act.wait_ge(up_done, MC * e + m + 1)
                    if m >= 2:
                        act.wait_ge(hlo_done, MC * e + m - 1)
                    nc.scalar.activation(h32[:, m % 2, :], up_ps[m % 2][:], ACT.Gelu_apprx_tanh,
                                         bias=g["cols"][:, bass.ds(b1 + MC * e + m, 1)]).then_inc(gelu_done, 1)

        @block.tensor
        def _(pe):
            mm = nc.tensor.matmul

            def three(out, lhs, rhs, start, stop):
                mm(out, lhs[0], rhs[0], start=start, stop=False)
                mm(out, lhs[1], rhs[0], start=False, stop=False)
                return mm(out, lhs[0], rhs[1], start=False, stop=stop)

            def transposes(e):
                pe.wait_ge(xn_done, e + 1)
                for k in range(KD):
                    for s in range(SC):
                        last = nc.tensor.transpose(tp_ps[k][:, s * P:(s + 1) * P], xn[:, s, k * P:(k + 1) * P],
                                                   g["ident"][:])
                last.then_inc(tp_done, 1)

            def body(e, more):
                pe.wait_ge(w1_lo, e + 1)
                pe.wait_ge(xlo_done, e + 1)
                for m in range(MC):
                    if m >= 2:
                        pe.wait_ge(gelu_done, MC * e + m - 1)
                    for k in range(KD):
                        last = three(up_ps[m % 2][:], [w[:, k, m * P:(m + 1) * P] for w in w1],
                                     [x[:, k, :] for x in xt], k == 0, k == KD - 1)
                    last.then_inc(up_done, 1)
                pe.wait_ge(down_free, e + 1)
                pe.wait_ge(w2_lo, e + 1)
                for m in range(MC):
                    pe.wait_ge(hlo_done, MC * e + m + 1)
                    for s in range(SC):
                        last = three(down_ps[s][:, 0:D], [x[:, m, s * P:(s + 1) * P] for x in h],
                                     [w[:, m, :] for w in w2], m == 0, m == MC - 1)
                    if m == 3 and more:
                        transposes(e + 1)
                last.then_inc(down_done, 1)

            transposes(0)
            with pe.Fori(0, E - 1) as e:
                body(e, True)
            body(E - 1, False)

        @block.vector
        def _(dve):
            V = nc.vector

            def normalise(e):
                dve.wait_ge(gathered, 16 * SC * e + 16 * SC)
                V.tensor_copy(weight_next[:], xg[:, :, bass.ds(D + e, 1)].squeeze(2)).then_inc(weight_done, 1)
                for s in range(SC):
                    V.bn_stats(stats[:, s, :], xg[:, s, 0:D]).then_inc(stats_done, 1)
                for s in range(SC):
                    dve.wait_ge(stats_done, SC * e + s + 1)
                    dve.sem_inc(passed_dve, 1)
                    V.bn_aggr(mv[:, s, :], stats[:, s, :]).then_inc(aggr_done, 1)
                dve.wait_ge(aggr_done, SC * e + SC)
                V.tensor_scalar(ve[:], mv[:, :, 1], 1e-5, None, ALU.add).then_inc(ve_done, 1)
                dve.wait_ge(rstd_done, e + 1)
                for s in range(SC):
                    ins = V.tensor_scalar(xn[:, s, :], xg[:, s, 0:D], mv[:, s, 0:1], rstd[:, s:s + 1],
                                          ALU.subtract, ALU.mult)
                ins.then_inc(xn_done, 1)

            def modulate(e):
                dve.wait_ge(tp_done, e + 1)
                gain, offset = COL_AT["L3_cond_mlp_g"], COL_AT["L3_cond_mlp_b"]
                for k in range(KD):
                    ins = V.tensor_scalar(xm[:, k, :], tp_ps[k][:], g["cols"][:, gain + k:gain + k + 1],
                                          g["cols"][:, offset + k:offset + k + 1], ALU.mult, ALU.add)
                ins.then_inc(xm_done, 1)
                dve.wait_ge(xhi_done, e + 1)
                V.tensor_tensor(xt[1][:], xm[:], xt[0][:].bitcast(F32), ALU.subtract).then_inc(xlo_done, 1)

            def low(e, hi_done, dst, src, done):
                dve.wait_ge(hi_done, e + 1)
                V.tensor_tensor(dst[1][:], src[:], dst[0][:].bitcast(F32), ALU.subtract).then_inc(done, 1)

            def weights_now(e):
                dve.wait_ge(weight_done, e + 1)
                V.tensor_copy(weight[:], weight_next[:]).then_inc(weight_now, 1)

            def body(e, more):
                for m in range(MC):
                    dve.wait_ge(hhi_done, MC * e + m + 1)
                    V.tensor_tensor(h[1][:, m, :], h32[:, m % 2, :], h[0][:, m, :].bitcast(F32), ALU.subtract)\
                        .then_inc(hlo_done, 1)
                    if m == 3 and more:
                        normalise(e + 1)
                if more:
                    low(e + 1, w1_hi, w1, stage1, w1_lo)
                    modulate(e + 1)
                dve.wait_ge(down_done, e + 1)
                dve.wait_ge(b2_in, 16 * e + 16)
                for s in range(SC):
                    ins = V.tensor_tensor(y[:, s, :], down_ps[s][:, 0:D], b2[:], ALU.add)
                ins.then_inc(down_free, 1)
                dve.wait_ge(down_free, e + 2)
                dve.wait_ge(weight_now, e + 1)
                dve.wait_ge(y2_free, e + 1)
                for s in range(SC):
                    ins = V.tensor_scalar(y2[:, s, :], y[:, s, :], weight[:, s:s + 1], None, ALU.mult)
                ins.then_inc(y_done, 1)
                if more:
                    dve.wait_ge(y_done, e + 1)
                    weights_now(e + 1)
                    low(e + 1, w2_hi, w2, stage2, w2_lo)

            dve.sem_inc(down_free, 1)
            normalise(0)
            low(0, w1_hi, w1, stage1, w1_lo)
            modulate(0)
            weights_now(0)
            low(0, w2_hi, w2, stage2, w2_lo)
            with dve.Fori(0, E - 1) as e:
                body(e, True)
            body(E - 1, False)


XT = TILES + T4


def program(nc, t, out, stop=None):
    with ExitStack() as ctx:
        sb = lambda n, s, d=F32: ctx.enter_context(nc.sbuf_tensor(n, s, d))
        sem = lambda n: ctx.enter_context(nc.semaphore(n))
        g = {"x": sb("x_sb", [P, XT, D]), "cols": sb("cols_sb", [P, NCOL]), "mod": sb("mod_sb", [P, NMOD, B + 2]),
             "ident": sb("ident_sb", [P, P]), "ones": sb("ones", [P, P]), "ones_r": sb("ones_r", [P, P], F32R),
             "hmask": sb("hmask_sb", [P, 10]), "neg_block": sb("neg_block_sb", [4, 512]),
             "block_ones": sb("block_ones_sb", [P, P]), "mhalf": sb("mhalf", [P, 8]),
             "idx": sb("idx_sb", [P, E, SC], U32)}
        x_in, set_up = sem("x_in"), sem("set_up")

        with nc.Block() as block:
            @block.sync
            def _(sp):
                sp.dma_start(g["x"][:, 0:TILES, :], t["x"].rearrange("b (t p) d -> p (b t) d", p=P)).then_inc(x_in, 16)
                for name in ("ident", "hmask", "neg_block", "block_ones"):
                    sp.dma_start(g[name][:], t[name]).then_inc(x_in, 16)
                sp.wait_ge(x_in, 16 * 5)

            @block.gpsimd
            def _(pool):
                nc.gpsimd.memset(g["x"][:, TILES:XT, :], 0.0).then_inc(set_up, 1)
                nc.gpsimd.memset(g["ones"][:], 1.0).then_inc(set_up, 1)
                nc.gpsimd.memset(g["ones_r"][:].bitcast(F32), 1.0).then_inc(set_up, 1)
                nc.gpsimd.memset(g["mhalf"][:], -0.5).then_inc(set_up, 1)
                pool.wait_ge(set_up, 4)

        conditioning(nc, t, g)
        phases = [("L0a", lambda: attention(nc, t, g, Attention("L0a", 16, 64, 64 ** -0.5, True, "layer", 1e-5))),
                  ("L0m", lambda: mlp(nc, t, g, "L0m", "layer", 1e-5)),
                  ("L1a", lambda: attention(nc, t, g, Attention("L1a", 1, 256, 256 ** -0.5, False, "rms", 1e-6))),
                  ("L1m", lambda: mlp(nc, t, g, "L1m", "rms", 1e-6)),
                  ("L2a", lambda: attention(nc, t, g, Attention("L2a", 16, 16, 16 ** -0.5, True, None, 1e-5))),
                  ("L2m", lambda: mlp(nc, t, g, "L2m", None, 1e-5)),
                  ("L3a", lambda: attention(nc, t, g, Attention("L3a", 16, 64, 64 ** -0.5, False, "layer", 1e-5)))]
        for name, phase in phases:
            phase()
            if stop == name:
                with nc.Block() as block:
                    @block.sync
                    def _(sp):
                        sp.dma_start(out.rearrange("b (t p) d -> p (b t) d", p=P), g["x"][:, 0:TILES, :]).then_inc(x_in, 16)
                        sp.wait_ge(x_in, 16 * 6)
                return
        route(nc, t, g, out)
        experts(nc, t, g, out)


def _laid_out(np, inputs):
    f = lambda a: np.ascontiguousarray(a)
    i = {k: np.asarray(v) for k, v in inputs.items()}
    h = {"x": i["x"], "c_t": f(i["cond_1024"].T), "mask": f(i["mask_BxS_bk0"]).view(np.int32),
         "mask_t": f(i["mask_BxS_bk0"].T).view(np.int32)}
    for n in ("q", "k"):
        for p in ("g", "b"):
            i[f"{n}n_{p}2"] = np.concatenate([i[f"L3_cond_{n}n_{p}"]] * 2)
    h["cols"] = f(np.concatenate([i[n].reshape(k, P).T for n, k in COL_VECS], axis=1))
    h["rows"] = f(np.concatenate([i[n].reshape(-1) for n, _ in ROW_VECS]))
    for n in ("L0_cond_W_mod", "L1_cond_film1_w", "L1_cond_film2_w", "L2_cond_ada1_w", "L2_cond_ada2_w",
              "L1_cond_proj_b", "L1_cond_mlp_b2", "L2_cond_proj_b", "L2_cond_fc2_b"):
        h[n] = i[n]
    h["W_ada_t"] = f(i["L3_cond_W_ada"].T)
    w = i["L0_cond_W_qkv"]
    h["L0a_wq"], h["L0a_wk"], h["L0a_wv"], h["L0a_wo"] = f(w[:, 0:1024]), f(w[:, 1024:2048]), f(w[:, 2048:3072]), i["L0_cond_W_out"]
    h["L1a_wq"], h["L1a_wk"], h["L1a_wv"], h["L1a_wo"] = (i[f"L1_cond_{n}_w"] for n in ("q", "k", "v", "proj"))
    w = i["L2_cond_qkv_w"]
    h["L2a_wq"], h["L2a_wk"] = f(w[:, 0:256]), f(w[:, 256:512])
    wv = np.zeros((256, 16, 32), np.float32)
    wv[:, :, 0:16] = w[:, 512:768].reshape(256, 16, 16)
    h["L2a_wv"] = wv.reshape(256, 512)
    wo = np.zeros((16, 32, 256), np.float32)
    wo[:, 0:16, :] = i["L2_cond_proj_w"].reshape(16, 16, 256)
    h["L2a_wo"] = wo.reshape(512, 256)
    w = f(i["L3_cond_Wqkv"].T)
    h["L3a_wq"], h["L3a_wk"], h["L3a_wv"] = f(w[:, 0:1024]), f(w[:, 1024:2048]), f(w[:, 2048:3072])
    h["L3a_wo"] = f(i["L3_cond_Wout"].T)
    h["L0m_w1"], h["L0m_w2"] = i["L0_cond_W1"], i["L0_cond_W2"]
    h["L1m_w1"], h["L1m_w2"] = i["L1_cond_mlp_w1"], i["L1_cond_mlp_w2"]
    h["L2m_w1"], h["L2m_w2"] = i["L2_cond_fc1_w"], i["L2_cond_fc2_w"]
    h["wg_t"] = f(i["L3_cond_Wgate"].T)
    h["moe_w1"], h["moe_w2"] = f(i["L3_cond_fc1s"].transpose(0, 2, 1)), f(i["L3_cond_fc2s"].transpose(0, 2, 1))
    h["L3_cond_b2s"] = i["L3_cond_b2s"]
    h["tri"] = np.triu(np.ones((P, P), np.float32), 1)
    h["iota"] = np.tile(np.arange(P, dtype=np.float32), (P, 1))
    h["tval"] = np.tile(np.arange(TILES, dtype=np.float32), (P, 1))
    h["pval"] = np.arange(P, dtype=np.float32)[:, None].copy()
    h["ident"] = np.eye(P, dtype=np.float32)
    hm = np.zeros((P, 10), np.float32)
    hm[0:64, 0] = hm[64:128, 1] = 1.0
    for m in range(8):
        hm[16 * m:16 * m + 16, 2 + m] = 1.0
    h["hmask"] = hm
    h["neg_block"] = np.repeat(-np.eye(4, dtype=np.float32), P, axis=1)
    h["block_ones"] = np.kron(np.eye(2, dtype=np.float32), np.ones((64, 64), np.float32))
    return h


def kernel(**inputs):
    import concourse.bacc as bacc
    from concourse.bass_utils import run_bass_kernel_spmd

    nc = bacc.Bacc("TRN2", target_bir_lowering=False, num_devices=1)
    arrays = _laid_out(np, inputs)
    t = {n: nc.dram_tensor(f"in_{n}", v.shape, mybir.dt.from_np(v.dtype), kind="ExternalInput").ap()
         for n, v in arrays.items()}
    t["gate_rows"] = nc.dram_tensor("gate_rows", (NGATE, B, D), F32, kind="Internal").ap()
    t["token_rows"] = nc.dram_tensor("token_rows", (B * N, ROW), F32, kind="Internal").ap()
    out = nc.dram_tensor("out_x", (B, N, D), F32, kind="ExternalOutput").ap()
    program(nc, t, out)
    r = run_bass_kernel_spmd(nc, [{f"in_{n}": v for n, v in arrays.items()}], core_ids=[0])
    return r.results[0]["out_x"]
```

```python
from contextlib import ExitStack, contextmanager

import numpy as np
import concourse.bass as bass
from concourse import mybir

F32 = mybir.dt.float32
F32R = mybir.dt.float32r
U8 = mybir.dt.uint8
U32 = mybir.dt.uint32
I32 = mybir.dt.int32
ALU = mybir.AluOpType
ACT = mybir.ActivationFunctionType
AX = mybir.AxisListType

P = 128
B, N, D = 16, 256, 256
TT = N // P
KD = D // P
TILES = B * TT
MLP = 1024
MC = MLP // P
E = 8
CAP = B * N // E
SC = CAP // P

COL_VECS = [("L0_cond_b_mod", 12), ("L0_cond_b1", 8),
            ("L1_cond_norm1_w", 2), ("L1_cond_film1_b", 4), ("L1_cond_q_b", 2), ("L1_cond_k_b", 2),
            ("L1_cond_v_b", 2), ("L1_cond_norm2_w", 2), ("L1_cond_film2_b", 4), ("L1_cond_mlp_b1", 8),
            ("L2_cond_fc1_b", 8), ("L2_cond_ada1_b", 2),
            ("L3_cond_b_ada", 2), ("L3_cond_ln1_g", 2), ("L3_cond_ln1_b", 2),
            ("qn_g2", 1), ("qn_b2", 1), ("kn_g2", 1), ("kn_b2", 1),
            ("L3_cond_mlp_g", 2), ("L3_cond_mlp_b", 2), ("L3_cond_b1s", 64)]
COL_AT = {}
for _name, _n in COL_VECS:
    COL_AT[_name] = sum(n for _, n in COL_VECS[:len(COL_AT)])
NCOL = sum(n for _, n in COL_VECS)
ROW_VECS = [("L0_cond_b_mod", 1536), ("L0_cond_b_out", 256), ("L0_cond_b2", 256), ("L2_cond_ada2_b", 1536)]
ROW_AT = {"L0_cond_b_mod": 0, "L0_cond_b_out": 1536, "L0_cond_b2": 1792, "L2_cond_ada2_b": 2048}
NROW = 3584

MOD_AT = {"L0a": 0, "L0m": 4, "L1a": 8, "L1m": 12, "L3a": 16}
NMOD = 20
GATE_AT = {"L0a": 0, "L0m": 2, "L2a": 4, "L2m": 6}
NGATE = 8


@contextmanager
def semaphores(nc, prefix):
    with ExitStack() as ctx:
        made = []

        def sem(name):
            made.append(ctx.enter_context(nc.semaphore(f"{prefix}_{name}")))
            return made[-1]

        yield sem
        with nc.Block() as block:
            @block.gpsimd
            def _(pool):
                for s in made:
                    pool.sem_clear(s)


def conditioning(nc, t, g):
    with semaphores(nc, "c") as sem, ExitStack() as ctx:
        sb = lambda n, s, d=F32: ctx.enter_context(nc.sbuf_tensor(n, s, d))
        ps = [ctx.enter_context(nc.psum_tensor(f"c_ps{i}", [P, 512], F32)) for i in range(4)]
        c_t = sb("c_t", [P, KD, B])
        silu_c = sb("c_silu", [P, KD, B])
        h1 = sb("c_h1", [P, KD, B])
        w_mod = sb("c_wmod", [P, KD, 1536])
        film = [sb(f"c_film{j}", [P, KD, 512]) for j in range(2)]
        ada1 = sb("c_ada1", [P, KD, 256])
        ada2 = sb("c_ada2", [P, KD, 1536])
        w_ada = sb("c_wada", [P, KD, 256])
        rows_b = sb("c_rows", [B, NROW])
        raw = sb("c_raw", [B, 2048])
        gates = sb("c_gates", [B, NGATE, D])
        colraw = sb("c_colraw", [P, 18, B])
        loaded, silu_done, mm_done, h1_done, v, stored, memz = (sem(f"s{i}") for i in range(7))
        chained = sem("chained")
        block = ctx.enter_context(nc.Block())
        chunked = lambda w: w.rearrange("(k p) n -> p k n", p=P)

        @block.sync
        def _(sp):
            sp.dma_start(c_t[:], chunked(t["c_t"])).then_inc(loaded, 16)
            sp.dma_start(g["cols"][:], t["cols"]).then_inc(loaded, 16)
            sp.dma_start(rows_b[:], t["rows"].partition_broadcast(B)).then_inc(loaded, 16)
            for dst, name in ((w_mod, "L0_cond_W_mod"), (film[0], "L1_cond_film1_w"),
                              (film[1], "L1_cond_film2_w"), (ada1, "L2_cond_ada1_w"),
                              (ada2, "L2_cond_ada2_w"), (w_ada, "W_ada_t")):
                sp.dma_start(dst[:], chunked(t[name])).then_inc(loaded, 16)
            sp.wait_ge(v, 1)
            sp.dma_start(t["gate_rows"].rearrange("g b d -> b g d"), gates[:]).then_inc(stored, 16)
            sp.wait_ge(stored, 16)

        @block.scalar
        def _(act):
            act.wait_ge(loaded, 16 * 9)
            nc.scalar.activation(silu_c[:], c_t[:], ACT.Silu).then_inc(silu_done, 1)
            act.wait_ge(mm_done, 2)
            for k in range(KD):
                nc.scalar.activation(h1[:, k, :], ps[2][:, k * B:(k + 1) * B], ACT.Silu,
                                     bias=g["cols"][:, COL_AT["L2_cond_ada1_b"] + k:COL_AT["L2_cond_ada1_b"] + k + 1]).then_inc(h1_done, 1)

        @block.tensor
        def _(pe):
            def columns(bank, j, w, col, x):
                for k in range(KD):
                    last = nc.tensor.matmul(bank[:, j * B:(j + 1) * B], w[:, k, col * P:(col + 1) * P],
                                            x[:, k, :], start=(k == 0), stop=(k == KD - 1))
                return last

            def row(bank, w, c0, n, x):
                for k in range(KD):
                    last = nc.tensor.matmul(bank[0:B, 0:n], x[:, k, :], w[:, k, c0:c0 + n],
                                            start=(k == 0), stop=(k == KD - 1))
                return last

            pe.wait_ge(silu_done, 1)
            for j, col in enumerate((0, 1, 2, 3, 6, 7, 8, 9)):
                columns(ps[0], j, w_mod, col, silu_c)
            for j in range(4):
                columns(ps[0], 8 + j, film[0], j, c_t)
            for j in range(4):
                columns(ps[0], 12 + j, film[1], j, c_t)
            for j in range(2):
                columns(ps[0], 16 + j, w_ada, j, silu_c)
            row(ps[1], w_mod, 512, 256, silu_c)
            for k in range(KD):
                last = nc.tensor.matmul(ps[1][0:B, 256:512], silu_c[:, k, :], w_mod[:, k, 1280:1536],
                                        start=(k == 0), stop=(k == KD - 1))
            last.then_inc(mm_done, 1)
            for j in range(2):
                last = columns(ps[2], j, ada1, j, c_t)
            last.then_inc(mm_done, 1)
            pe.wait_ge(h1_done, 2)
            pe.wait_ge(memz, 1)
            for n, bank in enumerate((ps[1], ps[2], ps[3])):
                last = row(bank, ada2, 512 * n, 512, h1)
            last.then_inc(mm_done, 1)

        @block.vector
        def _(dve):
            mod, cols = g["mod"], g["cols"]
            done = [0]
            chain = chained

            def step(ins):
                done[0] += 1
                ins.then_inc(chain, 1)
                dve.wait_ge(chain, done[0])

            dve.wait_ge(loaded, 16 * 9)
            step(nc.vector.memset(mod[:], 0.0))
            dve.wait_ge(mm_done, 1)
            step(nc.vector.tensor_copy(colraw[:], ps[0][:, 0:18 * B].rearrange("p (j b) -> p j b", b=B)))
            nc.vector.tensor_copy(raw[:, 0:512], ps[1][0:B, :]).then_inc(memz, 1)
            dve.wait_ge(memz, 1)

            def biased(j, bias, plus=0.0):
                step(nc.vector.tensor_scalar(colraw[:, j, :], colraw[:, j, :], cols[:, bias:bias + 1], plus,
                                             ALU.add, ALU.add))

            bm = COL_AT["L0_cond_b_mod"]
            for j, col in enumerate((0, 1, 2, 3, 6, 7, 8, 9)):
                biased(j, bm + col, 1.0 if j in (2, 3, 6, 7) else 0.0)
            for part, base in ((0, 8), (1, 12)):
                fb = COL_AT[f"L1_cond_film{part + 1}_b"]
                for j in range(4):
                    biased(base + j, fb + j, 1.0 if j < 2 else 0.0)
            for j in range(2):
                biased(16 + j, COL_AT["L3_cond_b_ada"] + j)
            for k in range(KD):
                for name, shift, scale in (("L0a", 0, 2), ("L0m", 4, 6), ("L1a", 10, 8), ("L1m", 14, 12)):
                    at = MOD_AT[name]
                    if name[1] == "0":
                        step(nc.vector.tensor_copy(mod[:, at + k, 0:B], colraw[:, scale + k, :]))
                    else:
                        nw = COL_AT["L1_cond_norm1_w" if name == "L1a" else "L1_cond_norm2_w"] + k
                        step(nc.vector.tensor_scalar(mod[:, at + k, 0:B], colraw[:, scale + k, :],
                                                     cols[:, nw:nw + 1], None, ALU.mult))
                    step(nc.vector.tensor_copy(mod[:, at + 2 + k, 0:B], colraw[:, shift + k, :]))
                at = MOD_AT["L3a"]
                gcol, bcol = COL_AT["L3_cond_ln1_g"] + k, COL_AT["L3_cond_ln1_b"] + k
                step(nc.vector.tensor_scalar(mod[:, at + k, 0:B], mod[:, at + k, 0:B],
                                             cols[:, gcol:gcol + 1], None, ALU.add))
                step(nc.vector.tensor_scalar(mod[:, at + 2 + k, 0:B], colraw[:, 16 + k, :],
                                             cols[:, bcol:bcol + 1], None, ALU.add))
            for half, name, bias in ((0, "L0a", "L0_cond_b_out"), (1, "L0m", "L0_cond_b2")):
                r = 512 if half == 0 else 1280
                at = GATE_AT[name]
                step(nc.vector.tensor_tensor(gates[:, at, :], raw[:, 256 * half:256 * half + 256],
                                             rows_b[:, r:r + 256], ALU.add))
                step(nc.vector.tensor_tensor(gates[:, at + 1, :], gates[:, at, :],
                                             rows_b[:, ROW_AT[bias]:ROW_AT[bias] + 256], ALU.mult))
            dve.wait_ge(mm_done, 3)
            ab = ROW_AT["L2_cond_ada2_b"]
            for n in range(3):
                step(nc.vector.tensor_tensor(raw[:, 512 + 512 * n:1024 + 512 * n], ps[n + 1][0:B, :],
                                             rows_b[:, ab + 512 * n:ab + 512 * n + 512], ALU.add))
            for half, name in ((0, "L2a"), (1, "L2m")):
                o = 512 + 768 * half
                at = GATE_AT[name]
                step(nc.vector.scalar_tensor_tensor(gates[:, at, :], raw[:, o + 256:o + 512], 1.0,
                                                    raw[:, o + 512:o + 768], ALU.add, ALU.mult))
                step(nc.vector.tensor_tensor(gates[:, at + 1, :], raw[:, o:o + 256],
                                             raw[:, o + 512:o + 768], ALU.mult))
            nc.vector.engine_nop().then_inc(v, 1)


def split_weights(nc, engines, stage, sems, pieces, centre=None):
    sp, pool, dve = engines
    landed, hi_done, lo_done = sems

    def sync_share():
        for n, (src, hi, lo, c) in enumerate(pieces):
            if n >= 2:
                sp.wait_ge(lo_done, n - 1)
            w = hi.shape[-1]
            sp.dma_start(stage[:, n % 2, 0:w], src).then_inc(landed[n % 2], 16)

    def pool_share():
        for n, (src, hi, lo, c) in enumerate(pieces):
            w = hi.shape[-1]
            if c:
                pool.wait_ge(centre[1], 2 * sum(x[3] for x in pieces[:n]) + 2)
            pool.wait_ge(landed[n % 2], 16 * (n // 2 + 1))
            nc.gpsimd.tensor_copy(hi, stage[:, n % 2, 0:w]).then_inc(hi_done, 1)

    def vector_share():
        seen = 0
        for n, (src, hi, lo, c) in enumerate(pieces):
            w = hi.shape[-1]
            if c:
                means, steps = centre
                dve.wait_ge(landed[n % 2], 16 * (n // 2 + 1))
                heads = stage[:, n % 2, 0:w].rearrange("p (h d) -> p h d", d=64)
                if seen:
                    dve.wait_ge(steps, 2 * seen)
                nc.vector.tensor_reduce(means[:], heads, AX.X, ALU.add).then_inc(steps, 1)
                dve.wait_ge(steps, 2 * seen + 1)
                mb = means[:].unsqueeze(2).to_broadcast([P, w // 64, 64])
                nc.vector.scalar_tensor_tensor(heads, mb, -1.0 / 64, heads, ALU.mult, ALU.add).then_inc(steps, 1)
                seen += 1
            dve.wait_ge(hi_done, n + 1)
            if lo is None:
                dve.sem_inc(lo_done, 1)
                continue
            nc.vector.tensor_tensor(lo, stage[:, n % 2, 0:w], hi.bitcast(F32), ALU.subtract).then_inc(lo_done, 1)

    return sync_share, pool_share, vector_share


class Attention:

    def __init__(self, name, heads, d, scale, gated, norm, eps):
        self.name, self.heads, self.d, self.scale = name, heads, d, scale
        self.gated, self.norm, self.eps = gated, norm, eps
        self.chunks = heads * d // P
        self.one = heads == 1
        self.units = 1 if self.one else heads // 2
        self.vd = max(d, 32) if not self.one else d
        self.vw = heads * self.vd
        self.oc = heads * self.vd // P
        self.vpiece = min(512, self.vw)
        self.vpieces = TT * self.vw // self.vpiece
        self.upc = 2 if self.vd == 32 else 1
        self.groups = self.units // self.upc
        self.hn = 2 if not self.one else 1
        self.per_chunk = P // d if d < P else 1
        self.pieces = self.oc // 2
        self.qknorm = name == "L3a"
        overs = [("over", n) for n in range(self.pieces)]
        turns = []
        for c in range(self.chunks):
            turns.append(("qk", c))
            if c >= 3 and overs:
                turns.append(overs.pop(0))
        turns += [("v", n) for n in range(self.vpieces)] + overs + [("out", 0)]
        if self.qknorm:
            turns.append(("norm", 0))
        self.ln_step = min(3, self.units)
        for step in range(self.units + 1):
            if step >= 1:
                turns.append(("max", step - 1))
            if self.qknorm and step + 1 < self.units:
                turns.append(("norm", step + 1))
            if step == self.ln_step:
                turns.append(("ln", 0))
        if len(turns) % 2:
            turns.append(("spare", 0))
        self.turns = turns


def o_row(a, u, h):
    return 64 * h if a.d == 64 else 64 * (u % 2) + 32 * h


def o_rows(a, u):
    return slice(64 * (u % 2), 64 * (u % 2) + 64) if a.vd == 32 else slice(0, P)


def residual(nc, dve, s, nm, i, tiles, outs, gate_of, eps, bufs, g, per, gate_ready):
    y, y2, stats, mv, ve, rstd, y_bias = bufs
    n = len(tiles)
    step = [0]

    def chained(ins, last):
        step[0] += 1
        ins.then_inc(s["step"], 1)
        if last:
            dve.wait_ge(s["step"], per * i + step[0])

    tile = lambda j: g["x"][:, bass.ds(tiles[0] + j, 1), :].squeeze(1)
    if gate_ready is not None:
        dve.wait_ge(*gate_ready)
    src = outs
    if nm[:2] == "L2":
        for j in range(n):
            chained(nc.vector.tensor_tensor(y[:, j, :], outs[j], y_bias[:], ALU.add), j == n - 1)
        for j in range(n):
            chained(nc.vector.bn_stats(stats[:, j, :], y[:, j, :]), j == n - 1)
        dve.sem_inc(s["passed"], 1)
        for j in range(n):
            chained(nc.vector.bn_aggr(mv[:, j, :], stats[:, j, :]), j == n - 1)
        nc.vector.tensor_scalar(ve[:, 0:n], mv[:, 0:n, 1], eps, None, ALU.add).then_inc(s["ve2"], 1)
        dve.wait_ge(s["rstd2"], i + 1)
        for j in range(n):
            chained(nc.vector.tensor_scalar(y2[:, j, :], y[:, j, :], mv[:, j, 0:1], rstd[:, j:j + 1],
                                            ALU.subtract, ALU.mult), j == n - 1)
        src = [y2[:, j, :] for j in range(n)]
    if nm[:2] in ("L0", "L2"):
        for j in range(n):
            chained(nc.vector.tensor_tensor(y[:, j, :], src[j], gate_of(j), ALU.mult), j == n - 1)
        src = [y[:, j, :] for j in range(n)]
    if nm[:2] != "L3":
        dve.wait_ge(s["xh"], n * (i + 1))
    for j in range(n):
        ins = nc.vector.tensor_tensor(tile(j), src[j], tile(j), ALU.add)
        if j == n - 1:
            ins.then_inc(s["done"], 1)
        else:
            ins.then_inc(s["step"], 1)
            step[0] += 1
    assert step[0] == per, (nm, step[0], per)


def residual_steps(nm, n):
    return {"L0": 2 * n - 1, "L1": n - 1, "L2": 6 * n - 1, "L3": n - 1}[nm[:2]]


def attention(nc, t, g, a):
    qknorm, masked = a.qknorm, a.name == "L2a"
    nm, C, U, HN, OC = a.name, a.chunks, a.units, a.hn, a.oc
    NR = len(a.turns)
    AT = {turn: n for n, turn in enumerate(a.turns)}
    bank_of = lambda *turn: ring[AT[turn] % 2]
    NB = 3
    KR = 4 if qknorm else C
    LN_STEP = a.ln_step
    MASK0 = 0 if a.d == 64 else 2
    cols = g["cols"]
    with semaphores(nc, nm) as sem, ExitStack() as ctx:
        sb = lambda n, s, d=F32: ctx.enter_context(nc.sbuf_tensor(f"{nm}_{n}", s, d))
        pb = lambda n: ctx.enter_context(nc.psum_tensor(f"{nm}_{n}", [P, 512], F32))
        ring = [pb("ring0"), pb("ring1")]
        s_ps = [pb("s0"), pb("s1")]
        st_ps = [pb("st0"), pb("st1")]
        o_ps, sum_ps = pb("o"), pb("sum")

        QW = a.heads * a.d
        wq = [sb(f"wq{j}", [P, KD, QW], F32R) for j in range(2)]
        wk = [sb(f"wk{j}", [P, KD, QW], F32R) for j in range(2)]
        wv = [sb(f"wv{j}", [P, KD, a.vw], F32R) for j in range(2)]
        wo = [sb(f"wo{j}", [P, OC, D], F32R) for j in range(2)]
        means = sb("means", [P, 16])
        xt = [sb(f"xt{j}", [P, KD, N], F32R) for j in range(2)]
        stats = sb("stats", [P, TT, 6])
        mv = sb("mv", [P, TT, 2])
        ve = sb("ve", [P, TT])
        rstd = sb("rstd", [P, TT])
        q32 = None if qknorm else sb("q32", [P, C, N])
        k_hi = sb("k_hi", [P, KR, N], F32R)
        k_lo = sb("k_lo", [P, KR, N], F32R)
        v = sb("v", [P, TT, a.vw])
        q_hi = sb("q_hi", [P, NB, 512], F32R)
        q_lo = sb("q_lo", [P, NB, 512], F32R)
        mx = sb("mx", [P, 4])
        shift = sb("shift", [P, 2, 512], F32R)
        prob = sb("prob", [P, 2, TT, 512])
        stage = prob[:].rearrange("p s t n -> p s (t n)")
        rsum = sb("rsum", [a.heads, N])
        rsum_hi, rsum_lo = sb("rsum_hi", [P, N], F32R), sb("rsum_lo", [P, N], F32R)
        spread = sb("spread", [P, OC * P], F32R)
        o_raw = sb("o_raw", [P, OC, N])
        o32 = sb("o32", [P, 2, 2 * N])
        y, y2 = (o32[:, j, :].rearrange("p (t d) -> p t d", d=D) for j in range(2))
        xm, xn = o32[:, 0, :].rearrange("p (k n) -> p k n", n=N), y2
        o_hi = sb("o_hi", [P, OC, N], F32R)
        o_lo = sb("o_lo", [P, OC, N], F32R)
        gate = y_bias = None
        if not qknorm:
            gate = sb("gate", [P, 2, D])
        if masked:
            y_bias = sb("y_bias", [P, D])
        if qknorm:
            raw = sb("raw", [P, C, 512])
            sq = sb("sq", [P, 512])
            rq_hi, rq_lo = sb("rq_hi", [P, 512], F32R), sb("rq_lo", [P, 512], F32R)
            qn = sb("qn", [P, 512])
            lnv, rstdq = qn[0:a.heads, :], sq[0:a.heads, :]
            eps_col = sb("eps_col", [P, 1])
        rstd2, ve2 = sb("rstd2", [P, TT]), sb("ve2", [P, TT])
        if masked:
            mask_u8 = sb("mask_u8", [P, TT, B], U8)
            kbias = sb("kbias", [P, TT])
            key_bias = sb("key_bias", [P, TT, B])
            mrow_u8 = sb("mrow_u8", [P, 2, B, N], U8)
            mrow = sb("mrow", [P, 512], F32R)

        landed = [sem("landed0"), sem("landed1")]
        hi_done, lo_done, centred = sem("hi_done"), sem("lo_done"), sem("centred")
        pre, consts = sem("pre"), sem("consts")
        stats_done, aggr_done, ve_done, rstd_done, xn_done = (sem(x) for x in ("stats", "aggr", "ve", "rstd", "xn"))
        xm_done, xhi_done, xlo_done = sem("xm"), sem("xhi"), sem("xlo")
        pe_first = sem("pe_first")
        turn_done, turn_free = sem("turn_done"), sem("turn_free")
        q32_done, khi_done = sem("q32"), sem("khi")
        qhi_done, qlo_done = sem("qhi"), sem("qlo")
        s_done, mx_done, shift_done = sem("s_done"), sem("mx"), sem("shift")
        st_done, p_done, pv_done = sem("st"), sem("p"), sem("pv")
        rsum_done, rsum_hi_done, rsum_lo_done = sem("rsum"), sem("rsum_hi"), sem("rsum_lo")
        o_done, on_done, ohi_done, olo_done = sem("o_raw"), sem("on"), sem("ohi"), sem("olo")
        klo_done = sem("klo")
        gate_in, ep_done, xh_done, ep_step = sem("gate_in"), sem("ep"), sem("xh"), sem("ep_step")
        passed = sem("passed")
        raw_done, sq_done, var_done, ln_done, rq_done = (sem(x) for x in ("raw", "sq", "var", "lnv", "rq"))
        rqhi_done, rqlo_done, qn_done, kn_done = (sem(x) for x in ("rqhi", "rqlo", "qn", "kn"))
        ve2_done, rstd2_done, passed_dve = sem("ve2"), sem("rstd2"), sem("passed_dve")
        mask_in, mrow_done, kb_done = sem("mask_in"), sem("mrow"), sem("kb")

        q_of = lambda c: raw[:, c, 0:N] if qknorm else q32[:, c, :]

        pieces = []
        part = lambda w, k, c0, c1: w[k * P:(k + 1) * P, c0:c1]
        for w_dram, dst, width in ((t[nm + "_wq"], wq, QW), (t[nm + "_wk"], wk, QW), (t[nm + "_wv"], wv, a.vw)):
            for k in range(KD):
                centred_piece = qknorm and dst is not wv
                pieces.append((w_dram[k * P:(k + 1) * P, :], dst[0][:, k, :], dst[1][:, k, :], centred_piece))
        for c in range(OC):
            pieces.append((t[nm + "_wo"][c * P:(c + 1) * P, :], wo[0][:, c, :], wo[1][:, c, :], False))
        pieces.append((t["spread_" + nm], spread[:], None, False))
        NP_ = len(pieces)

        block = ctx.enter_context(nc.Block())
        loader = lambda sp=None, pool=None, dve=None: split_weights(
            nc, (sp, pool, dve), stage, (landed, hi_done, lo_done), pieces, (means, centred))

        @block.sync
        def _(sp):
            if masked:
                sp.dma_start(mask_u8[:], t["mask_t"].bitcast(U8).rearrange("(k p) b -> p k b", p=P)).then_inc(mask_in, 16)
                for h in range(2):
                    sp.dma_start(mrow_u8[0:1, h, :, :], t["mask"].bitcast(U8).partition_broadcast(1)).then_inc(mask_in, 16)
            if a.gated:
                at = GATE_AT[nm]
                for j in range(2):
                    sp.dma_start(gate[:, j, :], t["gate_rows"][at + j, 0, :].partition_broadcast(P)).then_inc(gate_in, 16)
            elif nm == "L1a":
                sp.dma_start(gate[:, 0, :], t["L1_cond_proj_b"].partition_broadcast(P)).then_inc(gate_in, 16)
            if nm == "L2a":
                sp.dma_start(y_bias[:], t["L2_cond_proj_b"].partition_broadcast(P)).then_inc(gate_in, 16)
            loader(sp=sp)[0]()
            if a.gated:
                extra = 16 if nm == "L2a" else 0
                with sp.Fori(0, B - 1) as i:
                    sp.wait_ge(ep_done, i + 1)
                    for j in range(2):
                        sp.dma_start(gate[:, j, :], t["gate_rows"][at + j, bass.ds(i + 1, 1), :].squeeze(0).partition_broadcast(P)).then_inc(gate_in, 16)

        @block.gpsimd
        def _(pool):
            def gated_wait(s, val):
                pool.wait_ge(s, val)
                pool.sem_inc(passed, 1)

            for slot in range(2):
                nc.gpsimd.memset(shift[:, slot, :].bitcast(F32), 0.0).then_inc(pre, 1)
            for rows in [rsum_hi, rsum_lo] + ([rq_hi, rq_lo] if qknorm else []) + ([mrow] if masked else []):
                nc.gpsimd.memset(rows[:].bitcast(F32), 0.0).then_inc(pre, 1)
            loader(pool=pool)[1]()

            def token_rstd(i):
                gated_wait(ve_done, i + 1)
                nc.gpsimd.tensor_tensor(rstd[:], ve[:], g["mhalf"][:, 0:TT], ALU.pow).then_inc(rstd_done, 1)

            def x_hi(i):
                gated_wait(xm_done, i + 1)
                nc.gpsimd.tensor_copy(xt[0][:], xm[:]).then_inc(xhi_done, 1)

            if a.norm:
                token_rstd(0)
            x_hi(0)

            def tail(j):
                if a.gated or nm == "L1a":
                    gated_wait(gate_in, (32 * j + 32 + (16 if nm == "L2a" else 0)) if a.gated else 16)
                    for tt in range(TT):
                        hrow = gate[:, 1 if a.gated else 0, :]
                        tile = g["x"][:, bass.ds(j * TT + tt, 1), :].squeeze(1)
                        nc.gpsimd.tensor_tensor(tile, tile, hrow, ALU.add).then_inc(xh_done, 1)
                if nm == "L2a":
                    gated_wait(ve2_done, j + 1)
                    nc.gpsimd.tensor_tensor(rstd2[:], ve2[:], g["mhalf"][:, 0:TT], ALU.pow).then_inc(rstd2_done, 1)

            def next_tokens(i):
                if a.norm:
                    token_rstd(i + 1)
                x_hi(i + 1)

            next_tokens(0)
            with pool.Fori(1, B - 1) as i:
                tail(i - 1)
                next_tokens(i)
            tail(B - 2)
            tail(B - 1)

        @block.scalar
        def _(act):
            if masked:
                act.wait_ge(kb_done, 1)
            def tail_rows(j):
                act.wait_ge(rsum_done, j + 1)
                nc.scalar.activation(rsum_hi[0:a.heads, :], rsum[:], ACT.Copy).then_inc(rsum_hi_done, 1)

            def over(j, n):
                act.wait_ge(on_done, j * a.pieces + n + 1)
                if a.one:
                    for c in range(2):
                        vb = COL_AT["L1_cond_v_b"] + c
                        ins = nc.scalar.activation(o_hi[:, c, :], o32[:, 0, c * N:(c + 1) * N], ACT.Identity, bias=cols[:, vb:vb + 1])
                else:
                    ins = nc.scalar.activation(o_hi[:, 2 * n:2 * n + 2, :].rearrange("p c n -> p (c n)"), o32[:, n % 2, :], ACT.Copy)
                ins.then_inc(ohi_done, 1)

            def body(i, first):
                if not first:
                    tail_rows(i - 1)
                for kind, c in a.turns:
                    if kind == "over" and not first:
                        over(i - 1, c)
                    if kind != "qk":
                        continue
                    bank = bank_of("qk", c)
                    act.wait_ge(turn_done, i * NR + AT["qk", c] + 1)
                    if qknorm:
                        nc.scalar.activation(raw[:, c, :], bank[:], ACT.Copy).then_inc(raw_done, 1)
                        if c >= 1:
                            act.wait_ge(var_done, i * C + c)
                        nc.scalar.activation(sq[:], bank[:], ACT.Square).then_inc(sq_done, 1)
                    elif nm == "L1a":
                        qb, kb = COL_AT["L1_cond_q_b"] + c, COL_AT["L1_cond_k_b"] + c
                        nc.scalar.activation(q32[:, c, :], bank[:, 0:N], ACT.Identity, bias=cols[:, qb:qb + 1]).then_inc(q32_done, 1)
                        nc.scalar.activation(k_hi[:, c, :], bank[:, N:2 * N], ACT.Identity, bias=cols[:, kb:kb + 1]).then_inc(khi_done, 1)
                    else:
                        nc.scalar.activation(q32[:, c, :], bank[:, 0:N], ACT.Copy).then_inc(q32_done, 1)
                        nc.scalar.activation(k_hi[:, c, :], bank[:, N:2 * N], ACT.Copy).then_inc(khi_done, 1)
                if qknorm:
                    act.wait_ge(var_done, i * C + C)
                    nc.scalar.activation(lnv[:], s_ps[0][0:a.heads, :], ACT.Ln, bias=eps_col[0:a.heads, 0:1], scale=1.0 / a.d).then_inc(ln_done, 1)
                    act.wait_ge(ln_done, i + 1)
                    nc.scalar.activation(rstdq[:], lnv[:], ACT.Exp, scale=-0.5).then_inc(rq_done, 1)
                    act.wait_ge(rq_done, i + 1)
                    nc.scalar.activation(rq_hi[0:a.heads, :], rstdq[:], ACT.Copy).then_inc(rqhi_done, 1)

                def k_high(c):
                    act.wait_ge(kn_done, i * C + c + 1)
                    nc.scalar.activation(k_hi[:, c % KR, :], raw[:, c, N:2 * N], ACT.Copy).then_inc(khi_done, 1)

                def mask_q(u):
                    if a.one:
                        act.wait_ge(q32_done, i * C + C)
                        nc.scalar.activation(q_hi[:, 0, :], q32[:].rearrange("p c n -> p (c n)"), ACT.Copy).then_inc(qhi_done, 1)
                        return
                    c = 2 * u // a.per_chunk
                    act.wait_ge(q32_done, i * C + c + 1)
                    for h in range(2):
                        m = (2 * u + h) % a.per_chunk
                        ins = nc.scalar.activation(q_hi[:, u % NB, h * N:(h + 1) * N], q_of(c), ACT.Copy,
                                                   scale=g["hmask"][:, MASK0 + m:MASK0 + m + 1])
                    ins.then_inc(qhi_done, 1)

                def exp(u):
                    for kt in range(TT):
                        act.wait_ge(st_done, 2 * (i * U + u) + kt + 1)
                        if u >= 2 and kt == 0:
                            act.wait_ge(pv_done, i * U + u - 1)
                        bias = kbias[:, kt:kt + 1] if masked else 0.0
                        nc.scalar.activation(prob[:, u % 2, kt, 0:HN * N], st_ps[kt][:, 0:HN * N], ACT.Exp,
                                             scale=a.scale, bias=bias).then_inc(p_done, 1)

                def outputs(u):
                    rows = o_rows(a, u)
                    act.wait_ge(pv_done, i * U + u + 1)
                    if a.one:
                        nc.scalar.activation(o_raw[:].rearrange("p c n -> p (c n)"), o_ps[:], ACT.Copy).then_inc(o_done, 1)
                    else:
                        nc.scalar.activation(o_raw[rows, u // a.upc, :], o_ps[rows, 0:N], ACT.Copy).then_inc(o_done, 1)

                if qknorm:
                    k_high(0)
                mask_q(0)
                for step in range(U + 3):
                    if step >= 3:
                        outputs(step - 3)
                    if step + 1 < U:
                        if qknorm:
                            k_high(step + 1)
                        mask_q(step + 1)
                    if 1 <= step <= U:
                        exp(step - 1)

            body(0, True)
            with act.Fori(1, B - 1) as i:
                body(i, False)
            body(B - 1, False)
            tail_rows(B - 1)
            for n in range(a.pieces):
                over(B - 1, n)

        @block.tensor
        def _(pe):
            mm = nc.tensor.matmul

            def three(out, lhs, rhs, start, stop):
                mm(out, lhs[0], rhs[0], start=start, stop=False)
                mm(out, lhs[1], rhs[0], start=False, stop=False)
                return mm(out, lhs[0], rhs[1], start=False, stop=stop)

            def transposes(bank):
                for k in range(KD):
                    for tt in range(TT):
                        last = nc.tensor.transpose(bank[:, k * N + tt * P:k * N + (tt + 1) * P],
                                                   xn[:, tt, k * P:(k + 1) * P], g["ident"][:])
                return last

            pe.wait_ge(xn_done, 1)
            transposes(ring[0]).then_inc(pe_first, 1)
            pe.wait_ge(lo_done, NP_)
            pe.wait_ge(pre, 4 + 2 * qknorm + masked)

            def variances(i, c):
                pe.wait_ge(sq_done, i * C + c + 1)
                mm(s_ps[0][0:32, :], g["pair_sel"][:, 30 - 2 * c:62 - 2 * c], sq[:], start=(c == 0), stop=(c == C - 1),
                   skip_group_check=True).then_inc(var_done, 1)

            def take(i, *turn):
                pe.wait_ge(turn_free, i * NR + AT[turn] + 1)
                return bank_of(*turn)

            def over(i, n):
                bank = take(i, "over", n)
                for j in range(2):
                    c = 2 * n + j
                    mm(bank[:, j * N:(j + 1) * N], spread[:, c * P:(c + 1) * P], rsum_hi[:], start=True, stop=False)
                    last = mm(bank[:, j * N:(j + 1) * N], spread[:, c * P:(c + 1) * P], rsum_lo[:], start=False, stop=True)
                last.then_inc(turn_done, 1)

            def project(i):
                bank = take(i, "out", 0)
                pe.wait_ge(olo_done, i * a.pieces)
                for tt in range(TT):
                    for c in range(OC):
                        last = three(bank[:, tt * D:(tt + 1) * D],
                                     [o[:, c, tt * P:(tt + 1) * P] for o in (o_hi, o_lo)],
                                     [w[:, c, :] for w in wo], c == 0, c == OC - 1)
                last.then_inc(turn_done, 1)

            def body(i, first, final):
                def unused(n):
                    pe.wait_ge(turn_done, i * NR + n)
                    pe.sem_inc(turn_done, 1)

                pe.wait_ge(xlo_done, i + 1)
                qk_made = 0
                for n, (kind, c) in enumerate(a.turns):
                    if kind == "qk":
                        bank = take(i, kind, c)
                        for part, w in ((0, wq), (1, wk)):
                            for k in range(KD):
                                last = three(bank[:, part * N:(part + 1) * N],
                                             [w[j][:, k, c * P:(c + 1) * P] for j in range(2)],
                                             [xt[j][:, k, :] for j in range(2)], k == 0, k == KD - 1)
                        last.then_inc(turn_done, 1)
                        if qknorm and c >= 1:
                            variances(i, c - 1)
                    elif kind == "over" or kind == "out":
                        if first:
                            unused(n)
                            continue
                        if c == 0 and kind == "over":
                            pe.wait_ge(rsum_lo_done, i)
                        over(i, c) if kind == "over" else project(i)
                    elif kind == "v":
                        if qknorm and c == 0:
                            variances(i, C - 1)
                        tt, c0 = c * a.vpiece // a.vw, c * a.vpiece % a.vw
                        bank = take(i, kind, c)
                        for k in range(KD):
                            last = three(bank[:, 0:a.vpiece],
                                         [xt[j][:, k, tt * P:(tt + 1) * P] for j in range(2)],
                                         [wv[j][:, k, c0:c0 + a.vpiece] for j in range(2)], k == 0, k == KD - 1)
                        last.then_inc(turn_done, 1)

                def qk_scale(c):
                    bank = take(i, "norm", c)
                    if c == 0:
                        pe.wait_ge(rqlo_done, i + 1)
                    mm(bank[:], spread[:, c * P:(c + 1) * P], rq_hi[:], start=True, stop=False)
                    mm(bank[:], spread[:, c * P:(c + 1) * P], rq_lo[:], start=False, stop=True).then_inc(turn_done, 1)

                def scores(u):
                    pe.wait_ge(qhi_done, i * U + u + 1)
                    if masked and u == 0:
                        pe.wait_ge(mrow_done, i + 1)
                    for qt in range(TT):
                        if masked:
                            mm(s_ps[qt][:], g["ones_r"][:], mrow[:], start=True, stop=False, skip_group_check=True)
                        for h in range(HN):
                            if a.one:
                                for c in range(C):
                                    last = mm(s_ps[qt][:, 0:N], q_hi[:, 0, c * N + qt * P:c * N + (qt + 1) * P],
                                              k_hi[:, c, :], start=(c == 0), stop=(c == C - 1))
                            else:
                                last = mm(s_ps[qt][:, h * N:(h + 1) * N],
                                          q_hi[:, u % NB, h * N + qt * P:h * N + (qt + 1) * P],
                                          k_hi[:, 2 * u // a.per_chunk % KR, :], start=not masked, stop=True,
                                          skip_group_check=masked)
                        last.then_inc(s_done, 1)

                def max_rows(u):
                    pe.wait_ge(mx_done, i * U + u + 1)
                    n = 2 * HN
                    bank = take(i, "max", u)
                    nc.tensor.transpose(bank[0:n, 0:P], mx[:, 0:n], g["ident"][:]).then_inc(turn_done, 1)

                def scores_t(u):
                    pe.wait_ge(qlo_done, i * U + u + 1)
                    if qknorm:
                        pe.wait_ge(klo_done, i * C + u + 1)
                    for kt in range(TT):
                        if u >= 1:
                            pe.wait_ge(p_done, 2 * (i * U + u) - 1 + kt)
                        out = st_ps[kt][:, 0:HN * N]
                        ks = slice(kt * P, (kt + 1) * P)
                        if a.one:
                            for c in range(C):
                                three(out, [k_hi[:, c, ks], k_lo[:, c, ks]],
                                      [x[:, 0, c * N:(c + 1) * N] for x in (q_hi, q_lo)], c == 0, False)
                        else:
                            c = 2 * u // a.per_chunk % KR
                            three(out, [k_hi[:, c, ks], k_lo[:, c, ks]],
                                  [x[:, u % NB, :] for x in (q_hi, q_lo)], True, False)
                        if kt == 0:
                            pe.wait_ge(shift_done, i * U + u + 1)
                        mm(out, g["ones_r"][:], shift[:, u % 2, 0:HN * N], start=False, stop=True).then_inc(st_done, 1)

                def weighted(u):
                    if u or not first:
                        pe.wait_ge(o_done, i * U + u)
                    if u == 0 and not first:
                        pe.wait_ge(rsum_done, i)
                    for kt in range(TT):
                        pe.wait_ge(p_done, 2 * (i * U + u) + kt + 1)
                        for h in range(HN):
                            hd, ps = HN * u + h, prob[:, u % 2, kt, h * N:(h + 1) * N]
                            if a.one:
                                for c in range(C):
                                    mm(o_ps[:, c * N:(c + 1) * N], v[:, kt, c * P:(c + 1) * P], ps,
                                       start=(kt == 0 and c == 0), stop=(kt == TT - 1), skip_group_check=True)
                            else:
                                at = o_row(a, u, h)
                                mm(o_ps[at:at + a.vd, 0:N], v[:, kt, hd * a.vd:(hd + 1) * a.vd], ps,
                                   start=(kt == 0), stop=(kt == TT - 1), skip_group_check=True)
                            last = mm(sum_ps[0:32, 0:N], g["head_sel"][:, 31 - hd:63 - hd], ps,
                                      start=(kt == 0 and hd == 0), stop=(kt == TT - 1 and hd == a.heads - 1),
                                      skip_group_check=True)
                    last.then_inc(pv_done, 1)

                if qknorm:
                    qk_scale(0)
                for step in range(U + 2):
                    if 1 <= step <= U:
                        max_rows(step - 1)
                    if step < U:
                        scores(step)
                    if qknorm and step + 1 < U:
                        qk_scale(step + 1)
                    if 1 <= step <= U:
                        scores_t(step - 1)
                    if 2 <= step <= U + 1:
                        weighted(step - 2)
                    if step == LN_STEP and final:
                        unused(AT["ln", 0])
                    elif step == LN_STEP:
                        bank = take(i, "ln", 0)
                        pe.wait_ge(xn_done, i + 2)
                        transposes(bank).then_inc(turn_done, 1)
                if ("spare", 0) in AT:
                    unused(NR - 1)

            body(0, True, False)
            with pe.Fori(1, B - 1) as i:
                body(i, False, False)
            body(B - 1, False, True)
            pe.wait_ge(rsum_lo_done, B)
            for n, (kind, c) in enumerate(a.turns[:AT["out", 0]]):
                if kind == "over":
                    over(B, c)
                else:
                    pe.wait_ge(turn_done, B * NR + n)
                    pe.sem_inc(turn_done, 1)
            project(B)

        @block.vector
        def _(dve):
            V = nc.vector
            tile = lambda j: g["x"][:, bass.ds(j, 1), :].squeeze(1)
            column = lambda row, i: g["mod"][:, row, bass.ds(i, 1)]

            def normalise(j):
                if not a.norm:
                    for tt in range(TT):
                        ins = V.tensor_copy(xn[:, tt, :], tile(j * TT + tt))
                    ins.then_inc(xn_done, 1)
                    return
                for tt in range(TT):
                    V.bn_stats(stats[:, tt, :], tile(j * TT + tt)).then_inc(stats_done, 1)
                for tt in range(TT):
                    dve.wait_ge(stats_done, TT * j + tt + 1)
                    dve.sem_inc(passed_dve, 1)
                    V.bn_aggr(mv[:, tt, :], stats[:, tt, :]).then_inc(aggr_done, 1)
                if a.norm == "rms":
                    dve.wait_ge(aggr_done, (TT + 1) * j + TT)
                    V.tensor_tensor(ve2[:], mv[:, :, 0], mv[:, :, 0], ALU.mult).then_inc(aggr_done, 1)
                    dve.wait_ge(aggr_done, (TT + 1) * j + TT + 1)
                    V.scalar_tensor_tensor(ve[:], ve2[:], a.eps, mv[:, :, 1], ALU.add, ALU.add).then_inc(ve_done, 1)
                else:
                    dve.wait_ge(aggr_done, TT * (j + 1))
                    V.tensor_scalar(ve[:], mv[:, :, 1], a.eps, None, ALU.add).then_inc(ve_done, 1)
                dve.wait_ge(rstd_done, j + 1)
                for tt in range(TT):
                    if a.norm == "rms":
                        ins = V.tensor_scalar(xn[:, tt, :], tile(j * TT + tt), rstd[:, tt:tt + 1], None, ALU.mult)
                    else:
                        ins = V.tensor_scalar(xn[:, tt, :], tile(j * TT + tt), mv[:, tt, 0:1], rstd[:, tt:tt + 1],
                                              ALU.subtract, ALU.mult)
                ins.then_inc(xn_done, 1)

            def modulate(j, bank):
                for k in range(KD):
                    if nm == "L2a":
                        ins = V.tensor_copy(xm[:, k, :], bank[:, k * N:(k + 1) * N])
                    else:
                        at = MOD_AT[nm]
                        ins = V.tensor_scalar(xm[:, k, :], bank[:, k * N:(k + 1) * N], column(at + k, j),
                                              column(at + 2 + k, j), ALU.mult, ALU.add)
                ins.then_inc(xm_done, 1)

            def x_lo(j):
                dve.wait_ge(xhi_done, j + 1)
                V.tensor_tensor(xt[1][:], xm[:], xt[0][:].bitcast(F32), ALU.subtract).then_inc(xlo_done, 1)

            dve.sem_inc(turn_free, 2)
            if qknorm:
                V.memset(eps_col[:], a.eps).then_inc(consts, 1)
            loader(dve=dve)[2]()
            if masked:
                dve.wait_ge(mask_in, 48)
                V.tensor_scalar(key_bias[:], mask_u8[:], 1.0, 3.0e38, ALU.subtract, ALU.mult).then_inc(kb_done, 1)
                dve.wait_ge(kb_done, 1)
            dve.wait_ge(pre, 4 + 2 * qknorm + masked)
            normalise(0)
            dve.wait_ge(pe_first, 1)
            modulate(0, ring[0])
            x_lo(0)

            def tail_rows(j):
                dve.wait_ge(pv_done, j * U + U)
                V.reciprocal(rsum[:], sum_ps[0:a.heads, 0:N]).then_inc(rsum_done, 1)
                dve.wait_ge(rsum_hi_done, j + 1)
                V.tensor_tensor(rsum_lo[0:a.heads, :], rsum[:], rsum_hi[0:a.heads, :].bitcast(F32), ALU.subtract).then_inc(rsum_lo_done, 1)

            def over(i, n):
                bank = bank_of("over", n)
                dve.wait_ge(turn_done, i * NR + AT["over", n] + 1)
                dve.wait_ge(o_done, i * U)
                if n >= 2:
                    dve.wait_ge(olo_done, (i - 1) * a.pieces + n - 1)
                V.tensor_tensor(o32[:, n % 2, :], o_raw[:, 2 * n:2 * n + 2, :].rearrange("p c n -> p (c n)"), bank[:], ALU.mult)\
                    .then_inc(on_done, 1)
                dve.wait_ge(on_done, (i - 1) * a.pieces + n + 1)
                dve.sem_inc(turn_free, 1)

            def o_low(i, n):
                dve.wait_ge(ohi_done, (i - 1) * a.pieces + n + 1)
                if a.one:
                    for c in range(2):
                        vb = COL_AT["L1_cond_v_b"] + c
                        ins = V.scalar_tensor_tensor(o_lo[:, c, :], o32[:, 0, c * N:(c + 1) * N], cols[:, vb:vb + 1],
                                                     o_hi[:, c, :].bitcast(F32), ALU.add, ALU.subtract)
                else:
                    pair = lambda o: o[:, 2 * n:2 * n + 2, :].rearrange("p c n -> p (c n)")
                    ins = V.tensor_tensor(pair(o_lo), o32[:, n % 2, :], pair(o_hi).bitcast(F32), ALU.subtract)
                ins.then_inc(olo_done, 1)

            def finish(i):
                bank = bank_of("out", 0)
                dve.wait_ge(turn_done, i * NR + AT["out", 0] + 1)
                j = i - 1
                gates_at = None
                if a.gated:
                    gates_at = (gate_in, 32 * j + 32 + (16 if nm == "L2a" else 0))
                residual(nc, dve, {"step": ep_step, "done": ep_done, "xh": xh_done, "ve2": ve2_done, "rstd2": rstd2_done, "passed": passed_dve},
                         nm, j, [j * TT + tt for tt in range(TT)], [bank[:, tt * D:(tt + 1) * D] for tt in range(TT)],
                         lambda j: gate[:, 0, :], a.eps, (y, y2, stats, mv, ve2, rstd2, y_bias), g,
                         residual_steps(nm, TT), gates_at)
                dve.wait_ge(ep_done, i)
                dve.sem_inc(turn_free, 1)

            def body(i, first, final):
                def unused(n):
                    dve.wait_ge(turn_free, i * NR + n + 2)
                    dve.sem_inc(turn_free, 1)

                if not first:
                    tail_rows(i - 1)
                if masked:
                    V.tensor_copy(kbias[:], key_bias[:, :, bass.ds(i, 1)].squeeze(2)).then_inc(kb_done, 1)
                    V.tensor_scalar(mrow[0:1, :].rearrange("o (h n) -> o h n", h=2), mrow_u8[0:1, :, bass.ds(i, 1), :].squeeze(2),
                                    1.0, 1.0e30, ALU.subtract, ALU.mult).then_inc(mrow_done, 1)
                owed = []

                def qk_low_rows():
                    dve.wait_ge(rqhi_done, i + 1)
                    V.tensor_tensor(rq_lo[0:a.heads, :], rstdq[:], rq_hi[0:a.heads, :].bitcast(F32), ALU.subtract).then_inc(rqlo_done, 1)

                def pay(keep=0):
                    while len(owed) > keep:
                        o_low(i, owed.pop(0))

                for n, (kind, c) in enumerate(a.turns):
                    bank = ring[n % 2]
                    if kind == "qk" and qknorm:
                        dve.wait_ge(sq_done, i * C + c + 1)
                        dve.wait_ge(raw_done, i * C + c + 1)
                        dve.sem_inc(turn_free, 1)
                    elif kind == "qk":
                        dve.wait_ge(khi_done, i * C + c + 1)
                        if nm == "L1a":
                            kb = COL_AT["L1_cond_k_b"] + c
                            ins = V.scalar_tensor_tensor(k_lo[:, c, :], bank[:, N:2 * N], cols[:, kb:kb + 1],
                                                         k_hi[:, c, :].bitcast(F32), ALU.add, ALU.subtract)
                        else:
                            ins = V.tensor_tensor(k_lo[:, c, :], bank[:, N:2 * N], k_hi[:, c, :].bitcast(F32),
                                                  ALU.subtract)
                        ins.then_inc(turn_free, 1)
                    elif first and kind in ("over", "out"):
                        if qknorm and kind == "out":
                            qk_low_rows()
                        unused(n)
                    elif kind == "over":
                        pay(1)
                        over(i, c)
                        owed.append(c)
                    elif kind == "v":
                        tt, c0 = c * a.vpiece // a.vw, c * a.vpiece % a.vw
                        dve.wait_ge(turn_done, i * NR + n + 1)
                        V.tensor_copy(v[:, tt, c0:c0 + a.vpiece], bank[:, 0:a.vpiece]).then_inc(turn_free, 1)
                        pay()
                    elif kind == "out":
                        pay()
                        if qknorm:
                            qk_low_rows()
                        finish(i)
                

                def q_low(u):
                    dve.wait_ge(qhi_done, i * U + u + 1)
                    if a.one:
                        V.tensor_tensor(q_lo[:, 0, :], q32[:].rearrange("p c n -> p (c n)"),
                                        q_hi[:, 0, :].bitcast(F32), ALU.subtract).then_inc(qlo_done, 1)
                        return
                    if u >= NB:
                        dve.wait_ge(st_done, 2 * (i * U + u - NB) + 2)
                    for h in range(2):
                        m = MASK0 + (2 * u + h) % a.per_chunk
                        ins = V.scalar_tensor_tensor(q_lo[:, u % NB, h * N:(h + 1) * N], q_of(2 * u // a.per_chunk),
                                                     g["hmask"][:, m:m + 1],
                                                     q_hi[:, u % NB, h * N:(h + 1) * N].bitcast(F32),
                                                     ALU.mult, ALU.subtract)
                    ins.then_inc(qlo_done, 1)

                def maxes(u):
                    for qt in range(TT):
                        dve.wait_ge(s_done, 2 * (i * U + u) + qt + 1)
                        ins = V.tensor_reduce(mx[:, 0:2 * HN].rearrange("p (h q) -> p h q", q=2)[:, :, qt],
                                              s_ps[qt][:, 0:HN * N].rearrange("p (h n) -> p h n", h=HN), AX.X, ALU.max)
                    ins.then_inc(mx_done, 1)

                def shifts(u):
                    dve.wait_ge(turn_done, i * NR + AT["max", u] + 1)
                    if u >= 2:
                        dve.wait_ge(st_done, 2 * (i * U + u) - 2)
                    n = 2 * HN
                    rows = bank_of("max", u)[0:n, 0:P].unsqueeze(1).to_broadcast([n, n, P])
                    V.tensor_tensor(shift[0:n, u % 2, 0:HN * N].rearrange("r (b q) -> r b q", q=P),
                                    g["neg_eye"][0:n, 0:n].unsqueeze(2).to_broadcast([n, n, P]),
                                    rows, ALU.mult).then_inc(shift_done, 1)
                    dve.wait_ge(shift_done, i * U + u + 1)
                    dve.sem_inc(turn_free, 1)

                def qk_scaled(c):
                    col = lambda n: cols[:, COL_AT[n]:COL_AT[n] + 1]
                    bank = bank_of("norm", c)
                    dve.wait_ge(turn_done, i * NR + AT["norm", c] + 1)
                    V.tensor_tensor(qn[:], raw[:, c, :], bank[:], ALU.mult).then_inc(qn_done, 1)
                    dve.wait_ge(qn_done, i * C + c + 1)
                    dve.sem_inc(turn_free, 1)
                    V.tensor_scalar(raw[:, c, N:2 * N], qn[:, N:2 * N], col("kn_g2"), col("kn_b2"), ALU.mult, ALU.add)\
                        .then_inc(kn_done, 1)
                    V.tensor_scalar(q_of(c), qn[:, 0:N], col("qn_g2"), col("qn_b2"), ALU.mult, ALU.add)\
                        .then_inc(q32_done, 1)
                    dve.wait_ge(q32_done, i * C + c + 1)
                    dve.wait_ge(khi_done, i * C + c + 1)
                    V.tensor_tensor(k_lo[:, c % KR, :], raw[:, c, N:2 * N], k_hi[:, c % KR, :].bitcast(F32), ALU.subtract).then_inc(klo_done, 1)

                if qknorm:
                    qk_scaled(0)
                q_low(0)
                for step in range(U + 2):
                    if 1 <= step <= U:
                        shifts(step - 1)
                    if step < U:
                        maxes(step)
                    if step + 1 < U:
                        if qknorm:
                            qk_scaled(step + 1)
                        q_low(step + 1)
                    if step == 1 and not final:
                        normalise(i + 1)
                    if step == LN_STEP and final:
                        unused(AT["ln", 0])
                    elif step == LN_STEP:
                        dve.wait_ge(turn_done, i * NR + AT["ln", 0] + 1)
                        modulate(i + 1, bank_of("ln", 0))
                        dve.wait_ge(xm_done, i + 2)
                        dve.sem_inc(turn_free, 1)
                        x_lo(i + 1)
                if ("spare", 0) in AT:
                    unused(NR - 1)

            body(0, True, False)
            with dve.Fori(1, B - 1) as i:
                body(i, False, False)
            body(B - 1, False, True)
            tail_rows(B - 1)
            for n, (kind, c) in enumerate(a.turns[:AT["out", 0]]):
                if kind == "over":
                    over(B, c)
                    o_low(B, c)
                else:
                    dve.wait_ge(turn_free, B * NR + n + 2)
                    dve.sem_inc(turn_free, 1)
            finish(B)


BB = 2
T4 = BB * TT
NN = BB * N


def mlp(nc, t, g, nm, norm, eps):
    gated = nm != "L1m"
    with semaphores(nc, nm) as sem, ExitStack() as ctx:
        sb = lambda n, s, d=F32: ctx.enter_context(nc.sbuf_tensor(f"{nm}_{n}", s, d))
        pb = lambda n: ctx.enter_context(nc.psum_tensor(f"{nm}_{n}", [P, 512], F32))
        up_ps, tp_ps, down_ps = [pb(f"up{j}") for j in range(2)], [pb(f"tp{k}") for k in range(KD)], \
            [pb(f"down{j}") for j in range(T4)]
        w1 = [sb(f"w1{j}", [P, KD, MLP], F32R) for j in range(2)]
        w2 = [sb(f"w2{j}", [P, MC, D], F32R) for j in range(2)]
        stage = sb("stage", [P, 2, 1024])
        xn, xm = sb("xn", [P, T4, D]), sb("xm", [P, KD, NN])
        xt = [sb(f"xt{j}", [P, KD, NN], F32R) for j in range(2)]
        stats, mv = sb("stats", [P, T4, 6]), sb("mv", [P, T4, 2])
        ve, ve2, rstd, rstd2 = sb("ve", [P, T4]), sb("ve2", [P, T4]), sb("rstd", [P, T4]), sb("rstd2", [P, T4])
        h32 = sb("h32", [P, 2, NN])
        h = [sb(f"h{j}", [P, MC, NN], F32R) for j in range(2)]
        y, y2 = sb("y", [P, T4, D]), sb("y2", [P, T4, D])
        gate, y_bias = sb("gate", [P, BB, 2, D]), sb("y_bias", [P, D])

        landed = [sem("landed0"), sem("landed1")]
        hi_done, lo_done = sem("hi_done"), sem("lo_done")
        stats_done, aggr_done, ve_done, rstd_done, xn_done = (sem(x) for x in ("stats", "aggr", "ve", "rstd", "xn"))
        tp_done, xm_done, xhi_done, xlo_done = sem("tp"), sem("xm"), sem("xhi"), sem("xlo")
        up_done, gelu_done, hhi_done, hlo_done = sem("up"), sem("gelu"), sem("hhi"), sem("hlo")
        down_done, down_free, ep_done, ep_step, xh_done = (sem(x) for x in ("down", "down_free", "ep", "ep_step", "xh"))
        gate_in, ve2_done, rstd2_done, passed = sem("gate_in"), sem("ve2"), sem("rstd2"), sem("passed")
        passed_dve = sem("passed_dve")

        pieces = []
        for k in range(KD):
            pieces.append((t[nm + "_w1"][k * P:(k + 1) * P, :], w1[0][:, k, :], w1[1][:, k, :], False))
        for m in range(MC):
            pieces.append((t[nm + "_w2"][m * P:(m + 1) * P, :], w2[0][:, m, :], w2[1][:, m, :], False))
        loader = lambda sp=None, pool=None, dve=None: split_weights(
            nc, (sp, pool, dve), stage, (landed, hi_done, lo_done), pieces)
        extra = 16 if nm == "L2m" else 0
        gates_in = lambda i: 16 * 2 * BB * i + 16 * 2 * BB + extra
        IT = B // BB
        block = ctx.enter_context(nc.Block())

        @block.sync
        def _(sp):
            if gated:
                at = GATE_AT[nm]
                for bb in range(BB):
                    for j in range(2):
                        sp.dma_start(gate[:, bb, j, :], t["gate_rows"][at + j, bb, :].partition_broadcast(P)).then_inc(gate_in, 16)
            else:
                sp.dma_start(gate[:, 0, 0, :], t["L1_cond_mlp_b2"].partition_broadcast(P)).then_inc(gate_in, 16)
            if nm == "L2m":
                sp.dma_start(y_bias[:], t["L2_cond_fc2_b"].partition_broadcast(P)).then_inc(gate_in, 16)
            loader(sp=sp)[0]()
            if gated:
                with sp.Fori(0, IT - 1) as i:
                    sp.wait_ge(ep_done, i + 1)
                    for bb in range(BB):
                        for j in range(2):
                            sp.dma_start(gate[:, bb, j, :], t["gate_rows"][at + j, bass.ds(BB * i + BB + bb, 1), :]
                                         .squeeze(0).partition_broadcast(P)).then_inc(gate_in, 16)

        @block.gpsimd
        def _(pool):
            def gated_wait(s, val):
                pool.wait_ge(s, val)
                pool.sem_inc(passed, 1)

            def token_rstd(j):
                if norm:
                    gated_wait(ve_done, j + 1)
                    nc.gpsimd.tensor_tensor(rstd[:], ve[:], g["mhalf"][:, 0:T4], ALU.pow).then_inc(rstd_done, 1)

            def x_hi(j):
                gated_wait(xm_done, j + 1)
                nc.gpsimd.tensor_copy(xt[0][:], xm[:]).then_inc(xhi_done, 1)

            loader(pool=pool)[1]()
            token_rstd(0)
            x_hi(0)

            def body(i, more):
                for m in range(MC):
                    gated_wait(gelu_done, MC * i + m + 1)
                    nc.gpsimd.tensor_copy(h[0][:, m, :], h32[:, m % 2, :]).then_inc(hhi_done, 1)
                    if m == 3 and more:
                        token_rstd(i + 1)
                if more:
                    x_hi(i + 1)
                gated_wait(gate_in, gates_in(i) if gated else 16)
                for j in range(T4):
                    hrow = gate[:, j // TT, 1, :] if gated else gate[:, 0, 0, :]
                    tile = g["x"][:, bass.ds(i * T4 + j, 1), :].squeeze(1)
                    nc.gpsimd.tensor_tensor(tile, tile, hrow, ALU.add).then_inc(xh_done, 1)
                if nm == "L2m":
                    gated_wait(ve2_done, i + 1)
                    nc.gpsimd.tensor_tensor(rstd2[:], ve2[:], g["mhalf"][:, 0:T4], ALU.pow).then_inc(rstd2_done, 1)

            with pool.Fori(0, IT - 1) as i:
                body(i, True)
            body(IT - 1, False)

        @block.scalar
        def _(act):
            b1 = COL_AT[{"L0m": "L0_cond_b1", "L1m": "L1_cond_mlp_b1", "L2m": "L2_cond_fc1_b"}[nm]]
            with act.Fori(0, IT) as i:
                for m in range(MC):
                    act.wait_ge(up_done, MC * i + m + 1)
                    if m >= 2:
                        act.wait_ge(hlo_done, MC * i + m - 1)
                    nc.scalar.activation(h32[:, m % 2, :], up_ps[m % 2][:], ACT.Gelu,
                                         bias=g["cols"][:, b1 + m:b1 + m + 1]).then_inc(gelu_done, 1)

        @block.tensor
        def _(pe):
            mm = nc.tensor.matmul

            def three(out, lhs, rhs, start, stop):
                mm(out, lhs[0], rhs[0], start=start, stop=False)
                mm(out, lhs[1], rhs[0], start=False, stop=False)
                return mm(out, lhs[0], rhs[1], start=False, stop=stop)

            def transposes(j):
                pe.wait_ge(xn_done, j + 1)
                for k in range(KD):
                    for tt in range(T4):
                        last = nc.tensor.transpose(tp_ps[k][:, tt * P:(tt + 1) * P], xn[:, tt, k * P:(k + 1) * P],
                                                   g["ident"][:])
                last.then_inc(tp_done, 1)

            transposes(0)
            pe.wait_ge(lo_done, len(pieces))

            def body(i, more):
                pe.wait_ge(xlo_done, i + 1)
                for m in range(MC):
                    if m >= 2:
                        pe.wait_ge(gelu_done, MC * i + m - 1)
                    for k in range(KD):
                        last = three(up_ps[m % 2][:], [w[:, k, m * P:(m + 1) * P] for w in w1],
                                     [x[:, k, :] for x in xt], k == 0, k == KD - 1)
                    last.then_inc(up_done, 1)
                pe.wait_ge(down_free, i + 1)
                for m in range(MC):
                    pe.wait_ge(hlo_done, MC * i + m + 1)
                    for tt in range(T4):
                        last = three(down_ps[tt][:, 0:D], [x[:, m, tt * P:(tt + 1) * P] for x in h],
                                     [w[:, m, :] for w in w2], m == 0, m == MC - 1)
                    if m == 3 and more:
                        transposes(i + 1)
                last.then_inc(down_done, 1)

            with pe.Fori(0, IT - 1) as i:
                body(i, True)
            body(IT - 1, False)

        @block.vector
        def _(dve):
            V = nc.vector
            tile = lambda j: g["x"][:, bass.ds(j, 1), :].squeeze(1)

            def normalise(j):
                if not norm:
                    for tt in range(T4):
                        ins = V.tensor_copy(xn[:, tt, :], tile(j * T4 + tt))
                    ins.then_inc(xn_done, 1)
                    return
                for tt in range(T4):
                    V.bn_stats(stats[:, tt, :], tile(j * T4 + tt)).then_inc(stats_done, 1)
                for tt in range(T4):
                    dve.wait_ge(stats_done, T4 * j + tt + 1)
                    dve.sem_inc(passed_dve, 1)
                    V.bn_aggr(mv[:, tt, :], stats[:, tt, :]).then_inc(aggr_done, 1)
                if norm == "rms":
                    dve.wait_ge(aggr_done, (T4 + 1) * j + T4)
                    V.tensor_tensor(ve2[:], mv[:, :, 0], mv[:, :, 0], ALU.mult).then_inc(aggr_done, 1)
                    dve.wait_ge(aggr_done, (T4 + 1) * j + T4 + 1)
                    V.scalar_tensor_tensor(ve[:], ve2[:], eps, mv[:, :, 1], ALU.add, ALU.add).then_inc(ve_done, 1)
                else:
                    dve.wait_ge(aggr_done, T4 * (j + 1))
                    V.tensor_scalar(ve[:], mv[:, :, 1], eps, None, ALU.add).then_inc(ve_done, 1)
                dve.wait_ge(rstd_done, j + 1)
                for tt in range(T4):
                    if norm == "rms":
                        ins = V.tensor_scalar(xn[:, tt, :], tile(j * T4 + tt), rstd[:, tt:tt + 1], None, ALU.mult)
                    else:
                        ins = V.tensor_scalar(xn[:, tt, :], tile(j * T4 + tt), mv[:, tt, 0:1], rstd[:, tt:tt + 1],
                                              ALU.subtract, ALU.mult)
                ins.then_inc(xn_done, 1)

            def modulate(j):
                dve.wait_ge(tp_done, j + 1)
                for k in range(KD):
                    if not norm:
                        ins = V.tensor_copy(xm[:, k, :], tp_ps[k][:])
                        continue
                    at = MOD_AT[nm]
                    for bb in range(BB):
                        col = lambda row: g["mod"][:, row, bass.ds(BB * j + bb, 1)]
                        ins = V.tensor_scalar(xm[:, k, bb * N:(bb + 1) * N], tp_ps[k][:, bb * N:(bb + 1) * N],
                                              col(at + k), col(at + 2 + k), ALU.mult, ALU.add)
                ins.then_inc(xm_done, 1)
                dve.wait_ge(xhi_done, j + 1)
                V.tensor_tensor(xt[1][:], xm[:], xt[0][:].bitcast(F32), ALU.subtract).then_inc(xlo_done, 1)

            dve.sem_inc(down_free, 1)
            loader(dve=dve)[2]()
            normalise(0)
            modulate(0)

            def body(i, more):
                for m in range(MC):
                    dve.wait_ge(hhi_done, MC * i + m + 1)
                    V.tensor_tensor(h[1][:, m, :], h32[:, m % 2, :], h[0][:, m, :].bitcast(F32), ALU.subtract)\
                        .then_inc(hlo_done, 1)
                    if m == 3 and more:
                        normalise(i + 1)
                if more:
                    modulate(i + 1)
                dve.wait_ge(down_done, i + 1)
                residual(nc, dve, {"step": ep_step, "done": ep_done, "xh": xh_done, "ve2": ve2_done, "rstd2": rstd2_done, "passed": passed_dve},
                         nm, i, [i * T4 + tt for tt in range(T4)], [p[:, 0:D] for p in down_ps],
                         lambda j: gate[:, j // TT, 0, :], eps, (y, y2, stats, mv, ve2, rstd2, y_bias), g,
                         residual_steps(nm, T4), (gate_in, gates_in(i)) if gated else None)
                dve.wait_ge(ep_done, i + 1)
                dve.sem_inc(down_free, 1)

            with dve.Fori(0, IT - 1) as i:
                body(i, True)
            body(IT - 1, False)


BF16 = mybir.dt.bfloat16
ROW = D + E
BITS = 30


def route(nc, t, g, out):
    with semaphores(nc, "r") as sem, ExitStack() as ctx:
        sb = lambda n, s, d=F32: ctx.enter_context(nc.sbuf_tensor(f"r_{n}", s, d))
        pb = lambda n: ctx.enter_context(nc.psum_tensor(f"r_{n}", [P, 512], F32))
        tp_ps, lg_ps, cnt_ps, pre_ps, tot_ps = [pb("tp0"), pb("tp1")], pb("lg"), pb("cnt"), pb("pre"), pb("tot")
        list_ps = [pb("list0"), pb("list1")]
        wg, tri, iota_f = sb("wg", [P, KD, E]), sb("tri", [P, P]), sb("iota_f", [P, P])
        tval, pval = sb("tval", [P, TILES]), sb("pval", [P, 1])
        xs, xt = sb("xs", [P, T4, D]), sb("xt", [P, KD, NN])
        logit = sb("logit", [P, TILES, E])
        lmax, lsum, lrec, e_base = sb("lmax", [P, TILES]), sb("lsum", [P, TILES]), sb("lrec", [P, TILES]), sb("e_base", [P, TILES * E])
        centred, ex, gates = (sb(n, [P, TILES, E]) for n in ("centred", "ex", "gates"))
        ge = sb("ge", [P, E, TILES])
        thr, cand, bit = (sb(n, [P, E], U32) for n in ("thr", "cand", "bit"))
        hit, keep = sb("hit", [P, E, TILES]), sb("keep", [P, E], U32)
        part_count, need = sb("part_count", [P, E]), sb("need", [P, E])
        above, equal, sel = (sb(n, [P, E, TILES]) for n in ("above", "equal", "sel"))
        totals, scan, zeros = (sb(n, [P, E, TILES]) for n in ("totals", "scan", "zeros"))
        rank, low = sb("rank", [P, E, TILES]), sb("low", [P, E, TILES])
        ge_h = [sb(f"ge_h{h}", [P, E, TILES]) for h in range(SC + 1)]
        hs = sb("hs", [P, E, TILES])
        vals = sb("vals", [P, E, TILES, 2 * SC], BF16)
        onehot = sb("onehot", [P, 2, TILES, P], BF16)
        iota_b, low_b = sb("iota_b", [P, P], BF16), sb("low_b", [P, E, TILES], BF16)
        lists, idx_f = sb("lists", [P, E, 2 * SC]), sb("idx_f", [P, E, SC])

        const_in, xs_done, tp_done, xt_done, lg_done, lgc_done = (sem(n) for n in ("const", "xs", "tp", "xt", "lg", "lgc"))
        xt2_done, pow_in, pow_done, chain, made = sem("xt2"), sem("pow_in"), sem("pow"), sem("chain"), sem("made")
        count_in, count_done, pre_in, pre_done = sem("count_in"), sem("count_done"), sem("pre_in"), sem("pre_done")
        hot_done, list_done, list_read, stored, rows_ready = (sem(n) for n in ("hot", "list", "list_read", "stored", "rows"))
        bchain, passed = sem("bchain"), sem("passed")
        IT = TILES // T4
        block = ctx.enter_context(nc.Block())

        @block.sync
        def _(sp):
            for dst, name in ((tri, "tri"), (iota_f, "iota"), (tval, "tval"), (pval, "pval")):
                sp.dma_start(dst[:], t[name]).then_inc(const_in, 16)
            sp.dma_start(wg[:], t["wg_t"].rearrange("(k p) e -> p k e", p=P)).then_inc(const_in, 16)
            sp.dma_start(out.rearrange("b (t p) d -> p (b t) d", p=P), g["x"][:]).then_inc(stored, 16)
            rows = t["token_rows"].rearrange("(t p) r -> p t r", p=P)
            sp.dma_start(rows[:, :, 0:D], g["x"][:]).then_inc(stored, 16)
            sp.wait_ge(rows_ready, 1)
            sp.dma_start(rows[:, :, D:ROW], gates[:]).then_inc(stored, 16)
            sp.wait_ge(stored, 48)

        @block.gpsimd
        def _(pool):
            nc.gpsimd.memset(e_base[:], float(np.e)).then_inc(made, 1)
            nc.gpsimd.memset(zeros[:], 0.0).then_inc(made, 1)
            pool.wait_ge(pow_in, 1)
            pool.wait_ge(made, 2)
            nc.gpsimd.tensor_tensor(ex[:].rearrange("p t e -> p (t e)"), e_base[:],
                                    centred[:].rearrange("p t e -> p (t e)"), ALU.pow).then_inc(pow_done, 1)

        @block.scalar
        def _(act):
            with act.Fori(0, IT) as i:
                act.wait_ge(tp_done, i + 1)
                nc.scalar.activation(xt[:, 1, :], tp_ps[1][:], ACT.Copy).then_inc(xt2_done, 1)

        @block.tensor
        def _(pe):
            mm = nc.tensor.matmul
            pe.wait_ge(const_in, 80)
            with pe.Fori(0, IT) as i:
                pe.wait_ge(xs_done, i + 1)
                for k in range(KD):
                    for tt in range(T4):
                        last = nc.tensor.transpose(tp_ps[k][:, tt * P:(tt + 1) * P], xs[:, tt, k * P:(k + 1) * P],
                                                   g["ident"][:])
                last.then_inc(tp_done, 1)
                pe.wait_ge(xt_done, i + 1)
                pe.wait_ge(xt2_done, i + 1)
                for tt in range(T4):
                    for k in range(KD):
                        last = mm(lg_ps[:, tt * E:(tt + 1) * E], xt[:, k, tt * P:(tt + 1) * P], wg[:, k, :],
                                  start=(k == 0), stop=(k == KD - 1))
                last.then_inc(lg_done, 1)
            with pe.Fori(0, BITS + 1) as n:
                pe.wait_ge(count_in, n + 1)
                mm(cnt_ps[:, 0:E], g["ones"][:], part_count[:], start=True, stop=True).then_inc(count_done, 1)
            for n, what in enumerate((equal, sel)):
                pe.wait_ge(pre_in, n + 1)
                flat = what[:].rearrange("p e t -> p (e t)")
                mm(pre_ps[:, 0:E * TILES], tri[:], flat, start=True, stop=True)
                mm(tot_ps[:, 0:E * TILES], g["ones"][:], flat, start=True, stop=True).then_inc(pre_done, 1)
            with pe.Fori(0, E // 2) as i:
                for par in range(2):
                    pe.wait_ge(hot_done, 2 * i + par + 1)
                    for tile in range(TILES):
                        last = mm(list_ps[par][:, 0:2 * SC], onehot[:, par, tile, :],
                                  vals[:, bass.ds(2 * i + par, 1), tile, :].squeeze(1),
                                  start=(tile == 0), stop=(tile == TILES - 1))
                    last.then_inc(list_done, 1)

        @block.vector
        def _(dve):
            V = nc.vector
            done = [0]

            def step(ins):
                done[0] += 1
                ins.then_inc(chain, 1)
                dve.wait_ge(chain, done[0])

            with dve.Fori(0, IT) as i:
                V.tensor_copy(xs[:], g["x"][:, bass.ds(i * T4, T4), :]).then_inc(xs_done, 1)
                dve.wait_ge(tp_done, i + 1)
                V.tensor_copy(xt[:, 0, :], tp_ps[0][:]).then_inc(xt_done, 1)
                dve.wait_ge(lg_done, i + 1)
                V.tensor_copy(logit[:, bass.ds(i * T4, T4), :], lg_ps[:, 0:T4 * E].rearrange("p (t e) -> p t e", e=E))\
                    .then_inc(lgc_done, 1)
            dve.wait_ge(lgc_done, IT)
            bc = lambda col: col[:].unsqueeze(2).to_broadcast([P, TILES, E])
            step(V.tensor_reduce(lmax[:], logit[:], AX.X, ALU.max))
            step(V.tensor_tensor(centred[:], logit[:], bc(lmax), ALU.subtract))
            V.engine_nop().then_inc(pow_in, 1)
            dve.wait_ge(pow_done, 1)
            step(V.tensor_reduce(lsum[:], ex[:], AX.X, ALU.add))
            step(V.reciprocal(lrec[:], lsum[:]))
            step(V.tensor_tensor(gates[:], ex[:], bc(lrec), ALU.mult))
            V.engine_nop().then_inc(rows_ready, 1)
            step(V.tensor_copy(ge[:], gates[:].rearrange("p t e -> p e t")))
            step(V.memset(thr[:], 0))
            step(V.memset(bit[:], 1 << (BITS - 1)))
            over = lambda col: col[:].unsqueeze(2).to_broadcast([P, E, TILES])
            per = 5
            with dve.Fori(0, BITS) as n:
                V.tensor_tensor(cand[:], thr[:], bit[:], ALU.bitwise_or).then_inc(bchain, 1)
                dve.wait_ge(bchain, per * n + 1)
                V.tensor_tensor(hit[:], ge[:], over(cand).bitcast(F32), ALU.is_ge).then_inc(bchain, 1)
                V.tensor_scalar(bit[:], bit[:], 1, None, ALU.logical_shift_right).then_inc(bchain, 1)
                dve.wait_ge(bchain, per * n + 3)
                V.tensor_reduce(part_count[:], hit[:], AX.X, ALU.add).then_inc(count_in, 1)
                dve.wait_ge(count_done, n + 1)
                V.tensor_scalar(keep[:], cnt_ps[:, 0:E], float(CAP), None, ALU.is_ge).then_inc(bchain, 1)
                dve.wait_ge(bchain, per * n + 4)
                dve.sem_inc(passed, 1)
                V.copy_predicated(thr[:], keep[:], cand[:]).then_inc(bchain, 1)
                dve.wait_ge(bchain, per * n + 5)
            th = over(thr).bitcast(F32)
            step(V.tensor_tensor(above[:], ge[:], th, ALU.is_gt))
            step(V.tensor_tensor(equal[:], ge[:], th, ALU.is_equal))
            V.tensor_reduce(part_count[:], above[:], AX.X, ALU.add).then_inc(count_in, 1)
            V.engine_nop().then_inc(pre_in, 1)
            dve.wait_ge(count_done, BITS + 1)
            step(V.tensor_scalar(need[:], cnt_ps[:, 0:E], -1.0, float(CAP), ALU.mult, ALU.add))

            def ranks(n):
                dve.wait_ge(pre_done, n + 1)
                step(V.tensor_copy(totals[:].rearrange("p e t -> p (e t)"), tot_ps[:, 0:E * TILES]))
                for e in range(E):
                    step(V.tensor_tensor_scan(scan[:, e, :], totals[:, e, :], zeros[:, e, :], 0.0, ALU.add, ALU.add))
                step(V.tensor_tensor(scan[:], scan[:], totals[:], ALU.subtract))
                step(V.tensor_tensor(rank[:], pre_ps[:, 0:E * TILES].rearrange("p (e t) -> p e t", t=TILES),
                                     scan[:], ALU.add))

            dve.wait_ge(made, 2)
            dve.wait_ge(const_in, 80)
            ranks(0)
            step(V.tensor_tensor(sel[:], rank[:], over(need), ALU.is_lt))
            step(V.tensor_tensor(sel[:], sel[:], equal[:], ALU.mult))
            step(V.tensor_tensor(sel[:], sel[:], above[:], ALU.add))
            V.engine_nop().then_inc(pre_in, 1)
            ranks(1)
            for h in range(1, SC):
                step(V.tensor_scalar(ge_h[h][:], rank[:], float(P * h), None, ALU.is_ge))
            step(V.scalar_tensor_tensor(low[:], ge_h[1][:], -float(P), rank[:], ALU.mult, ALU.add))
            for h in range(2, SC):
                step(V.scalar_tensor_tensor(low[:], ge_h[h][:], -float(P), low[:], ALU.mult, ALU.add))
            step(V.scalar_tensor_tensor(low[:], low[:], 1.0, sel[:], ALU.add, ALU.mult))
            step(V.tensor_scalar(low_b[:], low[:], -1.0, None, ALU.add))
            step(V.tensor_copy(iota_b[:], iota_f[:]))
            step(V.memset(ge_h[0][:], 1.0))
            step(V.memset(ge_h[SC][:], 0.0))
            for h in range(SC):
                step(V.tensor_tensor(hs[:], ge_h[h][:], ge_h[h + 1][:], ALU.subtract))
                step(V.tensor_tensor(vals[:, :, :, 2 * h], hs[:], tval[:].unsqueeze(1).to_broadcast([P, E, TILES]), ALU.mult))
                step(V.tensor_scalar(vals[:, :, :, 2 * h + 1], hs[:], pval[:, 0:1], None, ALU.mult))
            with dve.Fori(0, E // 2) as i:
                for par in range(2):
                    V.tensor_tensor(onehot[:, par, :, :], iota_b[:].unsqueeze(1).to_broadcast([P, TILES, P]),
                                    low_b[:, bass.ds(2 * i + par, 1), :].squeeze(1).unsqueeze(2).to_broadcast([P, TILES, P]),
                                    ALU.is_equal).then_inc(hot_done, 1)
                for par in range(2):
                    dve.wait_ge(list_done, 2 * i + par + 1)
                    V.tensor_copy(lists[:, bass.ds(2 * i + par, 1), :].squeeze(1), list_ps[par][:, 0:2 * SC]).then_inc(list_read, 1)
            dve.wait_ge(list_read, E)
            pairs = lists[:].rearrange("p e (h two) -> p e h two", two=2)
            step(V.scalar_tensor_tensor(idx_f[:], pairs[:, :, :, 0], float(P), pairs[:, :, :, 1], ALU.mult, ALU.add))
            step(V.tensor_copy(g["idx"][:], idx_f[:]))


def experts(nc, t, g, out):
    nm = "moe"
    with semaphores(nc, nm) as sem, ExitStack() as ctx:
        sb = lambda n, s, d=F32: ctx.enter_context(nc.sbuf_tensor(f"{nm}_{n}", s, d))
        pb = lambda n: ctx.enter_context(nc.psum_tensor(f"{nm}_{n}", [P, 512], F32))
        up_ps, tp_ps, down_ps = [pb(f"up{j}") for j in range(2)], [pb(f"tp{k}") for k in range(KD)], \
            [pb(f"down{j}") for j in range(SC)]
        stage1, stage2 = sb("stage1", [P, KD, MLP]), sb("stage2", [P, MC, D])
        w1 = [sb(f"w1{j}", [P, KD, MLP], F32R) for j in range(2)]
        w2 = [sb(f"w2{j}", [P, MC, D], F32R) for j in range(2)]
        idx_now, idx_out = sb("idx_now", [P, SC], U32), sb("idx_out", [P, SC], U32)
        xg = sb("xg", [P, SC, ROW])
        weight, weight_next = sb("weight", [P, SC]), sb("weight_next", [P, SC])
        xn, xm = sb("xn", [P, SC, D]), sb("xm", [P, KD, CAP])
        xt = [sb(f"xt{j}", [P, KD, CAP], F32R) for j in range(2)]
        stats, mv = sb("stats", [P, SC, 6]), sb("mv", [P, SC, 2])
        ve, rstd = sb("ve", [P, SC]), sb("rstd", [P, SC])
        h32 = sb("h32", [P, 2, CAP])
        h = [sb(f"h{j}", [P, MC, CAP], F32R) for j in range(2)]
        b2, y, y2 = sb("b2", [P, D]), sb("y", [P, SC, D]), sb("y2", [P, SC, D])

        stats_done, aggr_done, ve_done, rstd_done, xn_done = (sem(x) for x in ("stats", "aggr", "ve", "rstd", "xn"))
        tp_done, xm_done, xhi_done, xlo_done = sem("tp"), sem("xm"), sem("xhi"), sem("xlo")
        up_done, gelu_done, hhi_done, hlo_done = sem("up"), sem("gelu"), sem("hhi"), sem("hlo")
        down_done, down_free, y_step, y_done = sem("down"), sem("down_free"), sem("y_step"), sem("y_done")
        w1_in, w2_in, b2_in, w1_hi, w1_lo, w2_hi, w2_lo = (sem(x) for x in ("w1_in", "w2_in", "b2_in", "w1_hi", "w1_lo", "w2_hi", "w2_lo"))
        idx_done, gathered, scattered, weight_done, passed, passed_dve = (sem(x) for x in ("idx", "gathered", "scattered", "weight", "passed", "passed_dve"))
        idxo_done, weight_now, y2_free = sem("idxo"), sem("weight_now"), sem("y2_free")
        block = ctx.enter_context(nc.Block())
        w1_d = t["moe_w1"].rearrange("e (k p) n -> e p k n", p=P)
        w2_d = t["moe_w2"].rearrange("e (m p) n -> e p m n", p=P)

        @block.sync
        def _(sp):
            sp.dma_start(stage1[:], w1_d[0]).then_inc(w1_in, 16)
            sp.dma_start(stage2[:], w2_d[0]).then_inc(w2_in, 16)
            sp.dma_start(b2[:], t["L3_cond_b2s"][0, :].partition_broadcast(P)).then_inc(b2_in, 16)
            with sp.Fori(0, E - 1) as e:
                sp.wait_ge(w1_lo, e + 1)
                sp.dma_start(stage1[:], w1_d[bass.ds(e + 1, 1), :, :, :].squeeze(0)).then_inc(w1_in, 16)
                sp.wait_ge(w2_lo, e + 1)
                sp.dma_start(stage2[:], w2_d[bass.ds(e + 1, 1), :, :, :].squeeze(0)).then_inc(w2_in, 16)
                sp.wait_ge(y_done, e + 1)
                sp.dma_start(b2[:], t["L3_cond_b2s"][bass.ds(e + 1, 1), :].squeeze(0).partition_broadcast(P)).then_inc(b2_in, 16)

        @block.gpsimd
        def _(pool):
            def gated_wait(s, val):
                pool.wait_ge(s, val)
                pool.sem_inc(passed, 1)

            def gather(e):
                nc.gpsimd.tensor_copy(idx_now[:], g["idx"][:, bass.ds(e, 1), :].squeeze(1)).then_inc(idx_done, 1)
                gated_wait(idx_done, e + 1)
                for s in range(SC):
                    pool.indirect_dma_start(xg[:, s, :], None, t["token_rows"][:, :],
                                            bass.IndirectOffsetOnAxis(ap=idx_now[:, s:s + 1], axis=0)).then_inc(gathered, 16)

            def token_rstd(e):
                gated_wait(ve_done, e + 1)
                nc.gpsimd.tensor_tensor(rstd[:], ve[:], g["mhalf"][:, 0:SC], ALU.pow).then_inc(rstd_done, 1)

            def x_hi(e):
                gated_wait(xm_done, e + 1)
                nc.gpsimd.tensor_copy(xt[0][:], xm[:]).then_inc(xhi_done, 1)

            def w1_high(e):
                gated_wait(w1_in, 16 * e + 16)
                nc.gpsimd.tensor_copy(w1[0][:], stage1[:]).then_inc(w1_hi, 1)

            def w2_high(e):
                gated_wait(w2_in, 16 * e + 16)
                nc.gpsimd.tensor_copy(w2[0][:], stage2[:]).then_inc(w2_hi, 1)

            def body(e, more):
                if more:
                    gated_wait(xn_done, e + 1)
                    gated_wait(weight_done, e + 1)
                    gather(e + 1)
                for m in range(MC):
                    gated_wait(gelu_done, MC * e + m + 1)
                    nc.gpsimd.tensor_copy(h[0][:, m, :], h32[:, m % 2, :]).then_inc(hhi_done, 1)
                    if m == 3 and more:
                        token_rstd(e + 1)
                if more:
                    w1_high(e + 1)
                    x_hi(e + 1)
                    gated_wait(down_done, e + 1)
                    w2_high(e + 1)
                nc.gpsimd.tensor_copy(idx_out[:], g["idx"][:, bass.ds(e, 1), :].squeeze(1)).then_inc(idxo_done, 1)
                gated_wait(idxo_done, e + 1)
                gated_wait(y_done, e + 1)
                for s in range(SC):
                    pool.indirect_dma_start(out.rearrange("b n d -> (b n) d"),
                                            bass.IndirectOffsetOnAxis(ap=idx_out[:, s:s + 1], axis=0),
                                            y2[:, s, :], None, compute_op=ALU.add).then_inc(scattered, 16)
                gated_wait(scattered, 16 * SC * e + 16 * SC)
                pool.sem_inc(y2_free, 1)

            pool.sem_inc(y2_free, 1)
            gather(0)
            w1_high(0)
            token_rstd(0)
            x_hi(0)
            w2_high(0)
            with pool.Fori(0, E - 1) as e:
                body(e, True)
            body(E - 1, False)
            pool.wait_ge(scattered, 16 * SC * E)

        @block.scalar
        def _(act):
            b1 = COL_AT["L3_cond_b1s"]
            with act.Fori(0, E) as e:
                for m in range(MC):
                    act.wait_ge(up_done, MC * e + m + 1)
                    if m >= 2:
                        act.wait_ge(hlo_done, MC * e + m - 1)
                    nc.scalar.activation(h32[:, m % 2, :], up_ps[m % 2][:], ACT.Gelu_apprx_tanh,
                                         bias=g["cols"][:, bass.ds(b1 + MC * e + m, 1)]).then_inc(gelu_done, 1)

        @block.tensor
        def _(pe):
            mm = nc.tensor.matmul

            def three(out, lhs, rhs, start, stop):
                mm(out, lhs[0], rhs[0], start=start, stop=False)
                mm(out, lhs[1], rhs[0], start=False, stop=False)
                return mm(out, lhs[0], rhs[1], start=False, stop=stop)

            def transposes(e):
                pe.wait_ge(xn_done, e + 1)
                for k in range(KD):
                    for s in range(SC):
                        last = nc.tensor.transpose(tp_ps[k][:, s * P:(s + 1) * P], xn[:, s, k * P:(k + 1) * P],
                                                   g["ident"][:])
                last.then_inc(tp_done, 1)

            def body(e, more):
                pe.wait_ge(w1_lo, e + 1)
                pe.wait_ge(xlo_done, e + 1)
                for m in range(MC):
                    if m >= 2:
                        pe.wait_ge(gelu_done, MC * e + m - 1)
                    for k in range(KD):
                        last = three(up_ps[m % 2][:], [w[:, k, m * P:(m + 1) * P] for w in w1],
                                     [x[:, k, :] for x in xt], k == 0, k == KD - 1)
                    last.then_inc(up_done, 1)
                pe.wait_ge(down_free, e + 1)
                pe.wait_ge(w2_lo, e + 1)
                for m in range(MC):
                    pe.wait_ge(hlo_done, MC * e + m + 1)
                    for s in range(SC):
                        last = three(down_ps[s][:, 0:D], [x[:, m, s * P:(s + 1) * P] for x in h],
                                     [w[:, m, :] for w in w2], m == 0, m == MC - 1)
                    if m == 3 and more:
                        transposes(e + 1)
                last.then_inc(down_done, 1)

            transposes(0)
            with pe.Fori(0, E - 1) as e:
                body(e, True)
            body(E - 1, False)

        @block.vector
        def _(dve):
            V = nc.vector

            def normalise(e):
                dve.wait_ge(gathered, 16 * SC * e + 16 * SC)
                V.tensor_copy(weight_next[:], xg[:, :, bass.ds(D + e, 1)].squeeze(2)).then_inc(weight_done, 1)
                for s in range(SC):
                    V.bn_stats(stats[:, s, :], xg[:, s, 0:D]).then_inc(stats_done, 1)
                for s in range(SC):
                    dve.wait_ge(stats_done, SC * e + s + 1)
                    dve.sem_inc(passed_dve, 1)
                    V.bn_aggr(mv[:, s, :], stats[:, s, :]).then_inc(aggr_done, 1)
                dve.wait_ge(aggr_done, SC * e + SC)
                V.tensor_scalar(ve[:], mv[:, :, 1], 1e-5, None, ALU.add).then_inc(ve_done, 1)
                dve.wait_ge(rstd_done, e + 1)
                for s in range(SC):
                    ins = V.tensor_scalar(xn[:, s, :], xg[:, s, 0:D], mv[:, s, 0:1], rstd[:, s:s + 1],
                                          ALU.subtract, ALU.mult)
                ins.then_inc(xn_done, 1)

            def modulate(e):
                dve.wait_ge(tp_done, e + 1)
                gain, offset = COL_AT["L3_cond_mlp_g"], COL_AT["L3_cond_mlp_b"]
                for k in range(KD):
                    ins = V.tensor_scalar(xm[:, k, :], tp_ps[k][:], g["cols"][:, gain + k:gain + k + 1],
                                          g["cols"][:, offset + k:offset + k + 1], ALU.mult, ALU.add)
                ins.then_inc(xm_done, 1)
                dve.wait_ge(xhi_done, e + 1)
                V.tensor_tensor(xt[1][:], xm[:], xt[0][:].bitcast(F32), ALU.subtract).then_inc(xlo_done, 1)

            def low(e, hi_done, dst, src, done):
                dve.wait_ge(hi_done, e + 1)
                V.tensor_tensor(dst[1][:], src[:], dst[0][:].bitcast(F32), ALU.subtract).then_inc(done, 1)

            def weights_now(e):
                dve.wait_ge(weight_done, e + 1)
                V.tensor_copy(weight[:], weight_next[:]).then_inc(weight_now, 1)

            def body(e, more):
                for m in range(MC):
                    dve.wait_ge(hhi_done, MC * e + m + 1)
                    V.tensor_tensor(h[1][:, m, :], h32[:, m % 2, :], h[0][:, m, :].bitcast(F32), ALU.subtract)\
                        .then_inc(hlo_done, 1)
                    if m == 3 and more:
                        normalise(e + 1)
                if more:
                    low(e + 1, w1_hi, w1, stage1, w1_lo)
                    modulate(e + 1)
                dve.wait_ge(down_done, e + 1)
                dve.wait_ge(b2_in, 16 * e + 16)
                for s in range(SC):
                    ins = V.tensor_tensor(y[:, s, :], down_ps[s][:, 0:D], b2[:], ALU.add)
                ins.then_inc(down_free, 1)
                dve.wait_ge(down_free, e + 2)
                dve.wait_ge(weight_now, e + 1)
                dve.wait_ge(y2_free, e + 1)
                for s in range(SC):
                    ins = V.tensor_scalar(y2[:, s, :], y[:, s, :], weight[:, s:s + 1], None, ALU.mult)
                ins.then_inc(y_done, 1)
                if more:
                    dve.wait_ge(y_done, e + 1)
                    weights_now(e + 1)
                    low(e + 1, w2_hi, w2, stage2, w2_lo)

            dve.sem_inc(down_free, 1)
            normalise(0)
            low(0, w1_hi, w1, stage1, w1_lo)
            modulate(0)
            weights_now(0)
            low(0, w2_hi, w2, stage2, w2_lo)
            with dve.Fori(0, E - 1) as e:
                body(e, True)
            body(E - 1, False)


def program(nc, t, out, stop=None):
    with ExitStack() as ctx:
        sb = lambda n, s, d=F32: ctx.enter_context(nc.sbuf_tensor(n, s, d))
        sem = lambda n: ctx.enter_context(nc.semaphore(n))
        g = {"x": sb("x_sb", [P, TILES, D]), "cols": sb("cols_sb", [P, NCOL]), "mod": sb("mod_sb", [P, NMOD, B + 2]),
             "ident": sb("ident_sb", [P, P]), "ones": sb("ones", [P, P]), "ones_r": sb("ones_r", [P, P], F32R),
             "hmask": sb("hmask_sb", [P, 10]), "neg_eye": sb("neg_eye_sb", [4, 4]),
             "head_sel": sb("head_sel_sb", [P, 63]), "pair_sel": sb("pair_sel_sb", [P, 62]), "mhalf": sb("mhalf", [P, 8]),
             "idx": sb("idx_sb", [P, E, SC], U32)}
        x_in, set_up = sem("x_in"), sem("set_up")

        with nc.Block() as block:
            @block.sync
            def _(sp):
                sp.dma_start(g["x"][:], t["x"].rearrange("b (t p) d -> p (b t) d", p=P)).then_inc(x_in, 16)
                for name in ("ident", "hmask", "neg_eye", "head_sel", "pair_sel"):
                    sp.dma_start(g[name][:], t[name]).then_inc(x_in, 16)
                sp.wait_ge(x_in, 16 * 6)

            @block.gpsimd
            def _(pool):
                nc.gpsimd.memset(g["ones"][:], 1.0).then_inc(set_up, 1)
                nc.gpsimd.memset(g["ones_r"][:].bitcast(F32), 1.0).then_inc(set_up, 1)
                nc.gpsimd.memset(g["mhalf"][:], -0.5).then_inc(set_up, 1)
                pool.wait_ge(set_up, 3)

        conditioning(nc, t, g)
        phases = [("L0a", lambda: attention(nc, t, g, Attention("L0a", 16, 64, 64 ** -0.5, True, "layer", 1e-5))),
                  ("L0m", lambda: mlp(nc, t, g, "L0m", "layer", 1e-5)),
                  ("L1a", lambda: attention(nc, t, g, Attention("L1a", 1, 256, 256 ** -0.5, False, "rms", 1e-6))),
                  ("L1m", lambda: mlp(nc, t, g, "L1m", "rms", 1e-6)),
                  ("L2a", lambda: attention(nc, t, g, Attention("L2a", 16, 16, 16 ** -0.5, True, None, 1e-5))),
                  ("L2m", lambda: mlp(nc, t, g, "L2m", None, 1e-5)),
                  ("L3a", lambda: attention(nc, t, g, Attention("L3a", 16, 64, 64 ** -0.5, False, "layer", 1e-5)))]
        for name, phase in phases:
            phase()
            if stop == name:
                with nc.Block() as block:
                    @block.sync
                    def _(sp):
                        sp.dma_start(out.rearrange("b (t p) d -> p (b t) d", p=P), g["x"][:]).then_inc(x_in, 16)
                        sp.wait_ge(x_in, 16 * 7)
                return
        route(nc, t, g, out)
        experts(nc, t, g, out)


def _laid_out(np, inputs):
    f = lambda a: np.ascontiguousarray(a)
    i = {k: np.asarray(v) for k, v in inputs.items()}
    h = {"x": i["x"], "c_t": f(i["cond_1024"].T), "mask": f(i["mask_BxS_bk0"]).view(np.int32),
         "mask_t": f(i["mask_BxS_bk0"].T).view(np.int32)}
    for n in ("q", "k"):
        for p in ("g", "b"):
            i[f"{n}n_{p}2"] = np.concatenate([i[f"L3_cond_{n}n_{p}"]] * 2)
    h["cols"] = f(np.concatenate([i[n].reshape(k, P).T for n, k in COL_VECS], axis=1))
    h["rows"] = f(np.concatenate([i[n].reshape(-1) for n, _ in ROW_VECS]))
    for n in ("L0_cond_W_mod", "L1_cond_film1_w", "L1_cond_film2_w", "L2_cond_ada1_w", "L2_cond_ada2_w",
              "L1_cond_proj_b", "L1_cond_mlp_b2", "L2_cond_proj_b", "L2_cond_fc2_b"):
        h[n] = i[n]
    h["W_ada_t"] = f(i["L3_cond_W_ada"].T)
    w = i["L0_cond_W_qkv"]
    h["L0a_wq"], h["L0a_wk"], h["L0a_wv"], h["L0a_wo"] = f(w[:, 0:1024]), f(w[:, 1024:2048]), f(w[:, 2048:3072]), i["L0_cond_W_out"]
    h["L1a_wq"], h["L1a_wk"], h["L1a_wv"], h["L1a_wo"] = (i[f"L1_cond_{n}_w"] for n in ("q", "k", "v", "proj"))
    w = i["L2_cond_qkv_w"]
    h["L2a_wq"], h["L2a_wk"] = f(w[:, 0:256]), f(w[:, 256:512])
    wv = np.zeros((256, 16, 32), np.float32)
    wv[:, :, 0:16] = w[:, 512:768].reshape(256, 16, 16)
    h["L2a_wv"] = wv.reshape(256, 512)
    wo = np.zeros((16, 32, 256), np.float32)
    wo[:, 0:16, :] = i["L2_cond_proj_w"].reshape(16, 16, 256)
    h["L2a_wo"] = wo.reshape(512, 256)
    w = f(i["L3_cond_Wqkv"].T)
    h["L3a_wq"], h["L3a_wk"], h["L3a_wv"] = f(w[:, 0:1024]), f(w[:, 1024:2048]), f(w[:, 2048:3072])
    h["L3a_wo"] = f(i["L3_cond_Wout"].T)
    h["L0m_w1"], h["L0m_w2"] = i["L0_cond_W1"], i["L0_cond_W2"]
    h["L1m_w1"], h["L1m_w2"] = i["L1_cond_mlp_w1"], i["L1_cond_mlp_w2"]
    h["L2m_w1"], h["L2m_w2"] = i["L2_cond_fc1_w"], i["L2_cond_fc2_w"]
    h["wg_t"] = f(i["L3_cond_Wgate"].T)
    h["moe_w1"], h["moe_w2"] = f(i["L3_cond_fc1s"].transpose(0, 2, 1)), f(i["L3_cond_fc2s"].transpose(0, 2, 1))
    h["L3_cond_b2s"] = i["L3_cond_b2s"]
    h["tri"] = np.triu(np.ones((P, P), np.float32), 1)
    h["iota"] = np.tile(np.arange(P, dtype=np.float32), (P, 1))
    h["tval"] = np.tile(np.arange(TILES, dtype=np.float32), (P, 1))
    h["pval"] = np.arange(P, dtype=np.float32)[:, None].copy()
    h["ident"] = np.eye(P, dtype=np.float32)
    hm = np.zeros((P, 10), np.float32)
    hm[0:64, 0] = hm[64:128, 1] = 1.0
    for m in range(8):
        hm[16 * m:16 * m + 16, 2 + m] = 1.0
    h["hmask"] = hm
    h["neg_eye"] = -np.eye(4, dtype=np.float32)
    sel = np.zeros((P, 63), np.float32)
    sel[:, 31] = 1.0
    h["head_sel"] = sel
    sel = np.zeros((P, 62), np.float32)
    sel[0:64, 30] = sel[64:128, 31] = 1.0
    h["pair_sel"] = sel
    for n, heads, width in (("L0a", 16, 64), ("L1a", 1, 256), ("L2a", 16, 32), ("L3a", 16, 64)):
        wide = np.zeros((P, heads * width), np.float32)
        wide[0:heads] = np.kron(np.eye(heads, dtype=np.float32), np.ones((1, width), np.float32))
        h["spread_" + n] = wide
    return h


def kernel(**inputs):
    import concourse.bacc as bacc
    from concourse.bass_utils import run_bass_kernel_spmd

    nc = bacc.Bacc("TRN2", target_bir_lowering=False, num_devices=1)
    arrays = _laid_out(np, inputs)
    t = {n: nc.dram_tensor(f"in_{n}", v.shape, mybir.dt.from_np(v.dtype), kind="ExternalInput").ap()
         for n, v in arrays.items()}
    t["gate_rows"] = nc.dram_tensor("gate_rows", (NGATE, B, D), F32, kind="Internal").ap()
    t["token_rows"] = nc.dram_tensor("token_rows", (B * N, ROW), F32, kind="Internal").ap()
    out = nc.dram_tensor("out_x", (B, N, D), F32, kind="ExternalOutput").ap()
    program(nc, t, out)
    r = run_bass_kernel_spmd(nc, [{f"in_{n}": v for n, v in arrays.items()}], core_ids=[0])
    return r.results[0]["out_x"]
```

```python
import math
from contextlib import ExitStack, contextmanager

import numpy as np
import concourse.bass as bass
from concourse import mybir

F32 = mybir.dt.float32
F32R = mybir.dt.float32r
U8 = mybir.dt.uint8
U32 = mybir.dt.uint32
I32 = mybir.dt.int32
ALU = mybir.AluOpType
ACT = mybir.ActivationFunctionType
AX = mybir.AxisListType

P = 128
B, N, D = 16, 256, 256
TT = N // P
KD = D // P
TILES = B * TT
MLP = 1024
MC = MLP // P
E = 8
CAP = B * N // E
SC = CAP // P

COL_VECS = [("L0_cond_b_mod", 12), ("L0_cond_b1", 8),
            ("L1_cond_norm1_w", 2), ("L1_cond_film1_b", 4), ("L1_cond_q_b", 2), ("L1_cond_k_b", 2),
            ("L1_cond_v_b", 2), ("L1_cond_norm2_w", 2), ("L1_cond_film2_b", 4), ("L1_cond_mlp_b1", 8),
            ("L2_cond_fc1_b", 8), ("L2_cond_ada1_b", 2),
            ("L3_cond_b_ada", 2), ("L3_cond_ln1_g", 2), ("L3_cond_ln1_b", 2),
            ("qn_g2", 1), ("qn_b2", 1), ("kn_g2", 1), ("kn_b2", 1),
            ("L3_cond_mlp_g", 2), ("L3_cond_mlp_b", 2), ("L3_cond_b1s", 64)]
COL_AT = {}
for _name, _n in COL_VECS:
    COL_AT[_name] = sum(n for _, n in COL_VECS[:len(COL_AT)])
NCOL = sum(n for _, n in COL_VECS)
ROW_VECS = [("L0_cond_b_mod", 1536), ("L0_cond_b_out", 256), ("L0_cond_b2", 256), ("L2_cond_ada2_b", 1536)]
ROW_AT = {"L0_cond_b_mod": 0, "L0_cond_b_out": 1536, "L0_cond_b2": 1792, "L2_cond_ada2_b": 2048}
NROW = 3584

MOD_AT = {"L0a": 0, "L0m": 4, "L1a": 8, "L1m": 12, "L3a": 16}
NMOD = 20
GATE_AT = {"L0a": 0, "L0m": 2, "L2a": 4, "L2m": 6}
NGATE = 8


@contextmanager
def semaphores(nc, prefix):
    with ExitStack() as ctx:
        made = []

        def sem(name):
            made.append(ctx.enter_context(nc.semaphore(f"{prefix}_{name}")))
            return made[-1]

        yield sem
        with nc.Block() as block:
            @block.gpsimd
            def _(pool):
                for s in made:
                    pool.sem_clear(s)


def conditioning(nc, t, g):
    with semaphores(nc, "c") as sem, ExitStack() as ctx:
        sb = lambda n, s, d=F32: ctx.enter_context(nc.sbuf_tensor(n, s, d))
        ps = [ctx.enter_context(nc.psum_tensor(f"c_ps{i}", [P, 512], F32)) for i in range(4)]
        c_t = sb("c_t", [P, KD, B])
        silu_c = sb("c_silu", [P, KD, B])
        h1 = sb("c_h1", [P, KD, B])
        w_mod = sb("c_wmod", [P, KD, 1536])
        film = [sb(f"c_film{j}", [P, KD, 512]) for j in range(2)]
        ada1 = sb("c_ada1", [P, KD, 256])
        ada2 = sb("c_ada2", [P, KD, 1536])
        w_ada = sb("c_wada", [P, KD, 256])
        rows_b = sb("c_rows", [B, NROW])
        raw = sb("c_raw", [B, 2048])
        gates = sb("c_gates", [B, NGATE, D])
        colraw = sb("c_colraw", [P, 18, B])
        loaded, silu_done, mm_done, h1_done, v, stored, memz = (sem(f"s{i}") for i in range(7))
        chained, x_in = sem("chained"), sem("x_in")
        block = ctx.enter_context(nc.Block())
        chunked = lambda w: w.rearrange("(k p) n -> p k n", p=P)

        @block.sync
        def _(sp):
            sp.dma_start(c_t[:], chunked(t["c_t"])).then_inc(loaded, 16)
            sp.dma_start(g["cols"][:], t["cols"]).then_inc(loaded, 16)
            sp.dma_start(rows_b[:], t["rows"].partition_broadcast(B)).then_inc(loaded, 16)
            for dst, name in ((w_mod, "L0_cond_W_mod"), (film[0], "L1_cond_film1_w"),
                              (film[1], "L1_cond_film2_w"), (ada1, "L2_cond_ada1_w"),
                              (ada2, "L2_cond_ada2_w"), (w_ada, "W_ada_t")):
                sp.dma_start(dst[:], chunked(t[name])).then_inc(loaded, 16)
            sp.dma_start(g["x"][:], t["x"].rearrange("b (t p) d -> p (b t) d", p=P)).then_inc(x_in, 16)
            sp.wait_ge(v, 1)
            sp.dma_start(t["gate_rows"].rearrange("g b d -> b g d"), gates[:]).then_inc(stored, 16)
            sp.wait_ge(stored, 16)
            sp.wait_ge(x_in, 16)

        @block.scalar
        def _(act):
            act.wait_ge(loaded, 16 * 9)
            nc.scalar.activation(silu_c[:], c_t[:], ACT.Silu).then_inc(silu_done, 1)
            act.wait_ge(mm_done, 2)
            for k in range(KD):
                nc.scalar.activation(h1[:, k, :], ps[2][:, k * B:(k + 1) * B], ACT.Silu,
                                     bias=g["cols"][:, COL_AT["L2_cond_ada1_b"] + k:COL_AT["L2_cond_ada1_b"] + k + 1]).then_inc(h1_done, 1)

        @block.tensor
        def _(pe):
            def columns(bank, j, w, col, x):
                for k in range(KD):
                    last = nc.tensor.matmul(bank[:, j * B:(j + 1) * B], w[:, k, col * P:(col + 1) * P],
                                            x[:, k, :], start=(k == 0), stop=(k == KD - 1))
                return last

            def row(bank, w, c0, n, x):
                for k in range(KD):
                    last = nc.tensor.matmul(bank[0:B, 0:n], x[:, k, :], w[:, k, c0:c0 + n],
                                            start=(k == 0), stop=(k == KD - 1))
                return last

            pe.wait_ge(silu_done, 1)
            for j, col in enumerate((0, 1, 2, 3, 6, 7, 8, 9)):
                columns(ps[0], j, w_mod, col, silu_c)
            for j in range(4):
                columns(ps[0], 8 + j, film[0], j, c_t)
            for j in range(4):
                columns(ps[0], 12 + j, film[1], j, c_t)
            for j in range(2):
                columns(ps[0], 16 + j, w_ada, j, silu_c)
            row(ps[1], w_mod, 512, 256, silu_c)
            for k in range(KD):
                last = nc.tensor.matmul(ps[1][0:B, 256:512], silu_c[:, k, :], w_mod[:, k, 1280:1536],
                                        start=(k == 0), stop=(k == KD - 1))
            last.then_inc(mm_done, 1)
            for j in range(2):
                last = columns(ps[2], j, ada1, j, c_t)
            last.then_inc(mm_done, 1)
            pe.wait_ge(h1_done, 2)
            pe.wait_ge(memz, 1)
            for n, bank in enumerate((ps[1], ps[2], ps[3])):
                last = row(bank, ada2, 512 * n, 512, h1)
            last.then_inc(mm_done, 1)

        @block.vector
        def _(dve):
            mod, cols = g["mod"], g["cols"]
            done = [0]
            chain = chained

            def step(ins):
                done[0] += 1
                ins.then_inc(chain, 1)
                dve.wait_ge(chain, done[0])

            dve.wait_ge(loaded, 16 * 9)
            step(nc.vector.memset(mod[:], 0.0))
            dve.wait_ge(mm_done, 1)
            step(nc.vector.tensor_copy(colraw[:], ps[0][:, 0:18 * B].rearrange("p (j b) -> p j b", b=B)))
            nc.vector.tensor_copy(raw[:, 0:512], ps[1][0:B, :]).then_inc(memz, 1)
            dve.wait_ge(memz, 1)

            def biased(j, bias, plus=0.0):
                step(nc.vector.tensor_scalar(colraw[:, j, :], colraw[:, j, :], cols[:, bias:bias + 1], plus,
                                             ALU.add, ALU.add))

            bm = COL_AT["L0_cond_b_mod"]
            for j, col in enumerate((0, 1, 2, 3, 6, 7, 8, 9)):
                biased(j, bm + col, 1.0 if j in (2, 3, 6, 7) else 0.0)
            for part, base in ((0, 8), (1, 12)):
                fb = COL_AT[f"L1_cond_film{part + 1}_b"]
                for j in range(4):
                    biased(base + j, fb + j, 1.0 if j < 2 else 0.0)
            for j in range(2):
                biased(16 + j, COL_AT["L3_cond_b_ada"] + j)
            for k in range(KD):
                for name, shift, scale in (("L0a", 0, 2), ("L0m", 4, 6), ("L1a", 10, 8), ("L1m", 14, 12)):
                    at = MOD_AT[name]
                    if name[1] == "0":
                        step(nc.vector.tensor_copy(mod[:, at + k, 0:B], colraw[:, scale + k, :]))
                    else:
                        nw = COL_AT["L1_cond_norm1_w" if name == "L1a" else "L1_cond_norm2_w"] + k
                        step(nc.vector.tensor_scalar(mod[:, at + k, 0:B], colraw[:, scale + k, :],
                                                     cols[:, nw:nw + 1], None, ALU.mult))
                    step(nc.vector.tensor_copy(mod[:, at + 2 + k, 0:B], colraw[:, shift + k, :]))
                at = MOD_AT["L3a"]
                gcol, bcol = COL_AT["L3_cond_ln1_g"] + k, COL_AT["L3_cond_ln1_b"] + k
                step(nc.vector.tensor_scalar(mod[:, at + k, 0:B], mod[:, at + k, 0:B],
                                             cols[:, gcol:gcol + 1], None, ALU.add))
                step(nc.vector.tensor_scalar(mod[:, at + 2 + k, 0:B], colraw[:, 16 + k, :],
                                             cols[:, bcol:bcol + 1], None, ALU.add))
            for half, name, bias in ((0, "L0a", "L0_cond_b_out"), (1, "L0m", "L0_cond_b2")):
                r = 512 if half == 0 else 1280
                at = GATE_AT[name]
                step(nc.vector.tensor_tensor(gates[:, at, :], raw[:, 256 * half:256 * half + 256],
                                             rows_b[:, r:r + 256], ALU.add))
                step(nc.vector.tensor_tensor(gates[:, at + 1, :], gates[:, at, :],
                                             rows_b[:, ROW_AT[bias]:ROW_AT[bias] + 256], ALU.mult))
            dve.wait_ge(mm_done, 3)
            ab = ROW_AT["L2_cond_ada2_b"]
            for n in range(3):
                step(nc.vector.tensor_tensor(raw[:, 512 + 512 * n:1024 + 512 * n], ps[n + 1][0:B, :],
                                             rows_b[:, ab + 512 * n:ab + 512 * n + 512], ALU.add))
            for half, name in ((0, "L2a"), (1, "L2m")):
                o = 512 + 768 * half
                at = GATE_AT[name]
                step(nc.vector.scalar_tensor_tensor(gates[:, at, :], raw[:, o + 256:o + 512], 1.0,
                                                    raw[:, o + 512:o + 768], ALU.add, ALU.mult))
                step(nc.vector.tensor_tensor(gates[:, at + 1, :], raw[:, o:o + 256],
                                             raw[:, o + 512:o + 768], ALU.mult))
            nc.vector.engine_nop().then_inc(v, 1)


def split_weights(nc, engines, stage, sems, pieces, centre=None):
    sp, act, dve = engines
    landed, hi_done, lo_done = sems
    flat = lambda ap: ap if len(ap.shape) == 2 else ap.rearrange("p c n -> p (c n)")
    like = lambda ap, hi: ap if len(hi.shape) == 2 else ap.rearrange("p (c n) -> p c n", n=hi.shape[2])

    def sync_share():
        for n, (src, hi, lo, c) in enumerate(pieces):
            if n >= 2:
                sp.wait_ge(lo_done, n - 1)
            w = flat(hi).shape[-1]
            sp.dma_start(like(stage[:, n % 2, 0:w], hi), src).then_inc(landed[n % 2], 16)

    def scalar_share():
        for n, (src, hi, lo, c) in enumerate(pieces):
            w = flat(hi).shape[-1]
            if c:
                act.wait_ge(centre[1], 2 * sum(x[3] for x in pieces[:n]) + 2)
            act.wait_ge(landed[n % 2], 16 * (n // 2 + 1))
            nc.scalar.activation(flat(hi), stage[:, n % 2, 0:w], ACT.Copy).then_inc(hi_done, 1)

    def vector_share():
        seen = 0
        for n, (src, hi, lo, c) in enumerate(pieces):
            w = flat(hi).shape[-1]
            if c:
                means, steps = centre
                dve.wait_ge(landed[n % 2], 16 * (n // 2 + 1))
                heads = stage[:, n % 2, 0:w].rearrange("p (h d) -> p h d", d=64)
                if seen:
                    dve.wait_ge(steps, 2 * seen)
                nc.vector.tensor_reduce(means[:], heads, AX.X, ALU.add).then_inc(steps, 1)
                dve.wait_ge(steps, 2 * seen + 1)
                mb = means[:].unsqueeze(2).to_broadcast([P, w // 64, 64])
                nc.vector.scalar_tensor_tensor(heads, mb, -1.0 / 64, heads, ALU.mult, ALU.add).then_inc(steps, 1)
                seen += 1
            dve.wait_ge(hi_done, n + 1)
            if lo is None:
                dve.sem_inc(lo_done, 1)
                continue
            nc.vector.tensor_tensor(flat(lo), stage[:, n % 2, 0:w], flat(hi).bitcast(F32), ALU.subtract).then_inc(lo_done, 1)

    return sync_share, scalar_share, vector_share


class Attention:

    def __init__(self, name, heads, d, scale, gated, norm, eps):
        self.name, self.heads, self.d, self.scale = name, heads, d, scale
        self.gated, self.norm, self.eps = gated, norm, eps
        self.chunks = heads * d // P
        self.one = heads == 1
        self.units = 1 if self.one else heads // 2
        self.vd = max(d, 32) if not self.one else d
        self.vw = heads * self.vd
        self.oc = heads * self.vd // P
        self.vpiece = min(512, self.vw)
        self.vpieces = TT * self.vw // self.vpiece
        self.upc = 2 if self.vd == 32 else 1
        self.groups = self.units // self.upc
        self.hn = 2 if not self.one else 1
        self.per_chunk = P // d if d < P else 1
        self.pieces = self.oc // 2
        self.qknorm = name == "L3a"
        turns = [("qk", c) for c in range(self.chunks)] + [("v", n) for n in range(self.vpieces)]
        if self.qknorm:
            turns += [("norm", 0), ("norm", 1)]
        self.ln_step = min(6, self.units)
        for step in range(self.units + 1):
            if step == self.ln_step:
                turns.append(("ln", 0))
            if self.qknorm and step + 2 < self.units:
                turns.append(("norm", step + 2))
        if len(turns) % 2:
            turns.append(("spare", 0))
        self.turns = turns


def o_row(a, u, h):
    return 64 * h if a.d == 64 else 64 * (u % 2) + 32 * h


def o_rows(a, u):
    return slice(64 * (u % 2), 64 * (u % 2) + 64) if a.vd == 32 else slice(0, P)


class Residual:

    def __init__(self, nc, dve, nm, n, s, bufs, g, eps):
        self.nc, self.dve, self.nm, self.n, self.s, self.bufs, self.g, self.eps = nc, dve, nm, n, s, bufs, g, eps

    def take(self, i, outs, gate, ready):
        nc, dve, s, (y, y2, stats, mv, ve, rstd, y_bias) = self.nc, self.dve, self.s, self.bufs
        dve.wait_ge(*ready)
        if self.nm[:2] in ("L0", "L2"):
            for t0, k, view in outs:
                if self.nm[:2] == "L2":
                    other = y_bias[:].unsqueeze(1).to_broadcast([P, k, D])
                else:
                    other = gate(t0, k)
                ins = nc.vector.tensor_tensor(y[:, t0:t0 + k, :], view, other, ALU.add if self.nm[:2] == "L2" else ALU.mult)
                ins.then_inc(s["taken"], 1)
            dve.wait_ge(s["taken"], len(outs) * (i + 1))
            return
        dve.wait_ge(s["xh"], i + 1) if self.nm[:2] == "L1" else None
        for t0, k, view in outs:
            tile = self.g["x"][:, bass.ds(i * self.n + t0, k), :]
            nc.vector.tensor_tensor(tile, view, tile, ALU.add).then_inc(s["taken"], 1)
        dve.wait_ge(s["taken"], len(outs) * (i + 1))

    def moments(self, i):
        nc, dve, s, n, (y, y2, stats, mv, ve, rstd, y_bias) = self.nc, self.dve, self.s, self.n, self.bufs
        if self.nm[:2] != "L2":
            return
        for j in range(n):
            nc.vector.bn_stats(stats[:, j, :], y[:, j, :]).then_inc(s["step"], 1)
        dve.wait_ge(s["step"], (2 * n + 2) * i + n)
        dve.sem_inc(s["passed"], 1)
        for j in range(n):
            nc.vector.bn_aggr(mv[:, j, :], stats[:, j, :]).then_inc(s["step"], 1)
        dve.wait_ge(s["step"], (2 * n + 2) * i + 2 * n)
        nc.vector.tensor_scalar(ve[:, 0:n], mv[:, 0:n, 1], self.eps, None, ALU.add).then_inc(s["ve2"], 1)

    def add(self, i, gate):
        nc, dve, s, n, (y, y2, stats, mv, ve, rstd, y_bias) = self.nc, self.dve, self.s, self.n, self.bufs
        if self.nm[:2] in ("L1", "L3"):
            return
        if self.nm[:2] == "L2":
            dve.wait_ge(s["rstd2"], i + 1)
            for j in range(n):
                ins = nc.vector.tensor_scalar(y2[:, j, :], y[:, j, :], mv[:, j, 0:1], rstd[:, j:j + 1],
                                              ALU.subtract, ALU.mult)
            ins.then_inc(s["step"], 1)
            dve.wait_ge(s["step"], (2 * n + 2) * i + 2 * n + 1)
            shaped = lambda v: v.rearrange("p (b t) d -> p b t d", t=TT)
            nc.vector.tensor_tensor(shaped(y[:, 0:n, :]), shaped(y2[:, 0:n, :]), gate, ALU.mult).then_inc(s["step"], 1)
            dve.wait_ge(s["step"], (2 * n + 2) * i + 2 * n + 2)
        dve.wait_ge(s["xh"], i + 1)
        tiles = self.g["x"][:, bass.ds(i * n, n), :]
        nc.vector.tensor_tensor(tiles, y[:, 0:n, :], tiles, ALU.add).then_inc(s["done"], 1)


def attention(nc, t, g, a):
    qknorm, masked = a.qknorm, a.name == "L2a"
    nm, C, U, HN, OC = a.name, a.chunks, a.units, a.hn, a.oc
    NR = len(a.turns)
    AT = {turn: n for n, turn in enumerate(a.turns)}
    bank_of = lambda *turn: ring[AT[turn] % 2]
    NB = 3
    KR = 4 if qknorm else C
    COPY = a.turns[1] if C == 8 else a.turns[0]
    FOLD, HIGH, LOW = a.turns[3:6] if C == 8 else a.turns[1:4]
    OVER = {a.turns[6 + n]: [n] for n in range(a.pieces)} if C == 8 else {}
    LATE = [] if C == 8 else range(a.pieces)
    MASK0 = 0 if a.d == 64 else 2
    LN_STEP = a.ln_step
    cols = g["cols"]
    with semaphores(nc, nm) as sem, ExitStack() as ctx:
        sb = lambda n, s, d=F32: ctx.enter_context(nc.sbuf_tensor(f"{nm}_{n}", s, d))
        pb = lambda n: ctx.enter_context(nc.psum_tensor(f"{nm}_{n}", [P, 512], F32))
        ring = [pb("ring0"), pb("ring1")]
        s_ps = [pb("s0"), pb("s1")]
        st_ps = [pb("st0"), pb("st1")]
        o_ps, sum_ps = pb("o"), pb("sum")

        QW = a.heads * a.d
        wq = [sb(f"wq{j}", [P, KD, QW], F32R) for j in range(2)]
        wk = [sb(f"wk{j}", [P, KD, QW], F32R) for j in range(2)]
        wv = [sb(f"wv{j}", [P, KD, a.vw], F32R) for j in range(2)]
        wo = [sb(f"wo{j}", [P, OC, D], F32R) for j in range(2)]
        means = sb("means", [P, 16])
        xt = [sb(f"xt{j}", [P, KD, N], F32R) for j in range(2)]
        stats = sb("stats", [P, TT, 6])
        mv = sb("mv", [P, TT, 2])
        ve = sb("ve", [P, TT])
        rstd = sb("rstd", [P, TT])
        q32 = None if qknorm else sb("q32", [P, C, N])
        k_hi = sb("k_hi", [P, KR, N], F32R)
        k_lo = sb("k_lo", [P, KR, N], F32R)
        v = sb("v", [P, TT, a.vw])
        q_hi = sb("q_hi", [P, NB, 512], F32R)
        q_lo = sb("q_lo", [P, NB, 512], F32R)
        mx = sb("mx", [P, 4])
        shift = sb("shift", [P, 2, 512], F32R)
        prob = sb("prob", [P, 2, TT, 512])
        stage = prob[:].rearrange("p s t n -> p s (t n)")
        sums = sb("sums", [P, N])
        rsum = sb("rsum", [a.heads, N])
        rsum_hi, rsum_lo = sb("rsum_hi", [P, N], F32R), sb("rsum_lo", [P, N], F32R)
        spread = sb("spread", [P, OC * P], F32R)
        o_raw = sb("o_raw", [P, OC, N])
        o32 = sb("o32", [P, 2, 2 * N])
        y, y2 = (o32[:, j, :].rearrange("p (t d) -> p t d", d=D) for j in range(2))
        xm, xn = o32[:, 0, :].rearrange("p (k n) -> p k n", n=N), y2
        o_hi = sb("o_hi", [P, OC, N], F32R)
        o_lo = sb("o_lo", [P, OC, N], F32R)
        gate = y_bias = None
        if not qknorm:
            gate = sb("gate", [P, 2, D])
        if masked:
            y_bias = sb("y_bias", [P, D])
        if qknorm:
            raw = sb("raw", [P, C, 512])
            sq = sb("sq", [P, 512])
            rq_hi, rq_lo = sb("rq_hi", [P, 512], F32R), sb("rq_lo", [P, 512], F32R)
            qn = sb("qn", [P, 512])
            lnv, rstdq = qn[0:a.heads, :], sq[0:a.heads, :]
            eps_col = sb("eps_col", [P, 1])
        rstd2, ve2 = sb("rstd2", [P, TT]), sb("ve2", [P, TT])
        if masked:
            mask_u8 = sb("mask_u8", [P, TT, B], U8)
            kbias = sb("kbias", [P, TT])
            key_bias = sb("key_bias", [P, TT, B])
            mrow_u8 = sb("mrow_u8", [P, 2, B, N], U8)
            mrow = sb("mrow", [P, 512], F32R)

        landed = [sem("landed0"), sem("landed1")]
        hi_done, lo_done, centred = sem("hi_done"), sem("lo_done"), sem("centred")
        pre, consts = sem("pre"), sem("consts")
        stats_done, aggr_done, ve_done, rstd_done, xn_done = (sem(x) for x in ("stats", "aggr", "ve", "rstd", "xn"))
        xm_done, xhi_done, xlo_done = sem("xm"), sem("xhi"), sem("xlo")
        pe_first = sem("pe_first")
        turn_done, turn_free = sem("turn_done"), sem("turn_free")
        q32_done, khi_done = sem("q32"), sem("khi")
        qhi_done, qlo_done = sem("qhi"), sem("qlo")
        s_done, mx_done, shift_done = sem("s_done"), sem("mx"), sem("shift")
        st_done, p_done, pv_done = sem("st"), sem("p"), sem("pv")
        rsum_done, rsum_hi_done, rsum_lo_done = sem("rsum"), sem("rsum_hi"), sem("rsum_lo")
        o_done, on_done, ohi_done, olo_done = sem("o_raw"), sem("on"), sem("ohi"), sem("olo")
        klo_done, sums_done, fold_done, over_done = sem("klo"), sem("sums"), sem("fold"), sem("over")
        out_done, taken = sem("out"), sem("taken")
        gate_in, ep_done, xh_done, ep_step = sem("gate_in"), sem("ep"), sem("xh"), sem("ep_step")
        passed = sem("passed")
        raw_done, sq_done, var_done, ln_done, rq_done = (sem(x) for x in ("raw", "sq", "var", "lnv", "rq"))
        rqhi_done, rqlo_done, qn_done, kn_done = (sem(x) for x in ("rqhi", "rqlo", "qn", "kn"))
        ve2_done, rstd2_done, passed_dve = sem("ve2"), sem("rstd2"), sem("passed_dve")
        mask_in, mrow_done, kb_done = sem("mask_in"), sem("mrow"), sem("kb")

        q_of = lambda c: raw[:, c, 0:N] if qknorm else q32[:, c, :]

        pieces = []
        part = lambda w, k, c0, c1: w[k * P:(k + 1) * P, c0:c1]
        for w_dram, dst, width in ((t[nm + "_wq"], wq, QW), (t[nm + "_wk"], wk, QW), (t[nm + "_wv"], wv, a.vw)):
            for k in range(KD):
                centred_piece = qknorm and dst is not wv
                pieces.append((w_dram[k * P:(k + 1) * P, :], dst[0][:, k, :], dst[1][:, k, :], centred_piece))
        for c in range(0, OC, 4):
            n = min(4, OC)
            pieces.append((t[nm + "_wo"][c * P:(c + n) * P, :].rearrange("(c p) n -> p c n", p=P),
                           wo[0][:, c:c + n, :], wo[1][:, c:c + n, :], False))
        pieces.append((t["spread_" + nm], spread[:], None, False))
        NP_ = len(pieces)

        block = ctx.enter_context(nc.Block())
        loader = lambda sp=None, act=None, dve=None: split_weights(
            nc, (sp, act, dve), stage, (landed, hi_done, lo_done), pieces, (means, centred))

        @block.sync
        def _(sp):
            if masked:
                sp.dma_start(mask_u8[:], t["mask_t"].bitcast(U8).rearrange("(k p) b -> p k b", p=P)).then_inc(mask_in, 16)
                for h in range(2):
                    sp.dma_start(mrow_u8[0:1, h, :, :], t["mask"].bitcast(U8).partition_broadcast(1)).then_inc(mask_in, 16)
            loader(sp=sp)[0]()
            if a.gated:
                at = GATE_AT[nm]
                for j in range(2):
                    sp.dma_start(gate[:, j, :], t["gate_rows"][at + j, 0, :].partition_broadcast(P)).then_inc(gate_in, 16)
            elif nm == "L1a":
                sp.dma_start(gate[:, 0, :], t["L1_cond_proj_b"].partition_broadcast(P)).then_inc(gate_in, 16)
            if nm == "L2a":
                sp.dma_start(y_bias[:], t["L2_cond_proj_b"].partition_broadcast(P)).then_inc(gate_in, 16)
            if a.gated:
                with sp.Fori(0, B - 1) as i:
                    sp.wait_ge(ep_done, i + 1)
                    for j in range(2):
                        sp.dma_start(gate[:, j, :], t["gate_rows"][at + j, bass.ds(i + 1, 1), :].squeeze(0).partition_broadcast(P)).then_inc(gate_in, 16)

        @block.gpsimd
        def _(pool):
            def gated_wait(s, val):
                pool.wait_ge(s, val)
                pool.sem_inc(passed, 1)

            for rows in [rsum_hi, rsum_lo] + ([rq_hi, rq_lo] if qknorm else []) + ([mrow] if masked else []):
                nc.gpsimd.memset(rows[:].bitcast(F32), 0.0).then_inc(pre, 1)

            def token_rstd(i):
                gated_wait(ve_done, i + 1)
                nc.gpsimd.tensor_tensor(rstd[:], ve[:], g["mhalf"][:, 0:TT], ALU.pow).then_inc(rstd_done, 1)

            if a.norm:
                token_rstd(0)

            def tail(j):
                if a.gated or nm == "L1a":
                    gated_wait(gate_in, (32 * j + 32 + (16 if nm == "L2a" else 0)) if a.gated else 16)
                    gated_wait(xn_done, j + 1)
                    tiles, row = g["x"][:, bass.ds(j * TT, TT), :], gate[:, 1 if a.gated else 0, :]
                    nc.gpsimd.tensor_tensor(tiles, tiles, row.unsqueeze(1).to_broadcast([P, TT, D]), ALU.add).then_inc(xh_done, 1)
                if nm == "L2a":
                    gated_wait(ve2_done, j + 1)
                    nc.gpsimd.tensor_tensor(rstd2[:], ve2[:], g["mhalf"][:, 0:TT], ALU.pow).then_inc(rstd2_done, 1)

            def next_tokens(i):
                if a.norm:
                    token_rstd(i + 1)

            def gains(i):
                col = lambda n: cols[:, COL_AT[n]:COL_AT[n] + 1]
                for c in range(C):
                    gated_wait(qn_done, i * C + c + 1)
                    nc.gpsimd.tensor_scalar(raw[:, c, N:2 * N], qn[:, N:2 * N], col("kn_g2"), col("kn_b2"), ALU.mult, ALU.add)\
                        .then_inc(kn_done, 1)
                    nc.gpsimd.tensor_scalar(q_of(c), qn[:, 0:N], col("qn_g2"), col("qn_b2"), ALU.mult, ALU.add)\
                        .then_inc(q32_done, 1)
                    if c == a.ln_step - 2 and not final_batch(i):
                        next_tokens(i)

            final_batch = lambda i: isinstance(i, int) and i == B - 1
            if qknorm:
                gains(0)
                with pool.Fori(1, B - 1) as i:
                    gains(i)
                gains(B - 1)
            else:
                next_tokens(0)
                with pool.Fori(1, B - 1) as i:
                    if a.one:
                        next_tokens(i)
                    tail(i - 1)
                    if not a.one:
                        next_tokens(i)
                tail(B - 2)
                tail(B - 1)

        @block.scalar
        def _(act):
            def tail_rows(j):
                act.wait_ge(rsum_done, j + 1)
                nc.scalar.activation(rsum_hi[0:a.heads, :], rsum[:], ACT.Copy).then_inc(rsum_hi_done, 1)

            def x_hi(i):
                act.wait_ge(xm_done, i + 1)
                nc.scalar.activation(xt[0][:], xm[:], ACT.Copy).then_inc(xhi_done, 1)

            def over(j, n):
                act.wait_ge(on_done, j * a.pieces + n + 1)
                if a.one:
                    for c in range(2):
                        vb = COL_AT["L1_cond_v_b"] + c
                        ins = nc.scalar.activation(o_hi[:, c, :], o32[:, 0, c * N:(c + 1) * N], ACT.Identity, bias=cols[:, vb:vb + 1])
                else:
                    ins = nc.scalar.activation(o_hi[:, 2 * n:2 * n + 2, :].rearrange("p c n -> p (c n)"), o32[:, n % 2, :], ACT.Copy)
                ins.then_inc(ohi_done, 1)

            def body(i, first, final):
                for kind, c in a.turns:
                    if not first and (kind, c) == HIGH:
                        tail_rows(i - 1)
                    for n in OVER.get((kind, c), []):
                        if not first:
                            over(i - 1, n)
                    if kind != "qk":
                        continue
                    bank = bank_of("qk", c)
                    act.wait_ge(turn_done, i * NR + AT["qk", c] + 1)
                    if qknorm:
                        nc.scalar.activation(raw[:, c, :], bank[:], ACT.Copy).then_inc(raw_done, 1)
                        if c >= 1:
                            act.wait_ge(var_done, i * C + c)
                        nc.scalar.activation(sq[:], bank[:], ACT.Square).then_inc(sq_done, 1)
                    elif nm == "L1a":
                        qb, kb = COL_AT["L1_cond_q_b"] + c, COL_AT["L1_cond_k_b"] + c
                        nc.scalar.activation(q32[:, c, :], bank[:, 0:N], ACT.Identity, bias=cols[:, qb:qb + 1]).then_inc(q32_done, 1)
                        nc.scalar.activation(k_hi[:, c, :], bank[:, N:2 * N], ACT.Identity, bias=cols[:, kb:kb + 1]).then_inc(khi_done, 1)
                    else:
                        nc.scalar.activation(q32[:, c, :], bank[:, 0:N], ACT.Copy).then_inc(q32_done, 1)
                        nc.scalar.activation(k_hi[:, c, :], bank[:, N:2 * N], ACT.Copy).then_inc(khi_done, 1)
                if qknorm:
                    act.wait_ge(var_done, i * C + C)
                    nc.scalar.activation(lnv[:], st_ps[0][0:a.heads, :], ACT.Ln, bias=eps_col[0:a.heads, 0:1], scale=1.0 / a.d).then_inc(ln_done, 1)
                    act.wait_ge(ln_done, i + 1)
                    nc.scalar.activation(rstdq[:], lnv[:], ACT.Exp, scale=-0.5).then_inc(rq_done, 1)
                    act.wait_ge(rq_done, i + 1)
                    nc.scalar.activation(rq_hi[0:a.heads, :], rstdq[:], ACT.Copy).then_inc(rqhi_done, 1)

                def k_high(c):
                    act.wait_ge(kn_done, i * C + c + 1)
                    nc.scalar.activation(k_hi[:, c % KR, :], raw[:, c, N:2 * N], ACT.Copy).then_inc(khi_done, 1)

                def mask_q(u):
                    if a.one:
                        act.wait_ge(q32_done, i * C + C)
                        nc.scalar.activation(q_hi[:, 0, :], q32[:].rearrange("p c n -> p (c n)"), ACT.Copy).then_inc(qhi_done, 1)
                        return
                    c = 2 * u // a.per_chunk
                    act.wait_ge(q32_done, i * C + c + 1)
                    for h in range(2):
                        m = (2 * u + h) % a.per_chunk
                        ins = nc.scalar.activation(q_hi[:, u % NB, h * N:(h + 1) * N], q_of(c), ACT.Copy,
                                                   scale=g["hmask"][:, MASK0 + m:MASK0 + m + 1])
                    ins.then_inc(qhi_done, 1)

                def exp(u):
                    for kt in range(TT):
                        act.wait_ge(st_done, 2 * (i * U + u) + kt + 1)
                        if u >= 2 and kt == 0:
                            act.wait_ge(pv_done, i * U + u - 1)
                        bias = kbias[:, kt:kt + 1] if masked else 0.0
                        nc.scalar.activation(prob[:, u % 2, kt, 0:HN * N], st_ps[kt][:, 0:HN * N], ACT.Exp,
                                             scale=a.scale, bias=bias).then_inc(p_done, 1)

                if not qknorm:
                    mask_q(0)
                for n in LATE:
                    if not first:
                        over(i - 1, n)

                def outputs(u):
                    rows = o_rows(a, u)
                    act.wait_ge(pv_done, i * U + u + 1)
                    if a.one:
                        nc.scalar.activation(o_raw[:].rearrange("p c n -> p (c n)"), o_ps[:], ACT.Copy).then_inc(o_done, 1)
                    else:
                        nc.scalar.activation(o_raw[rows, u // a.upc, :], o_ps[rows, 0:N], ACT.Copy).then_inc(o_done, 1)

                if qknorm:
                    k_high(0)
                    mask_q(0)
                    k_high(1)
                for step in range(U + 3):
                    if step >= 3:
                        outputs(step - 3)
                    if step + 1 < U:
                        mask_q(step + 1)
                    if 1 <= step <= U:
                        exp(step - 1)
                    if qknorm and step + 2 < U:
                        k_high(step + 2)
                    if step == LN_STEP and not final:
                        x_hi(i + 1)

            x_hi(0)
            loader(act=act)[1]()
            if masked:
                act.wait_ge(kb_done, 1)
            body(0, True, False)
            with act.Fori(1, B - 1) as i:
                body(i, False, False)
            body(B - 1, False, True)
            tail_rows(B - 1)
            for n in range(a.pieces):
                over(B - 1, n)

        @block.tensor
        def _(pe):
            mm = nc.tensor.matmul

            def three(out, lhs, rhs, start, stop):
                mm(out, lhs[0], rhs[0], start=start, stop=False)
                mm(out, lhs[1], rhs[0], start=False, stop=False)
                return mm(out, lhs[0], rhs[1], start=False, stop=stop)

            def transposes(bank):
                for k in range(KD):
                    for tt in range(TT):
                        last = nc.tensor.transpose(bank[:, k * N + tt * P:k * N + (tt + 1) * P],
                                                   xn[:, tt, k * P:(k + 1) * P], g["ident"][:])
                return last

            pe.wait_ge(xn_done, 1)
            transposes(ring[0]).then_inc(pe_first, 1)
            pe.wait_ge(lo_done, 2 * KD)
            pe.wait_ge(pre, 2 + 2 * qknorm + masked)

            def variances(i, c):
                pe.wait_ge(sq_done, i * C + c + 1)
                mm(st_ps[0][0:32, :], g["pair_sel"][:, 30 - 2 * c:62 - 2 * c], sq[:], start=(c == 0), stop=(c == C - 1),
                   skip_group_check=True).then_inc(var_done, 1)

            def take(i, *turn):
                pe.wait_ge(turn_free, i * NR + AT[turn] + 1)
                return bank_of(*turn)

            def fold_sums(j):
                pe.wait_ge(sums_done, j + 1)
                mm(sum_ps[0:16, N:2 * N], g["fold"][:], sums[:], start=True, stop=True).then_inc(fold_done, 1)

            def over(j, n):
                bank = s_ps[n % 2]
                if n == 0:
                    pe.wait_ge(rsum_lo_done, j + 1)
                if n >= 2:
                    pe.wait_ge(on_done, j * a.pieces + n - 1)
                for h in range(2):
                    c = 2 * n + h
                    mm(bank[:, h * N:(h + 1) * N], spread[:, c * P:(c + 1) * P], rsum_hi[:], start=True, stop=False)
                    last = mm(bank[:, h * N:(h + 1) * N], spread[:, c * P:(c + 1) * P], rsum_lo[:], start=False, stop=True)
                last.then_inc(over_done, 1)

            def project(j, tiles=range(TT)):
                pe.wait_ge(olo_done, (j + 1) * a.pieces)
                for tt in tiles:
                    for c in range(OC):
                        last = three(o_ps[:, tt * D:(tt + 1) * D],
                                     [o[:, c, tt * P:(tt + 1) * P] for o in (o_hi, o_lo)],
                                     [w[:, c, :] for w in wo], c == 0, c == OC - 1)
                    last.then_inc(out_done, 1)

            def body(i, first, final):
                def unused(n):
                    pe.wait_ge(turn_done, i * NR + n)
                    pe.sem_inc(turn_done, 1)

                pe.wait_ge(xlo_done, i + 1)
                for kind, c in a.turns:
                    if (kind, c) == FOLD and not first:
                        fold_sums(i - 1)
                    for n in OVER.get((kind, c), []):
                        if not first:
                            over(i - 1, n)
                    if kind == "qk":
                        bank = take(i, kind, c)
                        for part, w in ((0, wq), (1, wk)):
                            for k in range(KD):
                                last = three(bank[:, part * N:(part + 1) * N],
                                             [w[j][:, k, c * P:(c + 1) * P] for j in range(2)],
                                             [xt[j][:, k, :] for j in range(2)], k == 0, k == KD - 1)
                        last.then_inc(turn_done, 1)
                        if qknorm and c >= 1:
                            variances(i, c - 1)
                    elif kind == "v":
                        if qknorm and c == 0:
                            variances(i, C - 1)
                        tt, c0 = c * a.vpiece // a.vw, c * a.vpiece % a.vw
                        if first and c == 0:
                            pe.wait_ge(lo_done, NP_)
                        bank = take(i, kind, c)
                        for k in range(KD):
                            last = three(bank[:, 0:a.vpiece],
                                         [xt[j][:, k, tt * P:(tt + 1) * P] for j in range(2)],
                                         [wv[j][:, k, c0:c0 + a.vpiece] for j in range(2)], k == 0, k == KD - 1)
                        last.then_inc(turn_done, 1)

                for n in LATE:
                    if not first:
                        over(i - 1, n)

                def qk_scale(c):
                    bank = take(i, "norm", c)
                    if c == 0:
                        pe.wait_ge(rqlo_done, i + 1)
                    mm(bank[:], spread[:, c * P:(c + 1) * P], rq_hi[:], start=True, stop=False)
                    mm(bank[:], spread[:, c * P:(c + 1) * P], rq_lo[:], start=False, stop=True).then_inc(turn_done, 1)

                def scores(u):
                    pe.wait_ge(qhi_done, i * U + u + 1)
                    if u or not first:
                        pe.wait_ge(mx_done, 2 * (i * U + u))
                    if masked and u == 0:
                        pe.wait_ge(mrow_done, i + 1)
                    if u == 0 and not first:
                        pe.wait_ge(on_done, i * a.pieces)
                    for qt in range(TT):
                        if masked:
                            mm(s_ps[qt][:], g["ones_r"][:], mrow[:], start=True, stop=False, skip_group_check=True)
                        for h in range(HN):
                            if a.one:
                                for c in range(C):
                                    last = mm(s_ps[qt][:, 0:N], q_hi[:, 0, c * N + qt * P:c * N + (qt + 1) * P],
                                              k_hi[:, c, :], start=(c == 0), stop=(c == C - 1))
                            else:
                                last = mm(s_ps[qt][:, h * N:(h + 1) * N],
                                          q_hi[:, u % NB, h * N + qt * P:h * N + (qt + 1) * P],
                                          k_hi[:, 2 * u // a.per_chunk % KR, :], start=not masked, stop=True,
                                          skip_group_check=masked)
                        last.then_inc(s_done, 1)

                def scores_t(u):
                    pe.wait_ge(qlo_done, i * U + u + 1)
                    if qknorm:
                        pe.wait_ge(klo_done, i * C + u + 1)
                    for kt in range(TT):
                        if u >= 1:
                            pe.wait_ge(p_done, 2 * (i * U + u) - 1 + kt)
                        out = st_ps[kt][:, 0:HN * N]
                        ks = slice(kt * P, (kt + 1) * P)
                        if a.one:
                            for c in range(C):
                                three(out, [k_hi[:, c, ks], k_lo[:, c, ks]],
                                      [x[:, 0, c * N:(c + 1) * N] for x in (q_hi, q_lo)], c == 0, False)
                        else:
                            c = 2 * u // a.per_chunk % KR
                            three(out, [k_hi[:, c, ks], k_lo[:, c, ks]],
                                  [x[:, u % NB, :] for x in (q_hi, q_lo)], True, False)
                        if kt == 0:
                            pe.wait_ge(shift_done, i * U + u + 1)
                        mm(out, g["ones_r"][:], shift[:, u % 2, 0:HN * N], start=False, stop=True).then_inc(st_done, 1)

                def weighted(u):
                    if u or not first:
                        pe.wait_ge(o_done, i * U + u)
                    if u == 0 and not first:
                        pe.wait_ge(rsum_done, i)
                        pe.wait_ge(taken, i)

                    def products(kt, h):
                        hd = HN * u + h
                        ps = prob[:, u % 2, kt, h * N:(h + 1) * N]
                        if a.one:
                            for c in range(C):
                                mm(o_ps[:, c * N:(c + 1) * N], v[:, kt, c * P:(c + 1) * P], ps,
                                   start=(kt == 0 and c == 0), stop=(kt == TT - 1), skip_group_check=True)
                        else:
                            at = o_row(a, u, h)
                            mm(o_ps[at:at + a.vd, 0:N], v[:, kt, hd * a.vd:(hd + 1) * a.vd], ps,
                               start=(kt == 0), stop=(kt == TT - 1), skip_group_check=True)

                    def sum_rows(kt, h):
                        group = 2 * (1 - u % 2) + h if a.vd == 32 else 2 * kt + h
                        opens = u < 2 and kt == 0 if a.vd == 32 else u == 0
                        wide = 64 if a.one else 32
                        return mm(sum_ps[32 * group:32 * group + wide, 0:N], g["head_sel"][:, 31 - u:31 - u + wide],
                                  prob[:, u % 2, kt, h * N:(h + 1) * N], start=opens, stop=(u == U - 1), skip_group_check=True)

                    for kt in range(TT):
                        pe.wait_ge(p_done, 2 * (i * U + u) + kt + 1)
                        for h in range(HN):
                            products(kt, h)
                        if a.vd == 32:
                            for h in range(HN):
                                last = sum_rows(kt, h)
                    if a.vd != 32:
                        for kt in range(TT):
                            for h in range(HN):
                                last = sum_rows(kt, h)
                    last.then_inc(pv_done, 1)

                if qknorm:
                    if not first:
                        project(i - 1, [0])
                    qk_scale(0)
                    qk_scale(1)
                    if not first:
                        project(i - 1, [1])
                for step in range(U + 2):
                    if step < U:
                        scores(step)
                    if step == 0 and not first and not qknorm:
                        project(i - 1)
                    if step == LN_STEP and final:
                        unused(AT["ln", 0])
                    elif step == LN_STEP:
                        bank = take(i, "ln", 0)
                        pe.wait_ge(xn_done, i + 2)
                        transposes(bank).then_inc(turn_done, 1)
                    if qknorm and step + 2 < U:
                        qk_scale(step + 2)
                    if 1 <= step <= U:
                        scores_t(step - 1)
                    if 2 <= step <= U + 1:
                        weighted(step - 2)
                if ("spare", 0) in AT:
                    unused(NR - 1)

            body(0, True, False)
            with pe.Fori(1, B - 1) as i:
                body(i, False, False)
            body(B - 1, False, True)
            fold_sums(B - 1)
            for n in range(a.pieces):
                over(B - 1, n)
            project(B - 1)

        @block.vector
        def _(dve):
            V = nc.vector
            tile = lambda j: g["x"][:, bass.ds(j, 1), :].squeeze(1)
            column = lambda row, i: g["mod"][:, row, bass.ds(i, 1)]

            def moments(j):
                if not a.norm:
                    return
                for tt in range(TT):
                    V.bn_stats(stats[:, tt, :], tile(j * TT + tt)).then_inc(stats_done, 1)
                for tt in range(TT):
                    dve.wait_ge(stats_done, TT * j + tt + 1)
                    dve.sem_inc(passed_dve, 1)
                    V.bn_aggr(mv[:, tt, :], stats[:, tt, :]).then_inc(aggr_done, 1)
                if a.norm == "rms":
                    dve.wait_ge(aggr_done, (TT + 1) * j + TT)
                    V.tensor_tensor(ve2[:], mv[:, :, 0], mv[:, :, 0], ALU.mult).then_inc(aggr_done, 1)
                    dve.wait_ge(aggr_done, (TT + 1) * j + TT + 1)
                    V.scalar_tensor_tensor(ve[:], ve2[:], a.eps, mv[:, :, 1], ALU.add, ALU.add).then_inc(ve_done, 1)
                else:
                    dve.wait_ge(aggr_done, TT * (j + 1))
                    V.tensor_scalar(ve[:], mv[:, :, 1], a.eps, None, ALU.add).then_inc(ve_done, 1)

            def normalise(j):
                if not a.norm:
                    V.tensor_copy(xn, g["x"][:, bass.ds(j * TT, TT), :]).then_inc(xn_done, 1)
                    return
                dve.wait_ge(rstd_done, j + 1)
                for tt in range(TT):
                    if a.norm == "rms":
                        ins = V.tensor_scalar(xn[:, tt, :], tile(j * TT + tt), rstd[:, tt:tt + 1], None, ALU.mult)
                    else:
                        ins = V.tensor_scalar(xn[:, tt, :], tile(j * TT + tt), mv[:, tt, 0:1], rstd[:, tt:tt + 1],
                                              ALU.subtract, ALU.mult)
                ins.then_inc(xn_done, 1)

            def modulate(j, bank):
                for k in range(KD):
                    if nm == "L2a":
                        ins = V.tensor_copy(xm[:, k, :], bank[:, k * N:(k + 1) * N])
                    else:
                        at = MOD_AT[nm]
                        ins = V.tensor_scalar(xm[:, k, :], bank[:, k * N:(k + 1) * N], column(at + k, j),
                                              column(at + 2 + k, j), ALU.mult, ALU.add)
                ins.then_inc(xm_done, 1)

            def x_lo(j):
                dve.wait_ge(xhi_done, j + 1)
                V.tensor_tensor(xt[1][:], xm[:], xt[0][:].bitcast(F32), ALU.subtract).then_inc(xlo_done, 1)

            dve.sem_inc(turn_free, 2)
            if qknorm:
                V.memset(eps_col[:], a.eps).then_inc(consts, 1)
            if masked:
                dve.wait_ge(mask_in, 48)
                V.tensor_scalar(key_bias[:], mask_u8[:], 1.0, 3.0e38, ALU.subtract, ALU.mult).then_inc(kb_done, 1)
                dve.wait_ge(kb_done, 1)
            dve.wait_ge(pre, 2 + 2 * qknorm + masked)
            moments(0)
            normalise(0)
            dve.wait_ge(pe_first, 1)
            modulate(0, ring[0])
            x_lo(0)
            loader(dve=dve)[2]()

            def copy_sums(j):
                dve.wait_ge(pv_done, j * U + U)
                V.tensor_copy(sums[:], sum_ps[:, 0:N]).then_inc(sums_done, 1)

            def sums_over(j):
                dve.wait_ge(fold_done, j + 1)
                V.reciprocal(rsum[:], sum_ps[0:a.heads, N:2 * N]).then_inc(rsum_done, 1)

            def tail_rows(j):
                dve.wait_ge(rsum_hi_done, j + 1)
                V.tensor_tensor(rsum_lo[0:a.heads, :], rsum[:], rsum_hi[0:a.heads, :].bitcast(F32), ALU.subtract).then_inc(rsum_lo_done, 1)

            def over(j, n):
                dve.wait_ge(over_done, j * a.pieces + n + 1)
                dve.wait_ge(o_done, (j + 1) * U)
                if n >= 2:
                    dve.wait_ge(olo_done, j * a.pieces + n - 1)
                V.tensor_tensor(o32[:, n % 2, :], o_raw[:, 2 * n:2 * n + 2, :].rearrange("p c n -> p (c n)"), s_ps[n % 2][:], ALU.mult)\
                    .then_inc(on_done, 1)

            def o_low(j, n):
                dve.wait_ge(ohi_done, j * a.pieces + n + 1)
                if a.one:
                    for c in range(2):
                        vb = COL_AT["L1_cond_v_b"] + c
                        ins = V.scalar_tensor_tensor(o_lo[:, c, :], o32[:, 0, c * N:(c + 1) * N], cols[:, vb:vb + 1],
                                                     o_hi[:, c, :].bitcast(F32), ALU.add, ALU.subtract)
                else:
                    pair = lambda o: o[:, 2 * n:2 * n + 2, :].rearrange("p c n -> p (c n)")
                    ins = V.tensor_tensor(pair(o_lo), o32[:, n % 2, :], pair(o_hi).bitcast(F32), ALU.subtract)
                ins.then_inc(olo_done, 1)

            res = Residual(nc, dve, nm, TT, {"step": ep_step, "taken": taken, "done": ep_done, "xh": xh_done, "ve2": ve2_done,
                                             "rstd2": rstd2_done, "passed": passed_dve},
                           (y, y2, stats, mv, ve2, rstd2, y_bias), g, a.eps)
            gates_at = lambda j: (gate_in, 32 * j + 32 + (16 if nm == "L2a" else 0))
            the_gate = lambda k: gate[:, 0, :].unsqueeze(1).to_broadcast([P, k, D])

            def take_projection(j):
                dve.wait_ge(out_done, TT * (j + 1))
                dve.wait_ge(olo_done, (j + 1) * a.pieces)
                res.take(j, [(0, TT, o_ps[:].rearrange("p (t d) -> p t d", d=D))], lambda t0, k: the_gate(k),
                         gates_at(j) if a.gated else (out_done, TT * (j + 1)))

            def finish(j):
                res.moments(j)
                res.add(j, the_gate(TT).unsqueeze(1) if a.gated else None)

            def body(i, first, final):
                def unused(n):
                    dve.wait_ge(turn_free, i * NR + n + 2)
                    dve.sem_inc(turn_free, 1)

                if masked and not first:
                    dve.wait_ge(pv_done, i * U)
                if masked:
                    V.tensor_copy(kbias[:], key_bias[:, :, bass.ds(i, 1)].squeeze(2)).then_inc(kb_done, 1)
                    V.tensor_scalar(mrow[0:1, :].rearrange("o (h n) -> o h n", h=2), mrow_u8[0:1, :, bass.ds(i, 1), :].squeeze(2),
                                    1.0, 1.0e30, ALU.subtract, ALU.mult).then_inc(mrow_done, 1)
                owed = []

                def pay(keep=0):
                    while len(owed) > keep and not first:
                        o_low(i - 1, owed.pop(0))

                for n, (kind, c) in enumerate(a.turns):
                    if a.one and not final and n == 0:
                        moments(i + 1)
                    if a.one and not final and (kind, c) == ("v", 0):
                        normalise(i + 1)
                    bank = ring[n % 2]
                    if (kind, c) == COPY and not first:
                        copy_sums(i - 1)
                    if (kind, c) == FOLD and not first:
                        sums_over(i - 1)
                    if (kind, c) == LOW and not first:
                        tail_rows(i - 1)
                    for m in OVER.get((kind, c), []):
                        if not first:
                            pay(1)
                            over(i - 1, m)
                            owed.append(m)
                    if kind == "qk" and qknorm:
                        dve.wait_ge(sq_done, i * C + c + 1)
                        dve.wait_ge(raw_done, i * C + c + 1)
                        dve.sem_inc(turn_free, 1)
                    elif kind == "qk":
                        dve.wait_ge(khi_done, i * C + c + 1)
                        if nm == "L1a":
                            kb = COL_AT["L1_cond_k_b"] + c
                            ins = V.scalar_tensor_tensor(k_lo[:, c, :], bank[:, N:2 * N], cols[:, kb:kb + 1],
                                                         k_hi[:, c, :].bitcast(F32), ALU.add, ALU.subtract)
                        else:
                            ins = V.tensor_tensor(k_lo[:, c, :], bank[:, N:2 * N], k_hi[:, c, :].bitcast(F32),
                                                  ALU.subtract)
                        ins.then_inc(turn_free, 1)
                    elif kind == "v":
                        tt, c0 = c * a.vpiece // a.vw, c * a.vpiece % a.vw
                        dve.wait_ge(turn_done, i * NR + n + 1)
                        V.tensor_copy(v[:, tt, c0:c0 + a.vpiece], bank[:, 0:a.vpiece]).then_inc(turn_free, 1)
                        pay()
                for m in LATE:
                    if not first:
                        over(i - 1, m)
                        owed.append(m)
                pay()
                if qknorm:
                    dve.wait_ge(rqhi_done, i + 1)
                    V.tensor_tensor(rq_lo[0:a.heads, :], rstdq[:], rq_hi[0:a.heads, :].bitcast(F32), ALU.subtract).then_inc(rqlo_done, 1)

                def q_low(u):
                    dve.wait_ge(qhi_done, i * U + u + 1)
                    if a.one:
                        V.tensor_tensor(q_lo[:, 0, :], q32[:].rearrange("p c n -> p (c n)"),
                                        q_hi[:, 0, :].bitcast(F32), ALU.subtract).then_inc(qlo_done, 1)
                        return
                    if u >= NB:
                        dve.wait_ge(st_done, 2 * (i * U + u - NB) + 2)
                    for h in range(2):
                        m = MASK0 + (2 * u + h) % a.per_chunk
                        ins = V.scalar_tensor_tensor(q_lo[:, u % NB, h * N:(h + 1) * N], q_of(2 * u // a.per_chunk),
                                                     g["hmask"][:, m:m + 1],
                                                     q_hi[:, u % NB, h * N:(h + 1) * N].bitcast(F32),
                                                     ALU.mult, ALU.subtract)
                    ins.then_inc(qlo_done, 1)

                def maxes(u):
                    if u or not first:
                        dve.wait_ge(shift_done, i * U + u)
                    for qt in range(TT):
                        dve.wait_ge(s_done, 2 * (i * U + u) + qt + 1)
                        V.tensor_reduce(mx[:, 0:2 * HN].rearrange("p (h q) -> p h q", q=2)[:, :, qt],
                                        s_ps[qt][:, 0:HN * N].rearrange("p (h n) -> p h n", h=HN), AX.X, ALU.max)\
                            .then_inc(mx_done, 1)
                    dve.wait_ge(mx_done, 2 * (i * U + u) + 2)
                    if u >= 2:
                        dve.wait_ge(st_done, 2 * (i * U + u) - 2)
                    n = 2 * HN
                    V.tensor_tensor(shift[:, u % 2, 0:HN * N].rearrange("p (b q) -> p b q", q=P),
                                    g["neg_ident"][:].unsqueeze(1).to_broadcast([P, n, P]),
                                    mx[:, 0:n].unsqueeze(2).to_broadcast([P, n, P]), ALU.mult).then_inc(shift_done, 1)

                def qk_scaled(c):
                    bank = bank_of("norm", c)
                    dve.wait_ge(turn_done, i * NR + AT["norm", c] + 1)
                    if c or not first:
                        dve.wait_ge(q32_done, i * C + c)
                    V.tensor_tensor(qn[:], raw[:, c, :], bank[:], ALU.mult).then_inc(qn_done, 1)
                    dve.wait_ge(qn_done, i * C + c + 1)
                    dve.sem_inc(turn_free, 1)

                def k_low(c):
                    dve.wait_ge(khi_done, i * C + c + 1)
                    V.tensor_tensor(k_lo[:, c % KR, :], raw[:, c, N:2 * N], k_hi[:, c % KR, :].bitcast(F32), ALU.subtract).then_inc(klo_done, 1)

                if qknorm:
                    qk_scaled(0)
                    qk_scaled(1)
                    k_low(0)
                q_low(0)
                for step in range(U + 2):
                    if step < U:
                        maxes(step)
                    if step == LN_STEP and not final:
                        dve.wait_ge(turn_done, i * NR + AT["ln", 0] + 1)
                        modulate(i + 1, bank_of("ln", 0))
                        dve.wait_ge(xm_done, i + 2)
                        dve.sem_inc(turn_free, 1)
                    elif step == LN_STEP:
                        unused(AT["ln", 0])
                    if qknorm and step + 2 < U:
                        qk_scaled(step + 2)
                    if step + 1 < U:
                        q_low(step + 1)
                    if qknorm and step + 1 < U:
                        k_low(step + 1)
                    if step == 0 and not first:
                        take_projection(i - 1)
                    if step == min(1, U) and not first:
                        res.moments(i - 1)
                    if step == min(2, U) and not first:
                        res.add(i - 1, the_gate(TT).unsqueeze(1) if a.gated else None)
                    if final:
                        continue
                    if step == a.ln_step - 3 and not a.one:
                        moments(i + 1)
                    if step == a.ln_step - 2 and not a.one:
                        normalise(i + 1)
                    if step == LN_STEP + 1:
                        x_lo(i + 1)
                if ("spare", 0) in AT:
                    unused(NR - 1)

            body(0, True, False)
            with dve.Fori(1, B - 1) as i:
                body(i, False, False)
            body(B - 1, False, True)
            copy_sums(B - 1)
            sums_over(B - 1)
            tail_rows(B - 1)
            for n in range(a.pieces):
                over(B - 1, n)
                o_low(B - 1, n)
            take_projection(B - 1)
            finish(B - 1)


BB = 2
T4 = BB * TT
NN = BB * N


def mlp(nc, t, g, nm, norm, eps):
    gated = nm != "L1m"
    late = nm == "L2m"
    with semaphores(nc, nm) as sem, ExitStack() as ctx:
        sb = lambda n, s, d=F32: ctx.enter_context(nc.sbuf_tensor(f"{nm}_{n}", s, d))
        pb = lambda n: ctx.enter_context(nc.psum_tensor(f"{nm}_{n}", [P, 512], F32))
        up_ps, tp_ps, down_ps = [pb(f"up{j}") for j in range(2)], [pb(f"tp{k}") for k in range(KD)], \
            [pb(f"down{j}") for j in range(T4)]
        w1 = [sb(f"w1{j}", [P, KD, MLP], F32R) for j in range(2)]
        w2 = [sb(f"w2{j}", [P, MC, D], F32R) for j in range(2)]
        stage = sb("stage", [P, 2, 1024])
        xn, xm = sb("xn", [P, T4, D]), sb("xm", [P, KD, NN])
        xt = [sb(f"xt{j}", [P, KD, NN], F32R) for j in range(2)]
        stats, mv = sb("stats", [P, T4, 6]), sb("mv", [P, T4, 2])
        ve, ve2, rstd, rstd2 = sb("ve", [P, T4]), sb("ve2", [P, T4]), sb("rstd", [P, T4]), sb("rstd2", [P, T4])
        h32 = sb("h32", [P, 2, NN])
        h = [sb(f"h{j}", [P, MC, NN], F32R) for j in range(2)]
        y, y2 = sb("y", [P, T4, D]), sb("y2", [P, T4, D])
        gate, y_bias = sb("gate", [P, BB, 2, D]), sb("y_bias", [P, D])

        landed = [sem("landed0"), sem("landed1")]
        hi_done, lo_done = sem("hi_done"), sem("lo_done")
        stats_done, aggr_done, ve_done, rstd_done, xn_done = (sem(x) for x in ("stats", "aggr", "ve", "rstd", "xn"))
        tp_done, xm_done, xhi_done, xlo_done = sem("tp"), sem("xm"), sem("xhi"), sem("xlo")
        up_done, gelu_done, hhi_done, hlo_done = sem("up"), sem("gelu"), sem("hhi"), sem("hlo")
        down_done, down_free, ep_done, ep_step, xh_done = (sem(x) for x in ("down", "down_free", "ep", "ep_step", "xh"))
        gate_in, ve2_done, rstd2_done, passed = sem("gate_in"), sem("ve2"), sem("rstd2"), sem("passed")
        passed_dve, taken = sem("passed_dve"), sem("taken")

        pieces = []
        for k in range(KD):
            pieces.append((t[nm + "_w1"][k * P:(k + 1) * P, :], w1[0][:, k, :], w1[1][:, k, :], False))
        for m in range(0, MC, 4):
            pieces.append((t[nm + "_w2"][m * P:(m + 4) * P, :].rearrange("(c p) n -> p c n", p=P),
                           w2[0][:, m:m + 4, :], w2[1][:, m:m + 4, :], False))
        loader = lambda sp=None, act=None, dve=None: split_weights(
            nc, (sp, act, dve), stage, (landed, hi_done, lo_done), pieces)
        extra = 16 if nm == "L2m" else 0
        gates_in = lambda i: 16 * 2 * BB * i + 16 * 2 * BB + extra
        IT = B // BB
        block = ctx.enter_context(nc.Block())

        @block.sync
        def _(sp):
            loader(sp=sp)[0]()
            if gated:
                at = GATE_AT[nm]
                for bb in range(BB):
                    for j in range(2):
                        sp.dma_start(gate[:, bb, j, :], t["gate_rows"][at + j, bb, :].partition_broadcast(P)).then_inc(gate_in, 16)
            else:
                sp.dma_start(gate[:, 0, 0, :], t["L1_cond_mlp_b2"].partition_broadcast(P)).then_inc(gate_in, 16)
            if nm == "L2m":
                sp.dma_start(y_bias[:], t["L2_cond_fc2_b"].partition_broadcast(P)).then_inc(gate_in, 16)
            if gated:
                with sp.Fori(0, IT - 1) as i:
                    sp.wait_ge(ep_done, i + 1)
                    for bb in range(BB):
                        for j in range(2):
                            sp.dma_start(gate[:, bb, j, :], t["gate_rows"][at + j, bass.ds(BB * i + BB + bb, 1), :]
                                         .squeeze(0).partition_broadcast(P)).then_inc(gate_in, 16)

        @block.gpsimd
        def _(pool):
            def gated_wait(s, val):
                pool.wait_ge(s, val)
                pool.sem_inc(passed, 1)

            def token_rstd(j):
                if norm:
                    gated_wait(ve_done, j + 1)
                    nc.gpsimd.tensor_tensor(rstd[:], ve[:], g["mhalf"][:, 0:T4], ALU.pow).then_inc(rstd_done, 1)

            token_rstd(0)

            def rstd_out(i):
                gated_wait(ve2_done, i + 1)
                nc.gpsimd.tensor_tensor(rstd2[:], ve2[:], g["mhalf"][:, 0:T4], ALU.pow).then_inc(rstd2_done, 1)

            def body(i, first, more):
                if late and not first:
                    rstd_out(i - 1)
                if more:
                    token_rstd(i + 1)
                gated_wait(gate_in, gates_in(i) if gated else 16)
                gated_wait(xn_done, i + 1)
                tiles = g["x"][:, bass.ds(i * T4, T4), :]
                if gated:
                    shaped = tiles.rearrange("p (b t) d -> p b t d", t=TT)
                    row = gate[:, :, 1, :].unsqueeze(2).to_broadcast([P, BB, TT, D])
                else:
                    shaped, row = tiles, gate[:, 0, 0, :].unsqueeze(1).to_broadcast([P, T4, D])
                nc.gpsimd.tensor_tensor(shaped, shaped, row, ALU.add).then_inc(xh_done, 1)

            body(0, True, True)
            with pool.Fori(1, IT - 1) as i:
                body(i, False, True)
            body(IT - 1, False, False)
            if late:
                rstd_out(IT - 1)

        @block.scalar
        def _(act):
            b1 = COL_AT[{"L0m": "L0_cond_b1", "L1m": "L1_cond_mlp_b1", "L2m": "L2_cond_fc1_b"}[nm]]

            def x_hi(j):
                act.wait_ge(xm_done, j + 1)
                nc.scalar.activation(xt[0][:], xm[:], ACT.Copy).then_inc(xhi_done, 1)

            x_hi(0)
            loader(act=act)[1]()

            def body(i, more):
                for m in range(MC):
                    act.wait_ge(up_done, MC * i + m + 1)
                    if m >= 2:
                        act.wait_ge(hlo_done, MC * i + m - 1)
                    nc.scalar.activation(h32[:, m % 2, :], up_ps[m % 2][:], ACT.Gelu,
                                         bias=g["cols"][:, b1 + m:b1 + m + 1]).then_inc(gelu_done, 1)
                    act.wait_ge(gelu_done, MC * i + m + 1)
                    nc.scalar.activation(h[0][:, m, :], h32[:, m % 2, :], ACT.Copy).then_inc(hhi_done, 1)
                if more:
                    x_hi(i + 1)

            with act.Fori(0, IT - 1) as i:
                body(i, True)
            body(IT - 1, False)

        @block.tensor
        def _(pe):
            mm = nc.tensor.matmul

            def three(out, lhs, rhs, start, stop):
                mm(out, lhs[0], rhs[0], start=start, stop=False)
                mm(out, lhs[1], rhs[0], start=False, stop=False)
                return mm(out, lhs[0], rhs[1], start=False, stop=stop)

            def transposes(j):
                pe.wait_ge(xn_done, j + 1)
                for k in range(KD):
                    for tt in range(T4):
                        last = nc.tensor.transpose(tp_ps[k][:, tt * P:(tt + 1) * P], xn[:, tt, k * P:(k + 1) * P],
                                                   g["ident"][:])
                last.then_inc(tp_done, 1)

            transposes(0)
            pe.wait_ge(lo_done, KD)

            def body(i, more):
                pe.wait_ge(xlo_done, i + 1)
                for m in range(MC):
                    if m >= 2:
                        pe.wait_ge(gelu_done, MC * i + m - 1)
                    for k in range(KD):
                        last = three(up_ps[m % 2][:], [w[:, k, m * P:(m + 1) * P] for w in w1],
                                     [x[:, k, :] for x in xt], k == 0, k == KD - 1)
                    last.then_inc(up_done, 1)
                pe.wait_ge(down_free, i + 1)
                pe.wait_ge(lo_done, len(pieces))
                for m in range(MC):
                    pe.wait_ge(hlo_done, MC * i + m + 1)
                    for tt in range(T4):
                        last = three(down_ps[tt][:, 0:D], [x[:, m, tt * P:(tt + 1) * P] for x in h],
                                     [w[:, m, :] for w in w2], m == 0, m == MC - 1)
                    if m == 3 and more:
                        transposes(i + 1)
                last.then_inc(down_done, 1)

            with pe.Fori(0, IT - 1) as i:
                body(i, True)
            body(IT - 1, False)

        @block.vector
        def _(dve):
            V = nc.vector
            tile = lambda j: g["x"][:, bass.ds(j, 1), :].squeeze(1)

            def normalise(j):
                if not norm:
                    for tt in range(T4):
                        ins = V.tensor_copy(xn[:, tt, :], tile(j * T4 + tt))
                    ins.then_inc(xn_done, 1)
                    return
                for tt in range(T4):
                    V.bn_stats(stats[:, tt, :], tile(j * T4 + tt)).then_inc(stats_done, 1)
                for tt in range(T4):
                    dve.wait_ge(stats_done, T4 * j + tt + 1)
                    dve.sem_inc(passed_dve, 1)
                    V.bn_aggr(mv[:, tt, :], stats[:, tt, :]).then_inc(aggr_done, 1)
                if norm == "rms":
                    dve.wait_ge(aggr_done, (T4 + 1) * j + T4)
                    V.tensor_tensor(ve2[:], mv[:, :, 0], mv[:, :, 0], ALU.mult).then_inc(aggr_done, 1)
                    dve.wait_ge(aggr_done, (T4 + 1) * j + T4 + 1)
                    V.scalar_tensor_tensor(ve[:], ve2[:], eps, mv[:, :, 1], ALU.add, ALU.add).then_inc(ve_done, 1)
                else:
                    dve.wait_ge(aggr_done, T4 * (j + 1))
                    V.tensor_scalar(ve[:], mv[:, :, 1], eps, None, ALU.add).then_inc(ve_done, 1)
                dve.wait_ge(rstd_done, j + 1)
                for tt in range(T4):
                    if norm == "rms":
                        ins = V.tensor_scalar(xn[:, tt, :], tile(j * T4 + tt), rstd[:, tt:tt + 1], None, ALU.mult)
                    else:
                        ins = V.tensor_scalar(xn[:, tt, :], tile(j * T4 + tt), mv[:, tt, 0:1], rstd[:, tt:tt + 1],
                                              ALU.subtract, ALU.mult)
                ins.then_inc(xn_done, 1)

            def modulate(j):
                dve.wait_ge(tp_done, j + 1)
                for k in range(KD):
                    if not norm:
                        ins = V.tensor_copy(xm[:, k, :], tp_ps[k][:])
                        continue
                    at = MOD_AT[nm]
                    for bb in range(BB):
                        col = lambda row: g["mod"][:, row, bass.ds(BB * j + bb, 1)]
                        ins = V.tensor_scalar(xm[:, k, bb * N:(bb + 1) * N], tp_ps[k][:, bb * N:(bb + 1) * N],
                                              col(at + k), col(at + 2 + k), ALU.mult, ALU.add)
                ins.then_inc(xm_done, 1)
                dve.wait_ge(xhi_done, j + 1)
                V.tensor_tensor(xt[1][:], xm[:], xt[0][:].bitcast(F32), ALU.subtract).then_inc(xlo_done, 1)

            dve.sem_inc(down_free, 1)
            res = Residual(nc, dve, nm, T4, {"step": ep_step, "taken": taken, "done": ep_done, "xh": xh_done, "ve2": ve2_done,
                                             "rstd2": rstd2_done, "passed": passed_dve}, (y, y2, stats, mv, ve2, rstd2, y_bias), g, eps)
            normalise(0)
            modulate(0)
            loader(dve=dve)[2]()

            the_gate = gate[:, :, 0, :].unsqueeze(2).to_broadcast([P, BB, TT, D])

            def body(i, first, more):
                for m in range(MC):
                    dve.wait_ge(hhi_done, MC * i + m + 1)
                    V.tensor_tensor(h[1][:, m, :], h32[:, m % 2, :], h[0][:, m, :].bitcast(F32), ALU.subtract)\
                        .then_inc(hlo_done, 1)
                    if m == 3 and more:
                        normalise(i + 1)
                    if late and not first and m == 1:
                        res.moments(i - 1)
                    if late and not first and m == 5:
                        res.add(i - 1, the_gate)
                if more:
                    modulate(i + 1)
                dve.wait_ge(down_done, i + 1)
                res.take(i, [(j, 1, p[:, 0:D].unsqueeze(1)) for j, p in enumerate(down_ps)],
                         lambda t0, k: gate[:, t0 // TT, 0, :].unsqueeze(1), (gate_in, gates_in(i)) if gated else (down_done, i + 1))
                dve.sem_inc(down_free, 1)
                if not late:
                    res.add(i, the_gate)

            body(0, True, True)
            with dve.Fori(1, IT - 1) as i:
                body(i, False, True)
            body(IT - 1, False, False)
            if late:
                res.moments(IT - 1)
                res.add(IT - 1, the_gate)


BF16 = mybir.dt.bfloat16
ROW = D + E
ROUND = 1.5 * 2.0 ** 23
LN2_HIGH = 0.693359375
LN2_LOW = float(np.log(2.0) - LN2_HIGH)
BITS = 30


def route(nc, t, g, out, moe):
    with semaphores(nc, "r") as sem, ExitStack() as ctx:
        sb = lambda n, s, d=F32: ctx.enter_context(nc.sbuf_tensor(f"r_{n}", s, d))
        pb = lambda n: ctx.enter_context(nc.psum_tensor(f"r_{n}", [P, 512], F32))
        tp_ps, lg_ps, cnt_ps, pre_ps, tot_ps = [pb("tp0"), pb("tp1")], [pb("lg0"), pb("lg1")], pb("cnt"), pb("pre"), pb("tot")
        list_ps = [tp_ps[0], pb("list1")]
        wg, tri, iota_f = sb("wg", [P, KD, E]), sb("tri", [P, P]), sb("iota_f", [P, P])
        tval, pval = sb("tval", [P, TILES]), sb("pval", [P, 1])
        xs, xt = sb("xs", [P, 2, T4, D]), sb("xt", [P, 2, KD, NN])
        logit = sb("logit", [P, TILES, E])
        lmax, lsum, lrec = sb("lmax", [P, TILES]), sb("lsum", [P, TILES]), sb("lrec", [P, TILES])
        power, rest, word = sb("power", [P, TILES, E]), sb("rest", [P, TILES, E]), sb("word", [P, TILES, E], I32)
        centred, ex, gates = (sb(n, [P, TILES, E]) for n in ("centred", "ex", "gates"))
        ge = sb("ge", [P, E, TILES])
        thr, cand, bit = (sb(n, [P, E], U32) for n in ("thr", "cand", "bit"))
        hit, keep = sb("hit", [P, E, TILES]), sb("keep", [P, E], U32)
        part_count, need = sb("part_count", [P, E]), sb("need", [P, E])
        above, equal, sel = (sb(n, [P, E, TILES]) for n in ("above", "equal", "sel"))
        totals, scan, zeros = (sb(n, [P, E, TILES]) for n in ("totals", "scan", "zeros"))
        rank, low = sb("rank", [P, E, TILES]), sb("low", [P, E, TILES])
        ge_h = [sb(f"ge_h{h}", [P, E, TILES]) for h in range(SC + 1)]
        hs = sb("hs", [P, E, TILES])
        vals = sb("vals", [P, E, TILES, 2 * SC], BF16)
        onehot = sb("onehot", [P, 2, TILES, P], BF16)
        iota_b, low_b = sb("iota_b", [P, P], BF16), sb("low_b", [P, E, TILES], BF16)
        lists, idx_f = sb("lists", [P, E, 2 * SC]), sb("idx_f", [P, E, SC])

        const_in, xs_done, tp_done, xt_done, lg_done, lgc_done = (sem(n) for n in ("const", "xs", "tp", "xt", "lg", "lgc"))
        xt2_done, chain, made = sem("xt2"), sem("chain"), sem("made")
        count_in, count_done, pre_in, pre_done = sem("count_in"), sem("count_done"), sem("pre_in"), sem("pre_done")
        hot_done, list_done, list_read, stored, rows_ready = (sem(n) for n in ("hot", "list", "list_read", "stored", "rows"))
        bchain, passed = sem("bchain"), sem("passed")
        w_in, w_hi, w_lo = sem("w_in"), sem("w_hi"), sem("w_lo")
        IT = TILES // T4
        block = ctx.enter_context(nc.Block())

        @block.sync
        def _(sp):
            for dst, name in ((tri, "tri"), (iota_f, "iota"), (tval, "tval"), (pval, "pval")):
                sp.dma_start(dst[:], t[name]).then_inc(const_in, 16)
            sp.dma_start(wg[:], t["wg_t"].rearrange("(k p) e -> p k e", p=P)).then_inc(const_in, 16)
            sp.dma_start(out.rearrange("b (t p) d -> p (b t) d", p=P), g["x"][:]).then_inc(stored, 16)
            rows = t["token_rows"].rearrange("(t p) r -> p t r", p=P)
            sp.dma_start(rows[:, :, 0:D], g["x"][:]).then_inc(stored, 16)
            sp.dma_start(moe["stage1"][:], t["moe_w1"].rearrange("e (k p) n -> e p k n", p=P)[0]).then_inc(w_in, 16)
            sp.dma_start(moe["stage2"][:], t["moe_w2"].rearrange("e (m p) n -> e p m n", p=P)[0]).then_inc(w_in, 16)
            sp.wait_ge(rows_ready, 1)
            sp.dma_start(rows[:, :, D:ROW], gates[:]).then_inc(stored, 16)
            sp.wait_ge(stored, 48)

        @block.gpsimd
        def _(pool):
            nc.gpsimd.memset(zeros[:], 0.0).then_inc(made, 1)
            pool.wait_ge(w_in, 32)
            for n, (stage, w) in enumerate(((moe["stage1"], moe["w1"]), (moe["stage2"], moe["w2"]))):
                nc.gpsimd.tensor_copy(w[0][:], stage[:]).then_inc(w_hi, 1)
                pool.wait_ge(w_hi, n + 1)
                nc.gpsimd.tensor_tensor(w[1][:], stage[:], w[0][:].bitcast(F32), ALU.subtract).then_inc(w_lo, 1)
            pool.wait_ge(w_lo, 2)

        @block.scalar
        def _(act):
            with act.Fori(0, IT // 2) as pair:
                for s in range(2):
                    act.wait_ge(tp_done, 2 * pair + s + 1)
                    nc.scalar.activation(xt[:, s, 1, :], tp_ps[1][:], ACT.Copy).then_inc(xt2_done, 1)

        @block.tensor
        def _(pe):
            mm = nc.tensor.matmul
            pe.wait_ge(const_in, 80)
            def transposes(i, s):
                pe.wait_ge(xs_done, i + 1)
                for k in range(KD):
                    for tt in range(T4):
                        last = nc.tensor.transpose(tp_ps[k][:, tt * P:(tt + 1) * P], xs[:, s, tt, k * P:(k + 1) * P],
                                                   g["ident"][:])
                last.then_inc(tp_done, 1)

            def logits(i, s):
                for tt in range(T4):
                    for k in range(KD):
                        last = mm(lg_ps[s][:, tt * E:(tt + 1) * E], xt[:, s, k, tt * P:(tt + 1) * P], wg[:, k, :],
                                  start=(k == 0), stop=(k == KD - 1))
                last.then_inc(lg_done, 1)

            def pair_of(pair, more):
                for s in range(2):
                    i = 2 * pair + s
                    pe.wait_ge(xt_done, i + 1)
                    pe.wait_ge(xt2_done, i + 1)
                    if s == 0 or more:
                        transposes(i + 1, 1 - s)
                    logits(i, s)

            transposes(0, 0)
            with pe.Fori(0, IT // 2 - 1) as pair:
                pair_of(pair, True)
            pair_of(IT // 2 - 1, False)
            with pe.Fori(0, BITS + 1) as n:
                pe.wait_ge(count_in, n + 1)
                mm(cnt_ps[:, 0:E], g["ones"][:], part_count[:], start=True, stop=True).then_inc(count_done, 1)
            for n, what in enumerate((equal, sel)):
                pe.wait_ge(pre_in, n + 1)
                flat = what[:].rearrange("p e t -> p (e t)")
                mm(pre_ps[:, 0:E * TILES], tri[:], flat, start=True, stop=True)
                mm(tot_ps[:, 0:E * TILES], g["ones"][:], flat, start=True, stop=True).then_inc(pre_done, 1)
            with pe.Fori(0, E // 2) as i:
                for par in range(2):
                    pe.wait_ge(hot_done, 2 * i + par + 1)
                    for tile in range(TILES):
                        last = mm(list_ps[par][:, 0:2 * SC], onehot[:, par, tile, :],
                                  vals[:, bass.ds(2 * i + par, 1), tile, :].squeeze(1),
                                  start=(tile == 0), stop=(tile == TILES - 1))
                    last.then_inc(list_done, 1)

        @block.vector
        def _(dve):
            V = nc.vector
            done = [0]

            def step(ins):
                done[0] += 1
                ins.then_inc(chain, 1)
                dve.wait_ge(chain, done[0])

            def pair_of(pair, more):
                for s in range(2):
                    i = 2 * pair + s
                    if s == 0 or more:
                        V.tensor_copy(xs[:, 1 - s, :, :], g["x"][:, bass.ds((i + 1) * T4, T4), :]).then_inc(xs_done, 1)
                    dve.wait_ge(tp_done, i + 1)
                    V.tensor_copy(xt[:, s, 0, :], tp_ps[0][:]).then_inc(xt_done, 1)
                    dve.wait_ge(lg_done, i + 1)
                    V.tensor_copy(logit[:, bass.ds(i * T4, T4), :], lg_ps[s][:, 0:T4 * E].rearrange("p (t e) -> p t e", e=E))\
                        .then_inc(lgc_done, 1)

            V.tensor_copy(xs[:, 0, :, :], g["x"][:, 0:T4, :]).then_inc(xs_done, 1)
            with dve.Fori(0, IT // 2 - 1) as pair:
                pair_of(pair, True)
            pair_of(IT // 2 - 1, False)
            dve.wait_ge(lgc_done, IT)
            bc = lambda col: col[:].unsqueeze(2).to_broadcast([P, TILES, E])
            step(V.tensor_reduce(lmax[:], logit[:], AX.X, ALU.max))
            step(V.tensor_tensor(centred[:], logit[:], bc(lmax), ALU.subtract))
            step(V.tensor_scalar(centred[:], centred[:], -87.0, None, ALU.max))
            step(V.tensor_scalar(power[:], centred[:], float(1 / np.log(2)), ROUND, ALU.mult, ALU.add))
            step(V.tensor_scalar(power[:], power[:], ROUND, None, ALU.subtract))
            step(V.scalar_tensor_tensor(rest[:], power[:], -LN2_HIGH, centred[:], ALU.mult, ALU.add))
            step(V.scalar_tensor_tensor(rest[:], power[:], -LN2_LOW, rest[:], ALU.mult, ALU.add))
            step(V.tensor_scalar(ex[:], rest[:], 1.0 / math.factorial(7), None, ALU.mult))
            for k in range(6, 0, -1):
                step(V.scalar_tensor_tensor(ex[:], ex[:], 1.0 / math.factorial(k), rest[:], ALU.add, ALU.mult))
            step(V.tensor_scalar(word[:], power[:], 127.0, None, ALU.add))
            step(V.tensor_scalar(word[:], word[:], 23, None, ALU.logical_shift_left))
            step(V.scalar_tensor_tensor(ex[:], ex[:], 1.0, word[:].bitcast(F32), ALU.add, ALU.mult))
            step(V.tensor_reduce(lsum[:], ex[:], AX.X, ALU.add))
            step(V.reciprocal(lrec[:], lsum[:]))
            step(V.tensor_tensor(gates[:], ex[:], bc(lrec), ALU.mult))
            V.engine_nop().then_inc(rows_ready, 1)
            step(V.tensor_copy(ge[:], gates[:].rearrange("p t e -> p e t")))
            step(V.memset(thr[:], 0))
            step(V.memset(bit[:], 1 << (BITS - 1)))
            over = lambda col: col[:].unsqueeze(2).to_broadcast([P, E, TILES])
            per = 5

            def search(n):
                V.tensor_tensor(cand[:], thr[:], bit[:], ALU.bitwise_or).then_inc(bchain, 1)
                dve.wait_ge(bchain, per * n + 1)
                V.tensor_tensor(hit[:], ge[:], over(cand).bitcast(F32), ALU.is_ge).then_inc(bchain, 1)
                V.tensor_scalar(bit[:], bit[:], 1, None, ALU.logical_shift_right).then_inc(bchain, 1)
                dve.wait_ge(bchain, per * n + 3)
                V.tensor_reduce(part_count[:], hit[:], AX.X, ALU.add).then_inc(count_in, 1)
                dve.wait_ge(count_done, n + 1)
                V.tensor_scalar(keep[:], cnt_ps[:, 0:E], float(CAP), None, ALU.is_ge).then_inc(bchain, 1)
                dve.wait_ge(bchain, per * n + 4)
                dve.sem_inc(passed, 1)
                V.copy_predicated(thr[:], keep[:], cand[:]).then_inc(bchain, 1)
                dve.wait_ge(bchain, per * n + 5)

            with dve.Fori(0, BITS // 5) as block_of_5:
                for j in range(5):
                    search(5 * block_of_5 + j)
            th = over(thr).bitcast(F32)
            step(V.tensor_tensor(above[:], ge[:], th, ALU.is_gt))
            step(V.tensor_tensor(equal[:], ge[:], th, ALU.is_equal))
            V.tensor_reduce(part_count[:], above[:], AX.X, ALU.add).then_inc(count_in, 1)
            V.engine_nop().then_inc(pre_in, 1)
            dve.wait_ge(count_done, BITS + 1)
            step(V.tensor_scalar(need[:], cnt_ps[:, 0:E], -1.0, float(CAP), ALU.mult, ALU.add))

            def ranks(n):
                dve.wait_ge(pre_done, n + 1)
                step(V.tensor_copy(totals[:].rearrange("p e t -> p (e t)"), tot_ps[:, 0:E * TILES]))
                for e in range(E):
                    step(V.tensor_tensor_scan(scan[:, e, :], totals[:, e, :], zeros[:, e, :], 0.0, ALU.add, ALU.add))
                step(V.tensor_tensor(scan[:], scan[:], totals[:], ALU.subtract))
                step(V.tensor_tensor(rank[:], pre_ps[:, 0:E * TILES].rearrange("p (e t) -> p e t", t=TILES),
                                     scan[:], ALU.add))

            dve.wait_ge(made, 1)
            dve.wait_ge(const_in, 80)
            ranks(0)
            step(V.tensor_tensor(sel[:], rank[:], over(need), ALU.is_lt))
            step(V.tensor_tensor(sel[:], sel[:], equal[:], ALU.mult))
            step(V.tensor_tensor(sel[:], sel[:], above[:], ALU.add))
            V.engine_nop().then_inc(pre_in, 1)
            ranks(1)
            for h in range(1, SC):
                step(V.tensor_scalar(ge_h[h][:], rank[:], float(P * h), None, ALU.is_ge))
            step(V.scalar_tensor_tensor(low[:], ge_h[1][:], -float(P), rank[:], ALU.mult, ALU.add))
            for h in range(2, SC):
                step(V.scalar_tensor_tensor(low[:], ge_h[h][:], -float(P), low[:], ALU.mult, ALU.add))
            step(V.scalar_tensor_tensor(low[:], low[:], 1.0, sel[:], ALU.add, ALU.mult))
            step(V.tensor_scalar(low_b[:], low[:], -1.0, None, ALU.add))
            step(V.tensor_copy(iota_b[:], iota_f[:]))
            step(V.memset(ge_h[0][:], 1.0))
            step(V.memset(ge_h[SC][:], 0.0))
            for h in range(SC):
                step(V.tensor_tensor(hs[:], ge_h[h][:], ge_h[h + 1][:], ALU.subtract))
                step(V.tensor_tensor(vals[:, :, :, 2 * h], hs[:], tval[:].unsqueeze(1).to_broadcast([P, E, TILES]), ALU.mult))
                step(V.tensor_scalar(vals[:, :, :, 2 * h + 1], hs[:], pval[:, 0:1], None, ALU.mult))
            with dve.Fori(0, E // 2) as i:
                for par in range(2):
                    V.tensor_tensor(onehot[:, par, :, :], iota_b[:].unsqueeze(1).to_broadcast([P, TILES, P]),
                                    low_b[:, bass.ds(2 * i + par, 1), :].squeeze(1).unsqueeze(2).to_broadcast([P, TILES, P]),
                                    ALU.is_equal).then_inc(hot_done, 1)
                for par in range(2):
                    dve.wait_ge(list_done, 2 * i + par + 1)
                    V.tensor_copy(lists[:, bass.ds(2 * i + par, 1), :].squeeze(1), list_ps[par][:, 0:2 * SC]).then_inc(list_read, 1)
            dve.wait_ge(list_read, E)
            pairs = lists[:].rearrange("p e (h two) -> p e h two", two=2)
            step(V.scalar_tensor_tensor(idx_f[:], pairs[:, :, :, 0], float(P), pairs[:, :, :, 1], ALU.mult, ALU.add))
            step(V.tensor_copy(g["idx"][:], idx_f[:]))


def experts(nc, t, g, out, moe):
    nm = "moe"
    with semaphores(nc, nm) as sem, ExitStack() as ctx:
        sb = lambda n, s, d=F32: ctx.enter_context(nc.sbuf_tensor(f"{nm}_{n}", s, d))
        pb = lambda n: ctx.enter_context(nc.psum_tensor(f"{nm}_{n}", [P, 512], F32))
        up_ps, tp_ps, down_ps = [pb(f"up{j}") for j in range(2)], [pb(f"tp{k}") for k in range(KD)], \
            [pb(f"down{j}") for j in range(SC)]
        stage1, stage2, w1, w2 = (moe[x] for x in ("stage1", "stage2", "w1", "w2"))
        idx_now, idx_out = sb("idx_now", [P, SC], U32), sb("idx_out", [P, SC], U32)
        xg = sb("xg", [P, SC, ROW])
        weight, weight_next = sb("weight", [P, SC]), sb("weight_next", [P, SC])
        xn, xm = sb("xn", [P, SC, D]), sb("xm", [P, KD, CAP])
        xt = [sb(f"xt{j}", [P, KD, CAP], F32R) for j in range(2)]
        stats, mv = sb("stats", [P, SC, 6]), sb("mv", [P, SC, 2])
        ve, rstd = sb("ve", [P, SC]), sb("rstd", [P, SC])
        h32 = sb("h32", [P, 2, CAP])
        h = [sb(f"h{j}", [P, MC, CAP], F32R) for j in range(2)]
        b2, y, y2 = sb("b2", [P, D]), sb("y", [P, SC, D]), sb("y2", [P, SC, D])

        stats_done, aggr_done, ve_done, rstd_done, xn_done = (sem(x) for x in ("stats", "aggr", "ve", "rstd", "xn"))
        tp_done, xm_done, xhi_done, xlo_done = sem("tp"), sem("xm"), sem("xhi"), sem("xlo")
        up_done, gelu_done, hhi_done, hlo_done = sem("up"), sem("gelu"), sem("hhi"), sem("hlo")
        down_done, down_free, y_step, y_done = sem("down"), sem("down_free"), sem("y_step"), sem("y_done")
        w1_in, w2_in, b2_in, w1_hi, w1_lo, w2_hi, w2_lo = (sem(x) for x in ("w1_in", "w2_in", "b2_in", "w1_hi", "w1_lo", "w2_hi", "w2_lo"))
        idx_done, gathered, scattered, weight_done, passed, passed_dve = (sem(x) for x in ("idx", "gathered", "scattered", "weight", "passed", "passed_dve"))
        idxo_done, weight_now, y2_free = sem("idxo"), sem("weight_now"), sem("y2_free")
        block = ctx.enter_context(nc.Block())
        w1_d = t["moe_w1"].rearrange("e (k p) n -> e p k n", p=P)
        w2_d = t["moe_w2"].rearrange("e (m p) n -> e p m n", p=P)

        @block.sync
        def _(sp):
            sp.dma_start(b2[:], t["L3_cond_b2s"][0, :].partition_broadcast(P)).then_inc(b2_in, 16)
            sp.sem_inc(w1_lo, 1)
            sp.sem_inc(w2_lo, 1)
            with sp.Fori(0, E - 1) as e:
                sp.wait_ge(w1_lo, e + 1)
                sp.dma_start(stage1[:], w1_d[bass.ds(e + 1, 1), :, :, :].squeeze(0)).then_inc(w1_in, 16)
                sp.wait_ge(w2_lo, e + 1)
                sp.dma_start(stage2[:], w2_d[bass.ds(e + 1, 1), :, :, :].squeeze(0)).then_inc(w2_in, 16)
                sp.wait_ge(y_done, e + 1)
                sp.dma_start(b2[:], t["L3_cond_b2s"][bass.ds(e + 1, 1), :].squeeze(0).partition_broadcast(P)).then_inc(b2_in, 16)

        @block.gpsimd
        def _(pool):
            def gated_wait(s, val):
                pool.wait_ge(s, val)
                pool.sem_inc(passed, 1)

            def gather(e):
                nc.gpsimd.tensor_copy(idx_now[:], g["idx"][:, bass.ds(e, 1), :].squeeze(1)).then_inc(idx_done, 1)
                gated_wait(idx_done, e + 1)
                for s in range(SC):
                    pool.indirect_dma_start(xg[:, s, :], None, t["token_rows"][:, :],
                                            bass.IndirectOffsetOnAxis(ap=idx_now[:, s:s + 1], axis=0)).then_inc(gathered, 16)

            def token_rstd(e):
                gated_wait(ve_done, e + 1)
                nc.gpsimd.tensor_tensor(rstd[:], ve[:], g["mhalf"][:, 0:SC], ALU.pow).then_inc(rstd_done, 1)

            def body(e, first, more):
                if more:
                    gated_wait(xn_done, e + 1)
                    gated_wait(weight_done, e + 1)
                    gather(e + 1)
                if not first:
                    gated_wait(scattered, 16 * SC * e)
                pool.sem_inc(y2_free, 1)
                if more:
                    token_rstd(e + 1)
                nc.gpsimd.tensor_copy(idx_out[:], g["idx"][:, bass.ds(e, 1), :].squeeze(1)).then_inc(idxo_done, 1)
                gated_wait(idxo_done, e + 1)
                gated_wait(y_done, e + 1)
                for s in range(SC):
                    pool.indirect_dma_start(out.rearrange("b n d -> (b n) d"),
                                            bass.IndirectOffsetOnAxis(ap=idx_out[:, s:s + 1], axis=0),
                                            y2[:, s, :], None, compute_op=ALU.add).then_inc(scattered, 16)

            gather(0)
            token_rstd(0)
            body(0, True, True)
            with pool.Fori(1, E - 1) as e:
                body(e, False, True)
            body(E - 1, False, False)
            pool.wait_ge(scattered, 16 * SC * E)

        @block.scalar
        def _(act):
            b1 = COL_AT["L3_cond_b1s"]

            def x_hi(e):
                act.wait_ge(xm_done, e + 1)
                nc.scalar.activation(xt[0][:], xm[:], ACT.Copy).then_inc(xhi_done, 1)

            def body(e, more):
                for m in range(MC):
                    act.wait_ge(up_done, MC * e + m + 1)
                    if m >= 2:
                        act.wait_ge(hlo_done, MC * e + m - 1)
                    nc.scalar.activation(h32[:, m % 2, :], up_ps[m % 2][:], ACT.Gelu_apprx_tanh,
                                         bias=g["cols"][:, bass.ds(b1 + MC * e + m, 1)]).then_inc(gelu_done, 1)
                    act.wait_ge(gelu_done, MC * e + m + 1)
                    nc.scalar.activation(h[0][:, m, :], h32[:, m % 2, :], ACT.Copy).then_inc(hhi_done, 1)
                if more:
                    act.wait_ge(w1_in, 16 * e + 16)
                    nc.scalar.activation(w1[0][:], stage1[:], ACT.Copy).then_inc(w1_hi, 1)
                    x_hi(e + 1)
                    act.wait_ge(down_done, e + 1)
                    act.wait_ge(w2_in, 16 * e + 16)
                    nc.scalar.activation(w2[0][:], stage2[:], ACT.Copy).then_inc(w2_hi, 1)

            act.sem_inc(w1_hi, 1)
            act.sem_inc(w2_hi, 1)
            x_hi(0)
            with act.Fori(0, E - 1) as e:
                body(e, True)
            body(E - 1, False)

        @block.tensor
        def _(pe):
            mm = nc.tensor.matmul

            def three(out, lhs, rhs, start, stop):
                mm(out, lhs[0], rhs[0], start=start, stop=False)
                mm(out, lhs[1], rhs[0], start=False, stop=False)
                return mm(out, lhs[0], rhs[1], start=False, stop=stop)

            def transposes(e):
                pe.wait_ge(xn_done, e + 1)
                for k in range(KD):
                    for s in range(SC):
                        last = nc.tensor.transpose(tp_ps[k][:, s * P:(s + 1) * P], xn[:, s, k * P:(k + 1) * P],
                                                   g["ident"][:])
                last.then_inc(tp_done, 1)

            def body(e, more):
                pe.wait_ge(w1_lo, e + 1)
                pe.wait_ge(xlo_done, e + 1)
                for m in range(MC):
                    if m >= 2:
                        pe.wait_ge(gelu_done, MC * e + m - 1)
                    for k in range(KD):
                        last = three(up_ps[m % 2][:], [w[:, k, m * P:(m + 1) * P] for w in w1],
                                     [x[:, k, :] for x in xt], k == 0, k == KD - 1)
                    last.then_inc(up_done, 1)
                pe.wait_ge(down_free, e + 1)
                pe.wait_ge(w2_lo, e + 1)
                for m in range(MC):
                    pe.wait_ge(hlo_done, MC * e + m + 1)
                    for s in range(SC):
                        last = three(down_ps[s][:, 0:D], [x[:, m, s * P:(s + 1) * P] for x in h],
                                     [w[:, m, :] for w in w2], m == 0, m == MC - 1)
                    if m == 6 and more:
                        transposes(e + 1)
                last.then_inc(down_done, 1)

            transposes(0)
            with pe.Fori(0, E - 1) as e:
                body(e, True)
            body(E - 1, False)

        @block.vector
        def _(dve):
            V = nc.vector

            def normalise(e):
                dve.wait_ge(gathered, 16 * SC * e + 16 * SC)
                V.tensor_copy(weight_next[:], xg[:, :, bass.ds(D + e, 1)].squeeze(2)).then_inc(weight_done, 1)
                for s in range(SC):
                    V.bn_stats(stats[:, s, :], xg[:, s, 0:D]).then_inc(stats_done, 1)
                for s in range(SC):
                    dve.wait_ge(stats_done, SC * e + s + 1)
                    dve.sem_inc(passed_dve, 1)
                    V.bn_aggr(mv[:, s, :], stats[:, s, :]).then_inc(aggr_done, 1)
                dve.wait_ge(aggr_done, SC * e + SC)
                V.tensor_scalar(ve[:], mv[:, :, 1], 1e-5, None, ALU.add).then_inc(ve_done, 1)
                dve.wait_ge(rstd_done, e + 1)
                for s in range(SC):
                    ins = V.tensor_scalar(xn[:, s, :], xg[:, s, 0:D], mv[:, s, 0:1], rstd[:, s:s + 1],
                                          ALU.subtract, ALU.mult)
                ins.then_inc(xn_done, 1)

            def modulate(e):
                dve.wait_ge(tp_done, e + 1)
                gain, offset = COL_AT["L3_cond_mlp_g"], COL_AT["L3_cond_mlp_b"]
                for k in range(KD):
                    ins = V.tensor_scalar(xm[:, k, :], tp_ps[k][:], g["cols"][:, gain + k:gain + k + 1],
                                          g["cols"][:, offset + k:offset + k + 1], ALU.mult, ALU.add)
                ins.then_inc(xm_done, 1)
                dve.wait_ge(xhi_done, e + 1)
                V.tensor_tensor(xt[1][:], xm[:], xt[0][:].bitcast(F32), ALU.subtract).then_inc(xlo_done, 1)

            def low(e, hi_done, dst, src, done):
                dve.wait_ge(hi_done, e + 1)
                V.tensor_tensor(dst[1][:], src[:], dst[0][:].bitcast(F32), ALU.subtract).then_inc(done, 1)

            def weights_now(e):
                dve.wait_ge(weight_done, e + 1)
                V.tensor_copy(weight[:], weight_next[:]).then_inc(weight_now, 1)

            def body(e, more):
                for m in range(MC):
                    dve.wait_ge(hhi_done, MC * e + m + 1)
                    V.tensor_tensor(h[1][:, m, :], h32[:, m % 2, :], h[0][:, m, :].bitcast(F32), ALU.subtract)\
                        .then_inc(hlo_done, 1)
                if more:
                    normalise(e + 1)
                    low(e + 1, w1_hi, w1, stage1, w1_lo)
                    modulate(e + 1)
                dve.wait_ge(down_done, e + 1)
                dve.wait_ge(b2_in, 16 * e + 16)
                for s in range(SC):
                    ins = V.tensor_tensor(y[:, s, :], down_ps[s][:, 0:D], b2[:], ALU.add)
                ins.then_inc(down_free, 1)
                dve.wait_ge(down_free, e + 2)
                dve.wait_ge(weight_now, e + 1)
                dve.wait_ge(y2_free, e + 1)
                for s in range(SC):
                    ins = V.tensor_scalar(y2[:, s, :], y[:, s, :], weight[:, s:s + 1], None, ALU.mult)
                ins.then_inc(y_done, 1)
                if more:
                    dve.wait_ge(y_done, e + 1)
                    weights_now(e + 1)
                    low(e + 1, w2_hi, w2, stage2, w2_lo)

            dve.sem_inc(down_free, 1)
            normalise(0)
            modulate(0)
            weights_now(0)
            with dve.Fori(0, E - 1) as e:
                body(e, True)
            body(E - 1, False)


def program(nc, t, out, stop=None):
    with ExitStack() as ctx:
        sb = lambda n, s, d=F32: ctx.enter_context(nc.sbuf_tensor(n, s, d))
        sem = lambda n: ctx.enter_context(nc.semaphore(n))
        g = {"x": sb("x_sb", [P, TILES, D]), "cols": sb("cols_sb", [P, NCOL]), "mod": sb("mod_sb", [P, NMOD, B + 2]),
             "ident": sb("ident_sb", [P, P]), "ones": sb("ones", [P, P]), "ones_r": sb("ones_r", [P, P], F32R),
             "hmask": sb("hmask_sb", [P, 10]), "neg_ident": sb("neg_ident_sb", [P, P]),
             "head_sel": sb("head_sel_sb", [P, 95]), "fold": sb("fold_sb", [P, 16]), "pair_sel": sb("pair_sel_sb", [P, 62]), "mhalf": sb("mhalf", [P, 8]),
             "idx": sb("idx_sb", [P, E, SC], U32)}
        x_in, set_up = sem("x_in"), sem("set_up")

        with nc.Block() as block:
            @block.sync
            def _(sp):
                for name in ("ident", "hmask", "neg_ident", "head_sel", "pair_sel", "fold"):
                    sp.dma_start(g[name][:], t[name]).then_inc(x_in, 16)
                sp.wait_ge(x_in, 16 * 6)

            @block.gpsimd
            def _(pool):
                nc.gpsimd.memset(g["ones"][:], 1.0).then_inc(set_up, 1)
                nc.gpsimd.memset(g["ones_r"][:].bitcast(F32), 1.0).then_inc(set_up, 1)
                nc.gpsimd.memset(g["mhalf"][:], -0.5).then_inc(set_up, 1)
                pool.wait_ge(set_up, 3)

        conditioning(nc, t, g)
        phases = [("L0a", lambda: attention(nc, t, g, Attention("L0a", 16, 64, 64 ** -0.5, True, "layer", 1e-5))),
                  ("L0m", lambda: mlp(nc, t, g, "L0m", "layer", 1e-5)),
                  ("L1a", lambda: attention(nc, t, g, Attention("L1a", 1, 256, 256 ** -0.5, False, "rms", 1e-6))),
                  ("L1m", lambda: mlp(nc, t, g, "L1m", "rms", 1e-6)),
                  ("L2a", lambda: attention(nc, t, g, Attention("L2a", 16, 16, 16 ** -0.5, True, None, 1e-5))),
                  ("L2m", lambda: mlp(nc, t, g, "L2m", None, 1e-5)),
                  ("L3a", lambda: attention(nc, t, g, Attention("L3a", 16, 64, 64 ** -0.5, False, "layer", 1e-5)))]
        for name, phase in phases:
            phase()
            if stop == name:
                with nc.Block() as block:
                    @block.sync
                    def _(sp):
                        sp.dma_start(out.rearrange("b (t p) d -> p (b t) d", p=P), g["x"][:]).then_inc(x_in, 16)
                        sp.wait_ge(x_in, 16 * 7)
                return
        moe = {"stage1": sb("moe_stage1", [P, KD, MLP]), "stage2": sb("moe_stage2", [P, MC, D]),
               "w1": [sb(f"moe_w1{j}", [P, KD, MLP], F32R) for j in range(2)],
               "w2": [sb(f"moe_w2{j}", [P, MC, D], F32R) for j in range(2)]}
        route(nc, t, g, out, moe)
        experts(nc, t, g, out, moe)


def _laid_out(np, inputs):
    f = lambda a: np.ascontiguousarray(a)
    i = {k: np.asarray(v) for k, v in inputs.items()}
    h = {"x": i["x"], "c_t": f(i["cond_1024"].T), "mask": f(i["mask_BxS_bk0"]).view(np.int32),
         "mask_t": f(i["mask_BxS_bk0"].T).view(np.int32)}
    for n in ("q", "k"):
        for p in ("g", "b"):
            i[f"{n}n_{p}2"] = np.concatenate([i[f"L3_cond_{n}n_{p}"]] * 2)
    h["cols"] = f(np.concatenate([i[n].reshape(k, P).T for n, k in COL_VECS], axis=1))
    h["rows"] = f(np.concatenate([i[n].reshape(-1) for n, _ in ROW_VECS]))
    for n in ("L0_cond_W_mod", "L1_cond_film1_w", "L1_cond_film2_w", "L2_cond_ada1_w", "L2_cond_ada2_w",
              "L1_cond_proj_b", "L1_cond_mlp_b2", "L2_cond_proj_b", "L2_cond_fc2_b"):
        h[n] = i[n]
    h["W_ada_t"] = f(i["L3_cond_W_ada"].T)
    w = i["L0_cond_W_qkv"]
    h["L0a_wq"], h["L0a_wk"], h["L0a_wv"], h["L0a_wo"] = f(w[:, 0:1024]), f(w[:, 1024:2048]), f(w[:, 2048:3072]), i["L0_cond_W_out"]
    h["L1a_wq"], h["L1a_wk"], h["L1a_wv"], h["L1a_wo"] = (i[f"L1_cond_{n}_w"] for n in ("q", "k", "v", "proj"))
    w = i["L2_cond_qkv_w"]
    h["L2a_wq"], h["L2a_wk"] = f(w[:, 0:256]), f(w[:, 256:512])
    wv = np.zeros((256, 16, 32), np.float32)
    wv[:, :, 0:16] = w[:, 512:768].reshape(256, 16, 16)
    h["L2a_wv"] = wv.reshape(256, 512)
    wo = np.zeros((16, 32, 256), np.float32)
    wo[:, 0:16, :] = i["L2_cond_proj_w"].reshape(16, 16, 256)
    h["L2a_wo"] = wo.reshape(512, 256)
    w = f(i["L3_cond_Wqkv"].T)
    h["L3a_wq"], h["L3a_wk"], h["L3a_wv"] = f(w[:, 0:1024]), f(w[:, 1024:2048]), f(w[:, 2048:3072])
    h["L3a_wo"] = f(i["L3_cond_Wout"].T)
    h["L0m_w1"], h["L0m_w2"] = i["L0_cond_W1"], i["L0_cond_W2"]
    h["L1m_w1"], h["L1m_w2"] = i["L1_cond_mlp_w1"], i["L1_cond_mlp_w2"]
    h["L2m_w1"], h["L2m_w2"] = i["L2_cond_fc1_w"], i["L2_cond_fc2_w"]
    h["wg_t"] = f(i["L3_cond_Wgate"].T)
    h["moe_w1"], h["moe_w2"] = f(i["L3_cond_fc1s"].transpose(0, 2, 1)), f(i["L3_cond_fc2s"].transpose(0, 2, 1))
    h["L3_cond_b2s"] = i["L3_cond_b2s"]
    h["tri"] = np.triu(np.ones((P, P), np.float32), 1)
    h["iota"] = np.tile(np.arange(P, dtype=np.float32), (P, 1))
    h["tval"] = np.tile(np.arange(TILES, dtype=np.float32), (P, 1))
    h["pval"] = np.arange(P, dtype=np.float32)[:, None].copy()
    h["ident"] = np.eye(P, dtype=np.float32)
    hm = np.zeros((P, 10), np.float32)
    hm[0:64, 0] = hm[64:128, 1] = 1.0
    for m in range(8):
        hm[16 * m:16 * m + 16, 2 + m] = 1.0
    h["hmask"] = hm
    h["neg_ident"] = -np.eye(P, dtype=np.float32)
    sel = np.zeros((P, 95), np.float32)
    sel[:, 31] = 1.0
    h["head_sel"] = sel
    fold = np.zeros((P, 16), np.float32)
    for j in range(4):
        fold[32 * j + np.arange(8), 2 * np.arange(8) + j % 2] = 1.0
    h["fold"] = fold
    sel = np.zeros((P, 62), np.float32)
    sel[0:64, 30] = sel[64:128, 31] = 1.0
    h["pair_sel"] = sel
    for n, heads, width in (("L0a", 16, 64), ("L1a", 1, 256), ("L2a", 16, 32), ("L3a", 16, 64)):
        wide = np.zeros((P, heads * width), np.float32)
        wide[0:heads] = np.kron(np.eye(heads, dtype=np.float32), np.ones((1, width), np.float32))
        h["spread_" + n] = wide
    return h


def kernel(**inputs):
    import concourse.bacc as bacc
    from concourse.bass_utils import run_bass_kernel_spmd

    nc = bacc.Bacc("TRN2", target_bir_lowering=False, num_devices=1)
    arrays = _laid_out(np, inputs)
    t = {n: nc.dram_tensor(f"in_{n}", v.shape, mybir.dt.from_np(v.dtype), kind="ExternalInput").ap()
         for n, v in arrays.items()}
    t["gate_rows"] = nc.dram_tensor("gate_rows", (NGATE, B, D), F32, kind="Internal").ap()
    t["token_rows"] = nc.dram_tensor("token_rows", (B * N, ROW), F32, kind="Internal").ap()
    out = nc.dram_tensor("out_x", (B, N, D), F32, kind="ExternalOutput").ap()
    program(nc, t, out)
    r = run_bass_kernel_spmd(nc, [{f"in_{n}": v for n, v in arrays.items()}], core_ids=[0])
    return r.results[0]["out_x"]
```
